# Optimizing a Trainium2 kernel written in Bass

```python
import numpy as np
import jax
import jax.numpy as jnp

def _softmax(x, axis=-1):
    return jax.nn.softmax(x, axis=axis)

def _gelu(x):
    return jax.nn.gelu(x, approximate=True)

def _silu(x):
    return jax.nn.silu(x)

def _sigmoid(x):
    return jax.nn.sigmoid(x)

def _layernorm(x, axis=-1, eps=1e-05):
    m = jnp.mean(x, axis=axis, keepdims=True)
    v = jnp.var(x, axis=axis, keepdims=True)
    return (x - m) / jnp.sqrt(v + eps)

def _scatter_add(tgt, idx, src, axis=0):
    return tgt.at[idx].add(src)

def _segment_sum(src, seg, n):
    return jax.ops.segment_sum(src, seg, n)
kernel_name = 'mk_decoder_preln_d1_seqx_r4_e66c12'

def setup_inputs(seed: int=0):
    np.random.seed(seed)
    _w = jnp.asarray

    def _rec_inputs():
        import jax
        import jax.numpy as jnp
        _rk = jax.random.key(seed)
        x = -0.0003929 + 0.9999 * jax.random.normal(jax.random.fold_in(_rk, 1), (16, 100, 512), jnp.float32)
        _lenS = 100 - jax.random.randint(jax.random.fold_in(_rk, 7), (16,), 0, max(1, 100 // 4) + 1, jnp.int32)
        _lenS2 = 361 - jax.random.randint(jax.random.fold_in(_rk, 8), (16,), 0, max(1, 361 // 4) + 1, jnp.int32)
        _ctx_2048P = jax.random.normal(jax.random.fold_in(_rk, 11), (16, 16, 512), jnp.float32)
        _ctx_2048c = jax.random.dirichlet(jax.random.fold_in(_rk, 511), 0.3 * jnp.ones((16,), jnp.float32), (16, 361))
        _ctx_2048t = jnp.einsum('bsk,bkd->bsd', _ctx_2048c, _ctx_2048P)
        _ctx_2048t = _ctx_2048t * jax.lax.rsqrt(jnp.mean(jnp.square(_ctx_2048t)) + 1e-12) * 0.953939
        ctx_2048 = -0.000514642 + 1.00011 * (_ctx_2048t + 0.3 * jax.random.normal(jax.random.fold_in(_rk, 611), (16, 361, 512), jnp.float32))
        return (x, ctx_2048)
    x, ctx_2048 = _rec_inputs()

    def _L0_attn_setup():
        import jax, jax.numpy as jnp
        import numpy as np
        B, S, HID = (2, 512, 512)
        H, HKV, D = (16, 4, 128)
        ROPE_BASE = 1000000.0
        EPS = 1e-05

        def _layernorm(x, g, b):
            mu = jnp.mean(x, axis=-1, keepdims=True)
            var = jnp.mean(jnp.square(x - mu), axis=-1, keepdims=True)
            return (x - mu) * jax.lax.rsqrt(var + EPS) * g + b

        def _rope_tables(seq_len, dim, base):
            inv_freq = 1.0 / base ** (jnp.arange(0, dim, 2, dtype=jnp.float32) / dim)
            t = jnp.arange(seq_len, dtype=jnp.float32)
            freqs = jnp.outer(t, inv_freq)
            cos = jnp.concatenate([jnp.cos(freqs), jnp.cos(freqs)], axis=-1)
            sin = jnp.concatenate([jnp.sin(freqs), jnp.sin(freqs)], axis=-1)
            return (cos, sin)

        def _rotate_half(x):
            x1, x2 = jnp.split(x, 2, axis=-1)
            return jnp.concatenate([-x2, x1], axis=-1)
        key = jax.random.key(seed)
        k1, k2, k3 = jax.random.split(key, 3)
        return {'x': jax.random.normal(k1, (B, S, HID), dtype=jnp.float32), 'w_qkv': jax.random.normal(k2, ((H + 2 * HKV) * D, HID), dtype=jnp.float32) * 0.02, 'w_o': jax.random.normal(k3, (HID, H * D), dtype=jnp.float32) * 0.02, 'qn_g': jnp.ones((D,), jnp.float32), 'qn_b': jnp.zeros((D,), jnp.float32), 'kn_g': jnp.ones((D,), jnp.float32), 'kn_b': jnp.zeros((D,), jnp.float32)}
    _L0_attn_all = _L0_attn_setup()
    _L0_attn_in = {k: v for k, v in _L0_attn_all.items() if k in ('w_qkv', 'w_o', 'qn_g', 'qn_b', 'kn_g', 'kn_b')}
    del _L0_attn_all

    def _L0_xattn_setup():
        import jax, jax.numpy as jnp
        import numpy as np
        DIM = 512
        NHEADS = 32
        HEAD_DIM = DIM // NHEADS
        EPS = 1e-06

        def _rmsnorm(t):
            return t * jax.lax.rsqrt(jnp.mean(t * t, axis=-1, keepdims=True) + EPS)
        key = jax.random.key(seed)
        kx, kc, kq, kk, kv = jax.random.split(key, 5)
        x = jax.random.normal(kx, (2, 1024, DIM), dtype=jnp.float32)
        context = jax.random.normal(kc, (2, 128, DIM), dtype=jnp.float32)
        std = 0.02
        Wq = jax.random.normal(kq, (DIM, DIM), dtype=jnp.float32) * std
        Wk = jax.random.normal(kk, (DIM, DIM), dtype=jnp.float32) * std
        Wv = jax.random.normal(kv, (DIM, DIM), dtype=jnp.float32) * std
        return {'x': x, 'context': context, 'Wq': Wq, 'Wk': Wk, 'Wv': Wv}
    _L0_xattn_all = _L0_xattn_setup()
    _L0_xattn_in = {k: v for k, v in _L0_xattn_all.items() if k in ('Wq', 'Wk', 'Wv')}
    del _L0_xattn_all

    def _L0_ffn_setup():
        import jax, jax.numpy as jnp
        import numpy as np
        D_MODEL = 512
        D_EXPERT = 2048
        EPS = 1e-08

        def ternary_quant(w):
            scale = jnp.mean(jnp.abs(w)) + EPS
            q = jnp.clip(jnp.round(w / scale), -1.0, 1.0) * scale
            return w + jax.lax.stop_gradient(q - w)
        key = jax.random.key(seed)
        k_x, k_up, k_gate, k_down = jax.random.split(key, 4)
        std_in = 1.0 / np.sqrt(D_MODEL)
        std_exp = 1.0 / np.sqrt(D_EXPERT)
        return {'x': jax.random.normal(k_x, (4, 512, D_MODEL), dtype=jnp.float32), 'W_up': jax.random.normal(k_up, (D_EXPERT, D_MODEL), dtype=jnp.float32) * std_in, 'W_gate': jax.random.normal(k_gate, (D_EXPERT, D_MODEL), dtype=jnp.float32) * std_in, 'W_down': jax.random.normal(k_down, (D_MODEL, D_EXPERT), dtype=jnp.float32) * std_exp}
    _L0_ffn_all = _L0_ffn_setup()
    _L0_ffn_in = {k: v for k, v in _L0_ffn_all.items() if k in ('W_up', 'W_gate', 'W_down')}
    del _L0_ffn_all
    return {'x': x, 'ctx_2048': ctx_2048, 'L0_attn_w_qkv': _L0_attn_in['w_qkv'], 'L0_attn_w_o': _L0_attn_in['w_o'], 'L0_attn_qn_g': _L0_attn_in['qn_g'], 'L0_attn_qn_b': _L0_attn_in['qn_b'], 'L0_attn_kn_g': _L0_attn_in['kn_g'], 'L0_attn_kn_b': _L0_attn_in['kn_b'], 'L0_xattn_Wq': _L0_xattn_in['Wq'], 'L0_xattn_Wk': _L0_xattn_in['Wk'], 'L0_xattn_Wv': _L0_xattn_in['Wv'], 'L0_ffn_W_up': _L0_ffn_in['W_up'], 'L0_ffn_W_gate': _L0_ffn_in['W_gate'], 'L0_ffn_W_down': _L0_ffn_in['W_down']}

def reference(x, ctx_2048, L0_attn_w_qkv, L0_attn_w_o, L0_attn_qn_g, L0_attn_qn_b, L0_attn_kn_g, L0_attn_kn_b, L0_xattn_Wq, L0_xattn_Wk, L0_xattn_Wv, L0_ffn_W_up, L0_ffn_W_gate, L0_ffn_W_down):
    import jax
    import jax.numpy as jnp

    def _L0_attn_ref(x, w_qkv, w_o, qn_g, qn_b, kn_g, kn_b):
        import jax, jax.numpy as jnp
        import numpy as np
        B, S, HID = (2, 512, 512)
        H, HKV, D = (16, 4, 128)
        ROPE_BASE = 1000000.0
        EPS = 1e-05

        def _layernorm(x, g, b):
            mu = jnp.mean(x, axis=-1, keepdims=True)
            var = jnp.mean(jnp.square(x - mu), axis=-1, keepdims=True)
            return (x - mu) * jax.lax.rsqrt(var + EPS) * g + b

        def _rope_tables(seq_len, dim, base):
            inv_freq = 1.0 / base ** (jnp.arange(0, dim, 2, dtype=jnp.float32) / dim)
            t = jnp.arange(seq_len, dtype=jnp.float32)
            freqs = jnp.outer(t, inv_freq)
            cos = jnp.concatenate([jnp.cos(freqs), jnp.cos(freqs)], axis=-1)
            sin = jnp.concatenate([jnp.sin(freqs), jnp.sin(freqs)], axis=-1)
            return (cos, sin)

        def _rotate_half(x):
            x1, x2 = jnp.split(x, 2, axis=-1)
            return jnp.concatenate([-x2, x1], axis=-1)
        b, s, _ = x.shape
        qkv = jnp.einsum('bsh,oh->bso', x, w_qkv)
        q, k, v = jnp.split(qkv, [H * D, (H + HKV) * D], axis=-1)
        q = q.reshape(b, s, H, D).transpose(0, 2, 1, 3)
        k = k.reshape(b, s, HKV, D).transpose(0, 2, 1, 3)
        v = v.reshape(b, s, HKV, D).transpose(0, 2, 1, 3)
        q = _layernorm(q, qn_g, qn_b)
        k = _layernorm(k, kn_g, kn_b)
        cos, sin = _rope_tables(s, D, ROPE_BASE)
        q = q * cos + _rotate_half(q) * sin
        k = k * cos + _rotate_half(k) * sin
        rep = H // HKV
        k = jnp.repeat(k, rep, axis=1)
        v = jnp.repeat(v, rep, axis=1)
        scores = jnp.einsum('bhqd,bhkd->bhqk', q, k) / jnp.sqrt(jnp.float32(D))
        causal = jnp.triu(jnp.ones((s, s), dtype=bool), k=1)
        scores = jnp.where(causal, -jnp.inf, scores)
        weights = jax.nn.softmax(scores, axis=-1)
        attn = jnp.einsum('bhqk,bhkd->bhqd', weights, v)
        attn = attn.transpose(0, 2, 1, 3).reshape(b, s, H * D)
        return jnp.einsum('bsd,od->bso', attn, w_o)

    def _L0_xattn_ref(x, context, Wq, Wk, Wv):
        import jax, jax.numpy as jnp
        import numpy as np
        DIM = 512
        NHEADS = 32
        HEAD_DIM = DIM // NHEADS
        EPS = 1e-06

        def _rmsnorm(t):
            return t * jax.lax.rsqrt(jnp.mean(t * t, axis=-1, keepdims=True) + EPS)
        b, n, _ = x.shape
        m = context.shape[1]
        q = x @ Wq.T
        k_raw = context @ Wk.T
        v_raw = context @ Wv.T
        q = q.reshape(b, n, NHEADS, HEAD_DIM).transpose(0, 2, 1, 3)
        kv = jnp.concatenate([k_raw, v_raw], axis=-1)
        kv = kv.reshape(b, m, NHEADS, HEAD_DIM, 2)
        k = kv[..., 0].transpose(0, 2, 1, 3)
        v = kv[..., 1].transpose(0, 2, 1, 3)
        q = _rmsnorm(q)
        k = _rmsnorm(k)
        scale = HEAD_DIM ** (-0.5)
        scores = jnp.einsum('bhnd,bhmd->bhnm', q, k) * scale
        attn = jax.nn.softmax(scores, axis=-1)
        out = jnp.einsum('bhnm,bhmd->bhnd', attn, v)
        return out.transpose(0, 2, 1, 3).reshape(b, n, NHEADS * HEAD_DIM)

    def _L0_ffn_ref(x, W_up, W_gate, W_down):
        import jax, jax.numpy as jnp
        import numpy as np
        D_MODEL = 512
        D_EXPERT = 2048
        EPS = 1e-08

        def ternary_quant(w):
            scale = jnp.mean(jnp.abs(w)) + EPS
            q = jnp.clip(jnp.round(w / scale), -1.0, 1.0) * scale
            return w + jax.lax.stop_gradient(q - w)
        wu = ternary_quant(W_up)
        wg = ternary_quant(W_gate)
        wd = ternary_quant(W_down)
        up = jnp.einsum('bsd,ed->bse', x, wu)
        gate = jnp.einsum('bsd,ed->bse', x, wg)
        hidden = jax.nn.silu(up) * gate
        return jnp.einsum('bse,de->bsd', hidden, wd)
    x = x + _L0_attn_ref(_layernorm(x, axis=-1), L0_attn_w_qkv, L0_attn_w_o, L0_attn_qn_g, L0_attn_qn_b, L0_attn_kn_g, L0_attn_kn_b)
    x = x + _L0_xattn_ref(_layernorm(x, axis=-1), ctx_2048, L0_xattn_Wq, L0_xattn_Wk, L0_xattn_Wv)
    x = x + _L0_ffn_ref(_layernorm(x, axis=-1), L0_ffn_W_up, L0_ffn_W_gate, L0_ffn_W_down)
    return x

_drawn_inputs = setup_inputs


def setup_inputs(seed=0):
    import zlib

    import numpy as np

    out = dict(_drawn_inputs(seed))
    spreads = {'L0_attn_qn_g': (1.0, 0.6),
     'L0_attn_qn_b': (0.0, 0.8),
     'L0_attn_kn_g': (1.0, 0.6),
     'L0_attn_kn_b': (0.0, 0.8)}
    factors = {}
    for name, (base, spread) in spreads.items():
        noise = np.random.default_rng([zlib.crc32(name.encode()), seed]).standard_normal(out[name].shape)
        drawn = base * np.exp(spread * noise) if base else spread * noise
        out[name] = jnp.asarray(drawn.astype(out[name].dtype))
    for name, factor in factors.items():
        out[name] = (out[name] * factor).astype(out[name].dtype)
    return out
```

```python
from contextlib import ExitStack

import numpy as np
import concourse.bass as bass
from concourse import mybir

F32 = mybir.dt.float32
F16 = mybir.dt.float16
BF16 = mybir.dt.bfloat16
I32 = mybir.dt.int32
ALU = mybir.AluOpType
ACT = mybir.ActivationFunctionType
AX = mybir.AxisListType

NB, S, DM = 16, 100, 512
KT = DM // 128
H, HKV, D = 16, 4, 128
REP = H // HKV
ROPE_BASE = 1000000.0
EPS_LN = 1e-5
EPS_RMS = 1e-6
CTX = 361
XH, XD = 32, 16
KC = 122
NC = 3
CTXP = KC * NC
FE = 2048
HALF = D // 2

SX = 256.0
SW = 1024.0
SA = 512.0
SN = 1024.0
SV = 2.0 ** -10
SH = 8.0
VW = 2 * XD + 1
GH = 4
NG = XH // GH
UB = 4
ET = FE // 128

C_ID, C_COS, C_SIN, C_COST, C_SINT, C_MASK, C_ONE, C_END = 0, 128, 256, 384, 484, 584, 684, 687


def constants():
    inv = (np.float32(1.0) / np.float32(ROPE_BASE) ** (np.arange(0, D, 2, dtype=np.float32) / np.float32(D))).astype(np.float32)
    f = np.outer(np.arange(S, dtype=np.float32), inv).astype(np.float32)
    cos = np.concatenate([np.cos(f), np.cos(f)], -1).astype(np.float32)
    sin = np.concatenate([-np.sin(f), np.sin(f)], -1).astype(np.float32)
    c = np.zeros((128, C_END), np.float32)
    c[:, C_ID:C_ID + 128] = np.eye(128)
    c[:S, C_COS:C_COS + D] = cos
    c[:S, C_SIN:C_SIN + D] = sin
    c[:, C_COST:C_COST + S] = cos.T
    c[:, C_SINT:C_SINT + S] = sin.T
    c[:S, C_MASK:C_MASK + S] = np.where(np.triu(np.ones((S, S)), 1) > 0, np.float32(-1e30), np.float32(0))
    c[:KC, C_ONE:C_ONE + NC] = (np.arange(CTXP) < CTX).reshape(NC, KC).T
    return c


class Steps:

    def __init__(self, eng, sem):
        self.eng, self.sem, self.n, self.turn, self.per = eng, sem, 0, 0, 0

    def did(self, ins):
        ins.then_inc(self.sem, 1)
        self.n += 1

    def wait(self, back=0):
        self.eng.wait_ge(self.sem, self.turn + (self.n - back))

    def chain(self, ins):
        self.did(ins)
        self.wait()

    def begin(self, i, per):
        self.turn, self.per, self.first = i * per, per, self.n

    def end(self, turns):
        assert self.n - self.first == self.per, (self.n - self.first, self.per)
        self.n += (turns - 1) * self.per
        self.turn = 0


def build(nc, x, wqkv, wo, wx, ctxt, wffn, gains, bcols, consts, out):
    with ExitStack() as ctx:
        def sb(name, shape, dt=F32):
            return ctx.enter_context(nc.sbuf_tensor(name, shape, dt))

        def sem(name):
            return ctx.enter_context(nc.semaphore(name))

        xres = sb("xres", [S, NB, DM])
        cst = sb("cst", [128, C_END])
        idb = sb("idb", [S, S], BF16)
        maskb = sb("maskb", [S, REP, S], BF16)
        gain = sb("gain", [S, 4 * D])
        bcol = sb("bcol", [128, 4])
        stageb = sb("stageb", [128, 2 * KT * 512])
        stage = stageb[:, :].rearrange("p (t k n) -> p t k n", t=2, k=KT)
        ropeA = sb("ropeA", [S, 2, D])
        ropeB = sb("ropeB", [S, 2, D])
        ropeC = sb("ropeC", [128, 2, S])
        wmean = sb("wmean", [128, KT * 4])
        wxh = sb("wxh", [128, 3, KT, 512], F16)
        wxl = sb("wxl", [128, 3, KT, 512], F16)
        arena = sb("arena", [128, 20480])

        region2 = sb("region2", [128, 5 * 512])
        region3 = sb("region3", [128, H * S])

        def carver(region=arena):
            at = [0]

            def carve(shape, dt=F32):
                n = int(np.prod(shape[1:]))
                words = n * (2 if dt in (F16, BF16) else 4) // 4
                v = region[0:shape[0], at[0]:at[0] + words]
                at[0] += words
                if dt != F32:
                    v = v.bitcast(dt)
                names = "abcd"[:len(shape) - 1]
                if len(names) > 1:
                    v = v.rearrange(f"p ({' '.join(names)}) -> p {' '.join(names)}",
                                    **{k: n for k, n in zip(names[1:], shape[2:])})
                return v
            return carve

        carve = carver()
        wqh = carve([128, 6, KT, 512], F16)
        wql = carve([128, 6, KT, 512], F16)
        woh = carve([128, H, DM], F16)
        wol = carve([128, H, DM], F16)
        carve = carver()
        raw = [carve([KC, 4, 512]) for _ in range(2)]
        ctxs = carve([128, KT, CTXP])
        ch = carve([128, KT, CTXP], F16)
        cl = carve([128, KT, CTXP], F16)
        kn = [carve([KC, NC * GH, XD]) for _ in range(2)]
        kst = [carve([KC, NC, GH * 4 * XD], F16) for _ in range(2)]
        kT = [carve([128, 2 * NC, KC], F16) for _ in range(2)]
        qbd = [carve([128, 2, 2 * S], F16) for _ in range(2)]
        qn = carve([S, 512])
        qst = [carve([S, XH, 4, XD], F16) for _ in range(2)]
        vst = [carve([KC, NC, XH * VW + 0], F16) for _ in range(2)]
        eb = [carve([KC, NC, GH * S]) for _ in range(2)]
        eh = [carve([KC, NC, GH * S], F16) for _ in range(2)]
        el = [carve([KC, NC, GH * S], F16) for _ in range(2)]
        carve = carver(stageb)
        pT = carve([S, H * S])
        ah = carve([128, H, S], F16)
        al = carve([128, H, S], F16)
        carve = carver(region3)
        pr = carve([S, H * S])
        carve = carver(region3)
        ob = carve([S, XH, VW])
        osum = carve([S, DM])
        carve = carver(region2)
        zb = carve([S, 5, 512])
        carve = carver(region2)
        xsq = carve([KC, 2, 512])
        xssq = carve([KC, 128])
        xrstd = [carve([KC, 128]) for _ in range(2)]
        xnw = carve([KC, 2, 128])
        oinv = carve([S, XH])
        carve = carver()
        wf = carve([128, 12, 4, 512], BF16)
        fh = carve([128, KT, UB * S], F16)
        fl = carve([128, KT, UB * S], F16)
        sg = [carve([128, UB * S]) for _ in range(2)]
        hd = [carve([128, UB * S]) for _ in range(2)]
        hh = [carve([128, UB * S], F16) for _ in range(2)]
        hl = [carve([128, UB * S], F16) for _ in range(2)]
        wgt = carve([128, 2048], BF16)
        asum = sb("asum", [128, 12])
        fsc = sb("fsc", [128, 16])
        idh = sb("idh", [128, 128], F16)
        statc = sb("statc", [S, 6])
        stats = sb("stats", [S, 6])
        mv = sb("mv", [S, 2])
        ms1 = sb("ms1", [S, 1])
        nwt = sb("nwt", [128, 3, 32])
        rs1 = sb("rs1", [S, 1])
        xn = sb("xn", [S, DM])
        xh = sb("xh", [128, KT, S], F16)
        xl = sb("xl", [128, KT, S], F16)
        sq = sb("sq", [S, 2, 512])
        tb = sb("tb", [S, 2, 512])
        ub = sb("ub", [S, 2, 512])
        ssq = sb("ssq", [S, 5 * 4 + 1])
        rstd = sb("rstd", [S, 5 * 4 + 1])
        qk = sb("qk", [128, 5, REP, S])
        vv = sb("vv", [S, HKV * D])
        smax = sb("smax", [S, H])
        negm = sb("negm", [S, H])
        rsum = sb("rsum", [S, H])
        rinv = sb("rinv", [S, H])

        A = [ctx.enter_context(nc.psum_tensor(f"A{i}", [128, 512], F32)) for i in range(2)]
        B = [ctx.enter_context(nc.psum_tensor(f"B{i}", [128, 512], F32)) for i in range(2)]
        C = [ctx.enter_context(nc.psum_tensor(f"C{i}", [128, 512], F32)) for i in range(4)]

        ld_c = sem("ld_c")
        ld_x0 = sem("ld_x0")
        ld_x = sem("ld_x")
        ld_w = [sem("ld_w0"), sem("ld_w1")]
        g_setup = sem("g_setup")
        d_tab = sem("d_tab")
        d_wmean, g_wcen, a_whi, d_wlo = sem("d_wmean"), sem("g_wcen"), sem("a_whi"), sem("d_wlo")
        d_step = sem("d_step")
        g_step = sem("g_step")
        PER = dict(pe_xT=1, pe_qkv=6, pe_zT=5, pe_s=4, pe_pT=4, pe_av=4, pe_o=1,
                   a_xhi=1, a_sq=5, a_v=1, a_exp=16, a_pT=4, a_ahi=4,
                   d_xn=1, d_zT=5, d_xlo=1, d_negm=4, d_t=5, d_u=5, d_ssq=5, d_rstd=1, d_rinv=4,
                   d_alo=4, d_x1=1, g_w=5, g_z=5, g_p=4,
                   pe_xT2=1, pe_proj=7, pe_T=8, pe_sc=24, pe_pv=8,
                   a_ctx=1, a_x2=1, a_raw=4, a_sq2=4, a_qst=1, a_v2=3, a_kst=8, a_e=24, a_ob=4,
                   d_xn2=1, d_ctx=1, d_x2=1, d_ssq2=4, d_rstd2=1, d_qst=1, d_v2=3, d_kst=8, d_T=8,
                   d_eh=8, d_el=8, d_x2out=1,
                   g_kn=8, g_el=8, g_qn=1,
                   pe_xT3=4, pe_up=16, pe_dn=16, a_x3=4, a_sg=16, a_hh=16,
                   d_xn3=4, d_x3=4, d_hd=16, d_hl=16, d_y=4)
        sig = {n: sem(n) for n in PER}
        OWNER = {"p": "tensor", "a": "scalar", "d": "vector", "g": "gpsimd"}

        def credit(eng, who):
            for n in PER:
                if n[0] == who:
                    eng.sem_inc(sig[n], PER[n])

        def wait(eng, name, b, n):
            eng.wait_ge(sig[name], (b + 1) * PER[name] + n)

        wchunks = 6 + 4 + 3
        ld_ctx, g_zero, st_y = sem("ld_ctx"), sem("g_zero"), sem("st_y")
        ld_f = [sem("ld_f0"), sem("ld_f1")]
        a_abs, g_sum, d_fsc, d_tern = sem("a_abs"), sem("g_sum"), sem("d_fsc"), sem("d_tern")

        def later(b, m, k):
            return b + (m + k) // NG, (m + k) % NG

        def two_ways(eng, turn, st=None, per=0):
            with eng.Fori(0, NB // 2 - 1) as i:
                if st:
                    st.begin(i, per)
                turn(i * 2, 0, 0)
                turn(i * 2 + 1, 1, 0)
            if st:
                st.end(NB // 2 - 1)
            turn(NB - 2, 0, 1)
            turn(NB - 1, 1, 2)

        block = ctx.enter_context(nc.Block())

        @block.sync
        def _(sp):
            sp.dma_start(cst[:], consts).then_inc(ld_c, 16)
            sp.dma_start(gain[:], gains).then_inc(ld_c, 16)
            sp.dma_start(bcol[:], bcols).then_inc(ld_c, 16)
            xt = x.rearrange("(b p) f -> p b f", b=NB)
            sp.dma_start(xres[:, 0, :], xt[:, 0, :]).then_inc(ld_x0, 16)
            for j in range(wchunks):
                if j >= 2:
                    sp.wait_ge(a_whi, j - 1)
                    sp.wait_ge(d_wlo, j - 1)
                src = wqkv[:, j] if j < 6 else wo[:, j - 6] if j < 10 else wx[:, j - 10]
                sp.dma_start(stage[:, j % 2], src).then_inc(ld_w[j % 2], 16)
                if j == 1:
                    sp.dma_start(xres[:, 1:NB, :], xt[:, 1:NB, :]).then_inc(ld_x, 16)
            sp.wait_ge(sig["d_x1"], NB + 1)
            sp.wait_ge(g_zero, 1)
            with sp.Fori(0, NB) as b:
                wait(sp, "a_ctx", b - 1, 1)
                wait(sp, "d_ctx", b - 1, 1)
                sp.dma_start(ctxs[:, :, 0:CTX], ctxt[b]).then_inc(ld_ctx, 16)
            sp.wait_ge(sig["d_x2out"], NB + 1)
            for n in range(24):
                if 2 <= n < 14:
                    sp.wait_ge(a_abs, n - 1)
                elif n >= 14:
                    sp.wait_ge(d_tern, n - 13)
                sp.dma_start(stage[:, n % 2], wffn[:, n % 12]).then_inc(ld_f[n % 2], 16)
            with sp.Fori(0, NB // UB) as u:
                for r in range(UB):
                    wait(sp, "d_y", u, r + 1)
                    sp.dma_start(out.rearrange("(b p) f -> p b f", b=NB)[:, u * UB + r, :],
                                 xres[:, u * UB + r, :]).then_inc(st_y, 16)
            sp.wait_ge(st_y, 16 * NB)

        @block.gpsimd
        def _(pool):
            credit(pool, "g")
            pool.wait_ge(ld_c, 48)
            pool.tensor_copy(idh[:], cst[:, C_ID:C_ID + 128]).then_inc(g_setup, 1)
            pool.tensor_copy(idb[:], cst[0:S, C_ID:C_ID + S]).then_inc(g_setup, 1)
            m = cst[0:S, C_MASK:C_MASK + S].unsqueeze(1).broadcast_to([S, REP, S])
            pool.tensor_copy(maskb[:], m).then_inc(g_setup, 1)
            for j in range(5):
                pool.wait_ge(d_wmean, j + 1)
                w = stage[:, j % 2].rearrange("p k (h d) -> p (k h) d", h=4)
                pool.tensor_tensor(w, w, wmean[:].unsqueeze(2).broadcast_to([128, KT * 4, D]),
                                   ALU.subtract).then_inc(g_wcen, 1)

            def w_of(b, j):
                wait(pool, "d_t", b, j + 1)
                wait(pool, "d_u", b, j + 1)
                if j == 0:
                    wait(pool, "pe_zT", b - 1, 5)
                pool.tensor_tensor(zb[:, j], tb[:, j % 2], ub[:, j % 2], ALU.add).then_inc(sig["g_w"], 1)

            def z_of(b, j):
                wait(pool, "d_rstd", b, 1)
                wait(pool, "g_w", b, j + 1)
                r = rstd[:, 4 * j:4 * j + 4].unsqueeze(2).broadcast_to([S, 4, D])
                z = zb[:, j].rearrange("p (h d) -> p h d", h=4)
                pool.tensor_tensor(z, z, r, ALU.mult).then_inc(sig["g_z"], 1)

            def p_of(b, g):
                wait(pool, "d_rinv", b, g + 1)
                p = pr[:, g * 400:(g + 1) * 400].rearrange("p (h k) -> p h k", h=4)
                r = rinv[:, 4 * g:4 * g + 4].unsqueeze(2).broadcast_to([S, 4, S])
                pool.tensor_tensor(p, p, r, ALU.mult).then_inc(sig["g_p"], 1)

            for j in range(5):
                w_of(0, j)
            for j in range(5):
                z_of(0, j)

            def turn(b, last=False):
                for what, j in (("w", 0), ("w", 1), ("p", 0), ("w", 2), ("p", 1), ("p", 2), ("w", 3), ("p", 3), ("w", 4)):
                    if what == "p":
                        p_of(b, j)
                    elif not last:
                        w_of(b + 1, j)
                if not last:
                    for j in range(5):
                        z_of(b + 1, j)

            with pool.Fori(0, NB - 1) as b:
                turn(b)
            turn(NB - 1, last=True)

            pool.wait_ge(sig["d_x1"], NB + 1)
            pool.memset(ctxs[:, :, CTX:CTXP], 0.0).then_inc(g_zero, 1)
            for p in range(2):
                one = cst[0:KC, C_ONE:C_ONE + NC].unsqueeze(2).broadcast_to([KC, NC, XH])
                pool.tensor_copy(vst[p].rearrange("p c (h v) -> p c h v", h=XH)[:, :, :, 2 * XD], one)\
                    .then_inc(g_zero, 1)
                pool.memset(qbd[p], 0.0).then_inc(g_zero, 1)
            pool.memset(xssq[:], 1.0).then_inc(g_zero, 1)
            pool.memset(el[1][:, 0:2], 0.0).then_inc(g_zero, 1)

            def q_normed(b, par):
                wait(pool, "d_rstd2", b, 1)
                wait(pool, "d_qst", b - 1, 1)
                wait(pool, "a_qst", b - 1, 1)
                r = xrstd[par][0:S, 96:128].unsqueeze(2).broadcast_to([S, XH, XD])
                pool.tensor_tensor(qn.rearrange("p (h d) -> p h d", h=XH),
                                   raw[par][0:S, 3].rearrange("p (h d) -> p h d", h=XH), r,
                                   ALU.mult).then_inc(sig["g_qn"], 1)

            def k_normed(b, m, par):
                wait(pool, "d_rstd2", b, 1)
                bb, mm = later(b, m, -2)
                wait(pool, "a_kst", bb, mm + 1)
                wait(pool, "d_kst", bb, mm + 1)
                for c in range(NC):
                    r = xrstd[par][:, c * XH + m * GH:c * XH + (m + 1) * GH].unsqueeze(2).broadcast_to([KC, GH, XD])
                    ins = pool.tensor_tensor(kn[m % 2][:, c * GH:(c + 1) * GH, :],
                                             raw[par][:, c, m * GH * XD:(m + 1) * GH * XD]
                                             .rearrange("p (h d) -> p h d", h=GH), r, ALU.mult)
                ins.then_inc(sig["g_kn"], 1)

            def e_low(b, m):
                wait(pool, "d_eh", b, m + 1)
                bb, mm = later(b, m, -2)
                wait(pool, "pe_pv", bb, mm + 1)
                pool.tensor_tensor(el[m % 2][:, 0:2], eb[m % 2][:, 0:2], eh[m % 2][:, 0:2], ALU.subtract)\
                    .then_inc(sig["g_el"], 1)

            q_normed(0, 0)
            for m in range(3):
                k_normed(0, m, 0)
            e_low(0, 0)

            def turn(b, par, end):
                for m in range(NG):
                    bb, mm = later(b, m, 3)
                    if mm == 0 and end < 2:
                        q_normed(b + 1, 1 - par)
                    if mm > 2 or end < 2:
                        k_normed(bb, mm, par if mm > 2 else 1 - par)
                    bb, mm = later(b, m, 1)
                    if mm > 0 or end < 2:
                        e_low(bb, mm)

            two_ways(pool, turn)

            for w in range(3):
                pool.wait_ge(d_fsc, w + 1)
                pool.partition_all_reduce(fsc[:, 3 + w:4 + w], fsc[:, w:w + 1], 128,
                                          bass.bass_isa.ReduceOp.add).then_inc(g_sum, 1)

        @block.scalar
        def _(act):
            credit(act, "a")

            def w_hi(j):
                if j < 5:
                    act.wait_ge(g_wcen, j + 1)
                else:
                    act.wait_ge(ld_w[j % 2], 16 * (j // 2 + 1))
                dst = wqh[:, j] if j < 6 else woh[:, 4 * (j - 6):4 * (j - 5), :] if j < 10 else wxh[:, j - 10]
                act.activation(dst, stage[:, j % 2], ACT.Copy, scale=SW).then_inc(a_whi, 1)

            def x_hi(b):
                wait(act, "pe_xT", b, 1)
                wait(act, "pe_qkv", b - 1, 6)
                act.activation(xh[:], B[1][:, 0:KT * S].rearrange("p (k s) -> p k s", k=KT), ACT.Copy)\
                   .then_inc(sig["a_xhi"], 1)

            def square(b, j):
                wait(act, "pe_qkv", b, j + 1)
                if j >= 2:
                    wait(act, "d_ssq", b, j - 1)
                else:
                    wait(act, "d_ssq", b - 1, 4 + j)
                act.activation(sq[:, j % 2], A[j % 2][0:S, :], ACT.Square).then_inc(sig["a_sq"], 1)

            def v_of(b):
                wait(act, "pe_qkv", b, 6)
                wait(act, "pe_av", b - 1, 4)
                act.activation(vv[:], A[1][0:S, :], ACT.Copy, scale=1.0 / (SX * SW)).then_inc(sig["a_v"], 1)

            def exps(b, g):
                wait(act, "d_negm", b, g + 1)
                if g == 0:
                    wait(act, "pe_pT", b - 1, 4)
                    wait(act, "d_rinv", b - 1, 4)
                for h in range(4):
                    n = 4 * g + h
                    act.activation(pr[:, n * S:(n + 1) * S], C[g][0:S, h * S:(h + 1) * S], ACT.Exp,
                                   bias=negm[:, n:n + 1], scale=float(D) ** -0.5,
                                   accum_out=rsum[:, n:n + 1]).then_inc(sig["a_exp"], 1)

            def p_back(b, g):
                wait(act, "pe_pT", b, g + 1)
                wait(act, "pe_av", b - 1, g + 1)
                act.activation(pT[:, g * 400:(g + 1) * 400], B[g % 2][0:S, 0:400], ACT.Copy)\
                   .then_inc(sig["a_pT"], 1)

            def a_hi(b, g):
                wait(act, "pe_av", b, g + 1)
                wait(act, "pe_o", b - 1, 1)
                act.activation(ah[:, 4 * g:4 * g + 4, :], C[g][:, 0:400].rearrange("p (h s) -> p h s", h=4),
                               ACT.Copy, scale=SA).then_inc(sig["a_ahi"], 1)

            for j in range(6):
                w_hi(j)
            x_hi(0)
            for j in range(5):
                square(0, j)
            v_of(0)
            for j in range(6, wchunks):
                w_hi(j)

            def turn(b, last=False):
                if not last:
                    x_hi(b + 1)
                for g in range(4):
                    exps(b, g)
                    if not last:
                        square(b + 1, g)
                if not last:
                    square(b + 1, 4)
                for g in range(4):
                    p_back(b, g)
                for g in range(4):
                    a_hi(b, g)
                if not last:
                    v_of(b + 1)

            with act.Fori(0, NB - 1) as b:
                turn(b)
            turn(NB - 1, last=True)

            act.wait_ge(sig["d_x1"], NB + 1)
            act.wait_ge(g_zero, 7)

            def ctx_hi(b):
                act.wait_ge(ld_ctx, (b + 1) * 16)
                wait(act, "pe_proj", b - 1, 7)
                act.activation(ch, ctxs, ACT.Copy, scale=SX).then_inc(sig["a_ctx"], 1)

            def x2_hi(b):
                wait(act, "pe_xT2", b, 1)
                wait(act, "pe_proj", b - 1, 1)
                act.activation(xh[:], A[1][:, 0:KT * S].rearrange("p (k s) -> p k s", k=KT), ACT.Copy)\
                   .then_inc(sig["a_x2"], 1)

            def keep_raw(b, n, par):
                wait(act, "pe_proj", b, n + 1)
                rows, slot = (S, 3) if n == 0 else (KC, n - 1)
                if n == 0:
                    wait(act, "g_kn", b - 2, 8)
                    wait(act, "g_qn", b - 2, 1)
                act.activation(raw[par][0:rows, slot], A[n % 2][0:rows, :], ACT.Copy).then_inc(sig["a_raw"], 1)
                if n >= 2:
                    wait(act, "d_ssq2", b, n - 1)
                else:
                    wait(act, "d_ssq2", b - 1, n + 3)
                act.activation(xsq[0:rows, n % 2], A[n % 2][0:rows, :], ACT.Square).then_inc(sig["a_sq2"], 1)

            def v2_hi(b, c, par):
                wait(act, "pe_proj", b, 5 + c)
                if c == 0:
                    wait(act, "pe_pv", b - 2, 8)
                act.activation(vst[par][:, c].rearrange("p (h v) -> p h v", h=XH)[:, :, 0:XD],
                               A[c % 2][0:KC, :].rearrange("p (h d) -> p h d", h=XH), ACT.Copy, scale=SV)\
                   .then_inc(sig["a_v2"], 1)

            def q_stack(b, par):
                wait(act, "g_qn", b, 1)
                wait(act, "pe_T", b - 2, 8)
                act.activation(qst[par].rearrange("p h (u w) d -> p h u w d", u=2)[:, :, :, 0, :],
                               qn.rearrange("p (h d) -> p h d", h=XH).unsqueeze(2).broadcast_to([S, XH, 2, XD]),
                               ACT.Copy).then_inc(sig["a_qst"], 1)

            def k_stack(b, m):
                wait(act, "g_kn", b, m + 1)
                bb, mm = later(b, m, -2)
                wait(act, "pe_T", bb, mm + 1)
                act.activation(kst[m % 2].rearrange("p c (h u d) -> p (c h) u d", h=GH, u=4)[:, :, 0:2, :],
                               kn[m % 2].unsqueeze(2).broadcast_to([KC, NC * GH, 2, XD]), ACT.Copy)\
                   .then_inc(sig["a_kst"], 1)

            def exp2(b, m):
                for c in range(NC):
                    wait(act, "pe_sc", b, m * NC + c + 1)
                    if c == 0:
                        bb, mm = later(b, m, -2)
                        wait(act, "g_el", bb, mm + 1)
                        wait(act, "d_el", bb, mm + 1)
                    act.activation(eb[m % 2][:, c], C[(m * NC + c) % 4][0:KC, 0:GH * S], ACT.Exp,
                                   scale=float(XD) ** -0.5 / SN ** 2).then_inc(sig["a_e"], 1)

            def out_back(b, n):
                wait(act, "pe_pv", b, 2 * n + 2)
                if n == 0:
                    wait(act, "d_x2out", b - 1, 1)
                act.activation(ob[:, 8 * n:8 * n + 8, :], B[1][0:S, 0:8 * VW].rearrange("p (h v) -> p h v", h=8),
                               ACT.Copy).then_inc(sig["a_ob"], 1)

            ctx_hi(0)
            x2_hi(0)
            for n in range(4):
                keep_raw(0, n, 0)
            for c in range(NC):
                v2_hi(0, c, 0)
            ctx_hi(1)
            x2_hi(1)
            q_stack(0, 0)
            for m in range(3):
                k_stack(0, m)
            exp2(0, 0)

            def turn(b, par, end):
                for m in range(NG):
                    bb, mm = later(b, m, 3)
                    if mm == 0 and end < 2:
                        q_stack(b + 1, 1 - par)
                    if mm > 2 or end < 2:
                        k_stack(bb, mm)
                    bb, mm = later(b, m, 1)
                    if mm > 0 or end < 2:
                        exp2(bb, mm)
                    if end < 2:
                        if m < 4:
                            keep_raw(b + 1, m, 1 - par)
                        elif m < 7:
                            v2_hi(b + 1, m - 4, 1 - par)
                        elif end < 1:
                            ctx_hi(b + 2)
                            x2_hi(b + 2)
                    if m % 2:
                        out_back(b, m // 2)

            two_ways(act, turn)

            for n in range(12):
                act.wait_ge(ld_f[n % 2], 16 * (n // 2 + 1))
                act.activation(arena[:, 12288:14336].rearrange("p (k n) -> p k n", k=4), stage[:, n % 2], ACT.Abs,
                               accum_out=asum[:, n:n + 1]).then_inc(a_abs, 1)
                act.wait_ge(a_abs, n + 1)

            def x3_hi(u, r):
                wait(act, "pe_xT3", u, r + 1)
                wait(act, "pe_up", u - 1, 16)
                act.activation(fh[:, :, r * S:(r + 1) * S], C[r][:, 0:KT * S].rearrange("p (k s) -> p k s", k=KT),
                               ACT.Copy).then_inc(sig["a_x3"], 1)

            def silu(u, e):
                wait(act, "pe_up", u, e + 1)
                if e >= 2:
                    wait(act, "d_hd", u, e - 1)
                else:
                    wait(act, "d_hd", u - 1, 15 + e)
                act.activation(sg[e % 2], C[2 * (e % 2)][:, 0:UB * S], ACT.Silu, scale=fsc[:, 6:7])\
                   .then_inc(sig["a_sg"], 1)

            def hidden_hi(u, e):
                wait(act, "d_hd", u, e + 1)
                if e >= 2:
                    wait(act, "pe_dn", u, e - 1)
                else:
                    wait(act, "pe_dn", u - 1, 15 + e)
                act.activation(hh[e % 2], hd[e % 2], ACT.Copy).then_inc(sig["a_hh"], 1)

            act.wait_ge(d_tern, 12)
            for r in range(UB):
                x3_hi(0, r)

            def unit(u, last=False):
                silu(u, 0)
                for e in range(ET):
                    hidden_hi(u, e)
                    if e + 1 < ET:
                        silu(u, e + 1)
                if not last:
                    for r in range(UB):
                        x3_hi(u + 1, r)

            with act.Fori(0, NB // UB - 1) as u:
                unit(u)
            unit(NB // UB - 1, last=True)

        @block.vector
        def _(dve):
            credit(dve, "d")
            st = Steps(dve, d_step)

            def rsqrt(y, v, n, p=S):
                a, c = nwt[0:p, 0, 0:n], nwt[0:p, 1, 0:n]
                st.chain(dve.tensor_scalar(y.bitcast(I32), v.bitcast(I32), 1, None, ALU.logical_shift_right))
                st.chain(dve.tensor_scalar(y.bitcast(I32), y.bitcast(I32), -1, 0x5f3759df, ALU.mult, ALU.add))
                for _ in range(3):
                    st.chain(dve.scalar_tensor_tensor(a, y, -0.5, y, ALU.mult, ALU.mult))
                    st.chain(dve.tensor_tensor(c, a, v, ALU.mult))
                    ins = dve.scalar_tensor_tensor(y, c, 1.5, y, ALU.add, ALU.mult)
                    if _ < 2:
                        st.chain(ins)
                return ins

            def row_stats(b, var):
                st.chain(dve.bn_stats(stats[:], xres[:, b, :]))
                st.did(dve.tensor_copy(statc[:], stats[:]))
                st.chain(dve.bn_aggr(mv[:], stats[:]))
                st.did(dve.tensor_scalar(var, mv[:, 1:2], EPS_LN, SX ** -2, ALU.add, ALU.mult))

            def normed(b, rs):
                wait(dve, "pe_xT", b - 1, 1)
                dve.tensor_scalar(xn[:], xres[:, b, :], mv[:, 0:1], rs, ALU.subtract, ALU.mult)\
                   .then_inc(sig["d_xn"], 1)

            def x_lo(b):
                wait(dve, "a_xhi", b, 1)
                wait(dve, "pe_qkv", b - 1, 6)
                dve.tensor_tensor(xl[:], B[1][:, 0:KT * S].rearrange("p (k s) -> p k s", k=KT), xh[:],
                                  ALU.subtract).then_inc(sig["d_xlo"], 1)

            def proj(b, j):
                wait(dve, "pe_qkv", b, j + 1)
                wait(dve, "a_sq", b, j + 1)
                if j >= 2:
                    wait(dve, "g_w", b, j - 1)
                else:
                    wait(dve, "g_w", b - 1, 4 + j)
                which = 0 if j == 0 else 1
                bank = A[j % 2][0:S, :].rearrange("p (h d) -> p h d", h=4)
                t = tb[:, j % 2].rearrange("p (h d) -> p h d", h=4)
                u = ub[:, j % 2].rearrange("p (h d) -> p h d", h=4)

                def table(tab, lo, hi):
                    return tab[:, which, lo:hi].unsqueeze(1).broadcast_to([S, 4, hi - lo])

                dve.tensor_tensor(t, bank, table(ropeA, 0, D), ALU.mult).then_inc(sig["d_t"], 1)
                st.did(dve.tensor_tensor(u[:, :, 0:HALF], bank[:, :, HALF:D], table(ropeB, 0, HALF), ALU.mult))
                dve.tensor_tensor(u[:, :, HALF:D], bank[:, :, 0:HALF], table(ropeB, HALF, D), ALU.mult)\
                   .then_inc(sig["d_u"], 1)
                if j == 0:
                    wait(dve, "d_rstd", b - 1, 1)
                dve.tensor_reduce(ssq[:, 4 * j:4 * j + 4], sq[:, j % 2].rearrange("p (h d) -> p h d", h=4),
                                  AX.X, ALU.add).then_inc(sig["d_ssq"], 1)

            def head_norm(b):
                wait(dve, "d_ssq", b, 5)
                st.chain(dve.tensor_scalar(ssq[:, 0:20], ssq[:, 0:20], 1.0 / D, EPS_LN * (SX * SW) ** 2,
                                           ALU.mult, ALU.add))
                wait(dve, "g_z", b - 1, 5)
                rsqrt(rstd[:], ssq[:], 21).then_inc(sig["d_rstd"], 1)
                wait(dve, "d_rstd", b, 1)

            def z_back(b, g):
                wait(dve, "pe_zT", b, g + 1)
                if g == 0:
                    wait(dve, "pe_s", b - 1, 4)
                c = ropeC[:, 0 if g == 0 else 1, :].unsqueeze(1).broadcast_to([128, 4, S])
                dve.tensor_tensor(qk[:, g], B[g % 2][:, 0:400].rearrange("p (h s) -> p h s", h=4), c,
                                  ALU.add).then_inc(sig["d_zT"], 1)

            def row_max(b, g):
                wait(dve, "pe_s", b, g + 1)
                if g == 0:
                    wait(dve, "a_exp", b - 1, 16)
                st.chain(dve.tensor_reduce(smax[:, 4 * g:4 * g + 4],
                                           C[g][0:S, 0:400].rearrange("p (h k) -> p h k", h=4), AX.X, ALU.max))
                dve.tensor_scalar(negm[:, 4 * g:4 * g + 4], smax[:, 4 * g:4 * g + 4], -float(D) ** -0.5, None,
                                  ALU.mult).then_inc(sig["d_negm"], 1)

            def sums(b, g):
                wait(dve, "a_exp", b, 4 * g + 4)
                if g == 0:
                    wait(dve, "g_p", b - 1, 4)
                dve.reciprocal(rinv[:, 4 * g:4 * g + 4], rsum[:, 4 * g:4 * g + 4]).then_inc(sig["d_rinv"], 1)

            def a_lo(b, g):
                wait(dve, "a_ahi", b, g + 1)
                dve.scalar_tensor_tensor(al[:, 4 * g:4 * g + 4, :],
                                         C[g][:, 0:400].rearrange("p (h s) -> p h s", h=4), SA,
                                         ah[:, 4 * g:4 * g + 4, :], ALU.mult, ALU.subtract)\
                   .then_inc(sig["d_alo"], 1)

            def add_attn(b):
                wait(dve, "pe_o", b, 1)
                dve.scalar_tensor_tensor(xres[:, b, :], A[0][0:S, :], 1.0 / (SA * SW), xres[:, b, :],
                                         ALU.mult, ALU.add).then_inc(sig["d_x1"], 1)

            dve.wait_ge(ld_x0, 16)
            row_stats(0, ms1[:])
            st.wait()
            st.chain(rsqrt(rs1[:], ms1[:], 1))
            normed(0, rs1[:, 0:1])
            dve.wait_ge(ld_c, 48)
            for w, g in ((0, 2), (1, 0)):
                dve.tensor_tensor(ropeA[:, w], gain[:, g * D:(g + 1) * D], cst[0:S, C_COS:C_COS + D],
                                  ALU.mult).then_inc(d_tab, 1)
                dve.tensor_tensor(ropeB[:, w], gain[:, (g + 1) * D:(g + 2) * D], cst[0:S, C_SIN:C_SIN + D],
                                  ALU.mult).then_inc(d_tab, 1)
                st.chain(dve.tensor_scalar(ropeC[:, w], cst[:, C_COST:C_COST + S], bcol[:, g:g + 1], None, ALU.mult))
                dve.scalar_tensor_tensor(ropeC[:, w], cst[:, C_SINT:C_SINT + S], bcol[:, g + 1:g + 2],
                                         ropeC[:, w], ALU.mult, ALU.add).then_inc(d_tab, 1)
            dve.wait_ge(d_tab, 6)

            def w_mean(j):
                dve.wait_ge(ld_w[j % 2], 16 * (j // 2 + 1))
                if j > 0:
                    dve.wait_ge(g_wcen, j)
                st.chain(dve.tensor_reduce(wmean[:], stage[:, j % 2].rearrange("p k (h d) -> p (k h) d", h=4),
                                           AX.X, ALU.add))
                dve.tensor_scalar(wmean[:], wmean[:], 1.0 / D, None, ALU.mult).then_inc(d_wmean, 1)

            def w_lo(j):
                dve.wait_ge(a_whi, j + 1)
                dst, hi = (wql[:, j], wqh[:, j]) if j < 6 else (
                    wol[:, 4 * (j - 6):4 * (j - 5), :], woh[:, 4 * (j - 6):4 * (j - 5), :]) if j < 10 else (
                    wxl[:, j - 10], wxh[:, j - 10])
                dve.scalar_tensor_tensor(dst.rearrange("p k n -> p (k n)"),
                                         stage[:, j % 2].rearrange("p k n -> p (k n)"), SW,
                                         hi.rearrange("p k n -> p (k n)"), ALU.mult, ALU.subtract)\
                   .then_inc(d_wlo, 1)

            w_mean(0)
            for j in range(6):
                if j + 1 < 5:
                    w_mean(j + 1)
                w_lo(j)
            x_lo(0)
            for j in range(5):
                proj(0, j)
            dve.wait_ge(ld_x, 16)
            row_stats(1, ssq[:, 20:21])
            head_norm(0)
            normed(1, rstd[:, 20:21])
            for j in range(6, wchunks):
                w_lo(j)
            for g in range(2):
                z_back(0, g)

            def turn(b, end=0):
                for g in range(2, 5):
                    z_back(b, g)
                row_max(b, 0)
                if end < 2:
                    x_lo(b + 1)
                for g in range(1, 4):
                    row_max(b, g)
                for g in range(4):
                    if end < 2:
                        proj(b + 1, g)
                    sums(b, g)
                if end < 1:
                    row_stats(b + 2, ssq[:, 20:21])
                if end < 2:
                    proj(b + 1, 4)
                    head_norm(b + 1)
                if end < 1:
                    normed(b + 2, rstd[:, 20:21])
                for g in range(4):
                    a_lo(b, g)
                if end < 2:
                    for g in range(2):
                        z_back(b + 1, g)
                add_attn(b)

            with dve.Fori(0, NB - 2) as b:
                st.begin(b, 24)
                turn(b)
            st.end(NB - 2)
            turn(NB - 2, 1)
            turn(NB - 1, 2)

            dve.wait_ge(g_zero, 7)

            def rsqrt2(y, v):
                a, c = xnw[:, 0, :], xnw[:, 1, :]
                st.chain(dve.tensor_scalar(y.bitcast(I32), v.bitcast(I32), 1, None, ALU.logical_shift_right))
                st.chain(dve.tensor_scalar(y.bitcast(I32), y.bitcast(I32), -1, 0x5f3759df, ALU.mult, ALU.add))
                for n in range(3):
                    st.chain(dve.scalar_tensor_tensor(a, y, -0.5, y, ALU.mult, ALU.mult))
                    st.chain(dve.tensor_tensor(c, a, v, ALU.mult))
                    ins = dve.scalar_tensor_tensor(y, c, 1.5, y, ALU.add, ALU.mult)
                    if n < 2:
                        st.chain(ins)
                return ins

            def ctx_lo(b):
                wait(dve, "a_ctx", b, 1)
                wait(dve, "pe_proj", b - 1, 7)
                dve.scalar_tensor_tensor(cl.rearrange("p k n -> p (k n)"), ctxs.rearrange("p k n -> p (k n)"), SX,
                                         ch.rearrange("p k n -> p (k n)"), ALU.mult, ALU.subtract)\
                   .then_inc(sig["d_ctx"], 1)

            def layer_norm2(b):
                st.chain(dve.bn_stats(stats[:], xres[:, b, :]))
                st.did(dve.tensor_copy(statc[:], stats[:]))
                st.chain(dve.bn_aggr(mv[:], stats[:]))
                st.chain(dve.tensor_scalar(ms1[:], mv[:, 1:2], EPS_LN, SX ** -2, ALU.add, ALU.mult))
                st.chain(rsqrt(rs1[:], ms1[:], 1))

            def norm2(b):
                layer_norm2(b)
                wait(dve, "pe_xT2", b - 1, 1)
                dve.tensor_scalar(xn[:], xres[:, b, :], mv[:, 0:1], rs1[:, 0:1], ALU.subtract, ALU.mult)\
                   .then_inc(sig["d_xn2"], 1)

            def x2_lo(b):
                wait(dve, "a_x2", b, 1)
                wait(dve, "pe_proj", b - 1, 1)
                dve.tensor_tensor(xl[:], A[1][:, 0:KT * S].rearrange("p (k s) -> p k s", k=KT), xh[:],
                                  ALU.subtract).then_inc(sig["d_x2"], 1)

            def square_sums(b, n):
                wait(dve, "a_sq2", b, n + 1)
                rows, slot = (S, 3) if n == 0 else (KC, n - 1)
                if n == 0:
                    wait(dve, "d_rstd2", b - 1, 1)
                dve.tensor_reduce(xssq[0:rows, slot * XH:(slot + 1) * XH],
                                  xsq[0:rows, n % 2].rearrange("p (h d) -> p h d", h=XH), AX.X, ALU.add)\
                   .then_inc(sig["d_ssq2"], 1)

            def rms(b, par):
                wait(dve, "d_ssq2", b, 4)
                wait(dve, "g_kn", b - 2, 8)
                wait(dve, "g_qn", b - 2, 1)
                st.chain(dve.tensor_scalar(xssq[:], xssq[:], SN ** -2 / XD, EPS_RMS * (SX * SW / SN) ** 2,
                                           ALU.mult, ALU.add))
                rsqrt2(xrstd[par], xssq).then_inc(sig["d_rstd2"], 1)

            def v2_lo(b, c, par):
                wait(dve, "a_v2", b, c + 1)
                v = vst[par][:, c].rearrange("p (h v) -> p h v", h=XH)
                dve.scalar_tensor_tensor(v[:, :, XD:2 * XD], A[c % 2][0:KC, :].rearrange("p (h d) -> p h d", h=XH), SV,
                                         v[:, :, 0:XD], ALU.mult, ALU.subtract).then_inc(sig["d_v2"], 1)

            def q_stack_lo(b, par):
                wait(dve, "a_qst", b, 1)
                q = qst[par].rearrange("p h (u w) d -> p h u w d", u=2)
                dve.tensor_tensor(q[:, :, :, 1, :],
                                  qn.rearrange("p (h d) -> p h d", h=XH).unsqueeze(2).broadcast_to([S, XH, 2, XD]),
                                  q[:, :, :, 0, :], ALU.subtract).then_inc(sig["d_qst"], 1)

            def k_stack_lo(b, m):
                wait(dve, "a_kst", b, m + 1)
                k = kst[m % 2].rearrange("p c (h u d) -> p (c h) u d", h=GH, u=4)
                dve.tensor_tensor(k[:, :, 2:4, :], kn[m % 2].unsqueeze(2).broadcast_to([KC, NC * GH, 2, XD]),
                                  k[:, :, 0:2, :], ALU.subtract).then_inc(sig["d_kst"], 1)

            def turned_back(b, m):
                wait(dve, "pe_T", b, m + 1)
                bb, mm = later(b, m, -2)
                wait(dve, "pe_sc", bb, mm * NC + NC)
                bank = B[0][:, :].bitcast(F16)
                st.did(dve.tensor_copy(kT[m % 2], bank[:, 0:2 * NC * KC].rearrange("p (n k) -> p n k", n=2 * NC)))
                q = bank[:, 2 * NC * KC:2 * NC * KC + 2 * S].rearrange("p (n s) -> p n s", n=2)
                st.did(dve.tensor_copy(qbd[m % 2][0:64, :, 0:S], q[0:64]))
                dve.tensor_copy(qbd[m % 2][64:128, :, S:2 * S], q[64:128]).then_inc(sig["d_T"], 1)

            def e_high(b, m):
                wait(dve, "a_e", b, NC * (m + 1))
                bb, mm = later(b, m, -2)
                wait(dve, "pe_pv", bb, mm + 1)
                dve.tensor_copy(eh[m % 2], eb[m % 2]).then_inc(sig["d_eh"], 1)
                wait(dve, "d_eh", b, m + 1)
                dve.tensor_tensor(el[m % 2][:, 2], eb[m % 2][:, 2], eh[m % 2][:, 2], ALU.subtract)\
                   .then_inc(sig["d_el"], 1)

            def add_cross(b):
                wait(dve, "a_ob", b, 4)
                st.did(dve.reciprocal(oinv, ob[:, :, 2 * XD]))
                st.chain(dve.tensor_tensor(osum.rearrange("p (h d) -> p h d", h=XH), ob[:, :, 0:XD],
                                           ob[:, :, XD:2 * XD], ALU.add))
                o = osum.rearrange("p (h d) -> p h d", h=XH)
                st.chain(dve.tensor_tensor(o, o, oinv.unsqueeze(2).broadcast_to([S, XH, XD]), ALU.mult))
                dve.scalar_tensor_tensor(xres[:, b, :], osum, 1.0 / (SX * SW * SV), xres[:, b, :],
                                         ALU.mult, ALU.add).then_inc(sig["d_x2out"], 1)

            dve.wait_ge(sig["d_x1"], NB + 1)
            norm2(0)
            ctx_lo(0)
            x2_lo(0)
            norm2(1)
            for n in range(4):
                square_sums(0, n)
            rms(0, 0)
            for c in range(NC):
                v2_lo(0, c, 0)
            ctx_lo(1)
            x2_lo(1)
            q_stack_lo(0, 0)
            for m in range(3):
                k_stack_lo(0, m)
                if m < 2:
                    turned_back(0, m)
            e_high(0, 0)

            def turn(b, par, end):
                for m in range(NG):
                    bb, mm = later(b, m, 3)
                    if mm == 0 and end < 2:
                        q_stack_lo(b + 1, 1 - par)
                    if mm > 2 or end < 2:
                        k_stack_lo(bb, mm)
                    bb, mm = later(b, m, 2)
                    if mm > 1 or end < 2:
                        turned_back(bb, mm)
                    bb, mm = later(b, m, 1)
                    if mm > 0 or end < 2:
                        e_high(bb, mm)
                    if end < 2:
                        if m < 4:
                            square_sums(b + 1, m)
                            if m == 3:
                                rms(b + 1, 1 - par)
                        elif m < 7:
                            v2_lo(b + 1, m - 4, 1 - par)
                            if m == 5 and end < 1:
                                norm2(b + 2)
                        elif end < 1:
                            ctx_lo(b + 2)
                            x2_lo(b + 2)
                add_cross(b)

            two_ways(dve, turn, st, 90)

            dve.wait_ge(a_abs, 12)
            for w in range(3):
                dve.tensor_reduce(fsc[:, w:w + 1], asum[:, 4 * w:4 * w + 4], AX.X, ALU.add).then_inc(d_fsc, 1)
            dve.wait_ge(g_sum, 3)
            st.chain(dve.tensor_scalar(fsc[:, 3:6], fsc[:, 3:6], 1.0 / (FE * DM), 1e-8, ALU.mult, ALU.add))
            st.did(dve.tensor_scalar(fsc[:, 9:12], fsc[:, 3:6], 0.5, None, ALU.mult))
            st.did(dve.tensor_scalar(fsc[:, 12:15], fsc[:, 3:6], -0.5, None, ALU.mult))
            st.did(dve.tensor_scalar(fsc[:, 6:7], fsc[:, 3:4], -1.0 / SX, None, ALU.mult))
            st.chain(dve.reciprocal(fsc[:, 7:8], fsc[:, 3:4]))
            st.did(dve.tensor_scalar(fsc[:, 7:8], fsc[:, 7:8], 1.0 / (SX * SH), None, ALU.mult))
            st.chain(dve.tensor_tensor(fsc[:, 8:9], fsc[:, 3:4], fsc[:, 4:5], ALU.mult))
            st.chain(dve.scalar_tensor_tensor(fsc[:, 8:9], fsc[:, 8:9], SH, fsc[:, 5:6], ALU.mult, ALU.mult))
            for n in range(12):
                dve.wait_ge(ld_f[n % 2], 16 * ((12 + n) // 2 + 1))
                w = stage[:, n % 2].rearrange("p k n -> p (k n)")
                st.chain(dve.tensor_scalar(wgt, w, fsc[:, 9 + n // 4:10 + n // 4], None, ALU.is_gt))
                dve.scalar_tensor_tensor(wf[:, n].rearrange("p k n -> p (k n)"), w, fsc[:, 12 + n // 4:13 + n // 4],
                                         wgt, ALU.is_lt, ALU.subtract).then_inc(d_tern, 1)
                dve.wait_ge(d_tern, n + 1)

            def norm3(u, r):
                layer_norm2(u * UB + r)
                if r == 0:
                    wait(dve, "pe_xT3", u - 1, 4)
                else:
                    wait(dve, "pe_xT3", u, r)
                dve.tensor_scalar(xn[:], xres[:, u * UB + r, :], mv[:, 0:1], rs1[:, 0:1], ALU.subtract, ALU.mult)\
                   .then_inc(sig["d_xn3"], 1)

            def x3_lo(u, r):
                wait(dve, "a_x3", u, r + 1)
                wait(dve, "pe_up", u - 1, 16)
                dve.tensor_tensor(fl[:, :, r * S:(r + 1) * S],
                                  C[r][:, 0:KT * S].rearrange("p (k s) -> p k s", k=KT),
                                  fh[:, :, r * S:(r + 1) * S], ALU.subtract).then_inc(sig["d_x3"], 1)

            def hidden(u, e):
                wait(dve, "a_sg", u, e + 1)
                if e >= 2:
                    wait(dve, "a_hh", u, e - 1)
                    wait(dve, "d_hl", u, e - 1)
                else:
                    wait(dve, "a_hh", u - 1, 15 + e)
                    wait(dve, "d_hl", u - 1, 15 + e)
                dve.scalar_tensor_tensor(hd[e % 2], C[2 * (e % 2) + 1][:, 0:UB * S], fsc[:, 7:8], sg[e % 2],
                                         ALU.mult, ALU.mult).then_inc(sig["d_hd"], 1)

            def hidden_lo(u, e):
                wait(dve, "a_hh", u, e + 1)
                if e >= 2:
                    wait(dve, "pe_dn", u, e - 1)
                else:
                    wait(dve, "pe_dn", u - 1, 15 + e)
                dve.tensor_tensor(hl[e % 2], hd[e % 2], hh[e % 2], ALU.subtract).then_inc(sig["d_hl"], 1)

            for r in range(UB):
                norm3(0, r)
                x3_lo(0, r)

            def unit(u, last=False):
                hidden(u, 0)
                for e in range(ET):
                    hidden_lo(u, e)
                    if e + 1 < ET:
                        hidden(u, e + 1)
                if not last:
                    for r in range(UB):
                        norm3(u + 1, r)
                        x3_lo(u + 1, r)
                for r in range(UB):
                    wait(dve, "pe_dn", u, 16)
                    dve.scalar_tensor_tensor(xres[:, u * UB + r, :], (A + B)[r][0:S, :], fsc[0:S, 8:9],
                                             xres[:, u * UB + r, :], ALU.mult, ALU.add).then_inc(sig["d_y"], 1)

            with dve.Fori(0, NB // UB - 1) as u:
                st.begin(u, 60)
                unit(u)
            st.end(NB // UB - 1)
            unit(NB // UB - 1, last=True)

        @block.tensor
        def _(pe):
            credit(pe, "p")
            ident = cst[0:128, C_ID:C_ID + 128]

            def x_turn(b):
                wait(pe, "d_xn", b, 1)
                wait(pe, "d_zT", b - 1, 4)
                for k in range(KT):
                    ins = pe.transpose(B[1][:, k * S:(k + 1) * S], xn[:, k * 128:(k + 1) * 128], ident[0:S, 0:S])
                ins.then_inc(sig["pe_xT"], 1)

            def project(b, j):
                if j == 0:
                    wait(pe, "a_xhi", b, 1)
                    wait(pe, "d_xlo", b, 1)
                    wait(pe, "d_x1", b - 2, 1)
                elif j == 1:
                    wait(pe, "a_v", b - 1, 1)
                else:
                    wait(pe, "a_sq", b, j - 1)
                    wait(pe, "d_t", b, j - 1)
                    wait(pe, "d_u", b, j - 1)
                n = 0
                for xp, wp in ((xh, wqh), (xh, wql), (xl, wqh)):
                    for k in range(KT):
                        ins = pe.matmul(A[j % 2][0:S, :], xp[:, k, :], wp[:, j, k, :], start=(n == 0), stop=(n == 11))
                        n += 1
                ins.then_inc(sig["pe_qkv"], 1)

            def z_turn(b, g):
                wait(pe, "g_z", b, g + 1)
                if g < 2:
                    wait(pe, "a_pT", b - 1, 3 + g)
                else:
                    wait(pe, "d_zT", b, g - 1)
                for h in range(4):
                    ins = pe.transpose(B[g % 2][:, h * S:(h + 1) * S], zb[:, g, h * D:(h + 1) * D], ident[0:S, 0:S])
                ins.then_inc(sig["pe_zT"], 1)

            def scores(b, g):
                wait(pe, "d_zT", b, g + 2)
                wait(pe, "d_alo", b - 1, g + 1)
                bank = C[g][0:S, 0:400]
                pe.matmul(bank, idb[:], maskb[:].rearrange("p h k -> p (h k)"), start=True, stop=True)
                for h in range(4):
                    ins = pe.matmul(bank[:, h * S:(h + 1) * S], qk[:, g + 1, h, :], qk[:, 0, g, :],
                                    start=False, stop=True, skip_group_check=True)
                ins.then_inc(sig["pe_s"], 1)

            def p_turn(b, g):
                wait(pe, "g_p", b, g + 1)
                if g == 0:
                    wait(pe, "d_zT", b, 5)
                elif g >= 2:
                    wait(pe, "a_pT", b, g - 1)
                for h in range(4):
                    n = 4 * g + h
                    ins = pe.transpose(B[g % 2][0:S, h * S:(h + 1) * S], pr[:, n * S:(n + 1) * S], ident[0:S, 0:S])
                ins.then_inc(sig["pe_pT"], 1)

            def attend(b, g):
                wait(pe, "a_pT", b, g + 1)
                if g == 0:
                    wait(pe, "a_v", b, 1)
                pe.matmul(C[g][:, 0:400], vv[:, g * D:(g + 1) * D], pT[:, g * 400:(g + 1) * 400],
                          start=True, stop=True).then_inc(sig["pe_av"], 1)

            def project_out(b):
                n = 0
                for g in range(4):
                    wait(pe, "a_ahi", b, g + 1)
                    wait(pe, "d_alo", b, g + 1)
                    for h in range(4 * g, 4 * g + 4):
                        for ap, wp in ((ah, woh), (ah, wol), (al, woh)):
                            ins = pe.matmul(A[0][0:S, :], ap[:, h, :], wp[:, h, :], start=(n == 0), stop=(n == 47))
                            n += 1
                ins.then_inc(sig["pe_o"], 1)

            pe.wait_ge(ld_c, 48)
            pe.wait_ge(g_setup, 3)
            x_turn(0)
            for j in range(6):
                pe.wait_ge(a_whi, j + 1)
                pe.wait_ge(d_wlo, j + 1)
                project(0, j)

            def turn(b, last=False):
                z_turn(b, 2)
                z_turn(b, 3)
                scores(b, 0)
                z_turn(b, 4)
                scores(b, 1)
                if not last:
                    x_turn(b + 1)
                scores(b, 2)
                scores(b, 3)
                if not last:
                    for j in range(5):
                        project(b + 1, j)
                p_turn(b, 0)
                p_turn(b, 1)
                attend(b, 0)
                p_turn(b, 2)
                attend(b, 1)
                p_turn(b, 3)
                attend(b, 2)
                attend(b, 3)
                if not last:
                    project(b + 1, 5)
                    z_turn(b + 1, 0)
                    z_turn(b + 1, 1)
                project_out(b)

            z_turn(0, 0)
            z_turn(0, 1)
            pe.wait_ge(a_whi, wchunks)
            pe.wait_ge(d_wlo, wchunks)
            with pe.Fori(0, NB - 1) as b:
                turn(b)
            turn(NB - 1, last=True)

            pe.wait_ge(sig["d_x1"], NB + 1)
            pe.wait_ge(g_zero, 7)

            def x2_turn(b):
                wait(pe, "d_xn2", b, 1)
                wait(pe, "d_v2", b - 1, 2)
                for k in range(KT):
                    ins = pe.transpose(A[1][:, k * S:(k + 1) * S], xn[:, k * 128:(k + 1) * 128], ident[0:S, 0:S])
                ins.then_inc(sig["pe_xT2"], 1)

            def project2(b, n):
                if n == 0:
                    wait(pe, "a_x2", b, 1)
                    wait(pe, "d_x2", b, 1)
                    wait(pe, "d_v2", b - 1, 3)
                elif n == 1:
                    wait(pe, "a_ctx", b, 1)
                    wait(pe, "d_ctx", b, 1)
                elif n <= 5:
                    wait(pe, "a_sq2", b, n - 1)
                else:
                    wait(pe, "d_v2", b, 1)
                i = 0
                for hi, wp in ((1, wxh), (1, wxl), (0, wxh)):
                    for k in range(KT):
                        if n == 0:
                            rows, lhs = S, (xh if hi else xl)[:, k, :]
                        else:
                            c = (n - 1) % 3
                            rows, lhs = KC, (ch if hi else cl)[:, k, c * KC:(c + 1) * KC]
                        ins = pe.matmul(A[n % 2][0:rows, :], lhs, wp[:, 0 if n == 0 else 1 if n < 4 else 2, k, :],
                                        start=(i == 0), stop=(i == 11))
                        i += 1
                ins.then_inc(sig["pe_proj"], 1)

            def turn_heads(b, m, par):
                wait(pe, "d_kst", b, m + 1)
                wait(pe, "a_kst", b, m + 1)
                wait(pe, "d_qst", b, 1)
                bb, mm = later(b, m, -1)
                wait(pe, "d_T", bb, mm + 1)
                bank = B[0][:, :].bitcast(F16)
                for j in range(2):
                    for c in range(NC):
                        n = j * NC + c
                        pe.transpose(bank[:, n * KC:(n + 1) * KC], kst[m % 2][:, c, j * 128:(j + 1) * 128],
                                     idh[0:KC, 0:KC])
                at = 2 * NC * KC
                for j in range(2):
                    h = m * GH + 2 * j
                    ins = pe.transpose(bank[:, at + j * S:at + (j + 1) * S],
                                       qst[par][:, h:h + 2].rearrange("p h u d -> p (h u d)"), idh[0:S, 0:S])
                ins.then_inc(sig["pe_T"], 1)

            def scores2(b, m):
                wait(pe, "d_T", b, m + 1)
                for c in range(NC):
                    n = m * NC + c
                    bb, mm = (b, n) if n >= 4 else (b - 1, n + 24)
                    wait(pe, "a_e", bb, mm - 3)
                    for j in range(2):
                        ins = pe.matmul(C[n % 4][0:KC, j * 2 * S:(j + 1) * 2 * S], kT[m % 2][:, j * NC + c, :],
                                        qbd[m % 2][:, j, :], start=True, stop=True)
                    ins.then_inc(sig["pe_sc"], 1)

            def attend2(b, m, par):
                wait(pe, "d_eh", b, m + 1)
                wait(pe, "d_el", b, m + 1)
                wait(pe, "g_el", b, m + 1)
                if m == 0:
                    wait(pe, "a_v2", b, 3)
                    wait(pe, "d_v2", b, 3)
                if m % 2 == 0:
                    bb, mm = (b, m // 2) if m else (b - 1, 4)
                    wait(pe, "a_ob", bb, mm)
                for h in range(GH):
                    n = 0
                    at = ((m % 2) * GH + h) * VW
                    for c in range(NC):
                        for e in (eh, el):
                            ins = pe.matmul(B[1][0:S, at:at + VW], e[m % 2][:, c, h * S:(h + 1) * S],
                                            vst[par][:, c, (m * GH + h) * VW:(m * GH + h + 1) * VW],
                                            start=(n == 0), stop=(n == 5))
                            n += 1
                ins.then_inc(sig["pe_pv"], 1)

            x2_turn(0)
            for n in range(7):
                project2(0, n)
            x2_turn(1)
            turn_heads(0, 0, 0)
            turn_heads(0, 1, 0)
            scores2(0, 0)

            def turn(b, par, end):
                for m in range(NG):
                    if end < 2:
                        if m < 7:
                            project2(b + 1, m)
                        elif end < 1:
                            x2_turn(b + 2)
                    bb, mm = later(b, m, 2)
                    if mm > 1 or end < 2:
                        turn_heads(bb, mm, par if mm > 1 else 1 - par)
                    bb, mm = later(b, m, 1)
                    if mm > 0 or end < 2:
                        scores2(bb, mm)
                    attend2(b, m, par)

            two_ways(pe, turn)

            def x3_turn(u):
                for r in range(UB):
                    wait(pe, "d_xn3", u, r + 1)
                    if r == 0:
                        wait(pe, "d_hd", u - 1, 16)
                    for k in range(KT):
                        ins = pe.transpose(C[r][:, k * S:(k + 1) * S], xn[:, k * 128:(k + 1) * 128], ident[0:S, 0:S])
                    ins.then_inc(sig["pe_xT3"], 1)

            def up_gate(u, e):
                if e == 0:
                    wait(pe, "d_x3", u, 4)
                if e >= 2:
                    wait(pe, "d_hd", u, e - 1)
                for half in range(2):
                    n = 0
                    for part in (fh, fl):
                        for k in range(KT):
                            ins = pe.matmul(C[2 * (e % 2) + half][:, 0:UB * S],
                                            wf[:, 4 * half + e // 4, k, (e % 4) * 128:(e % 4 + 1) * 128],
                                            part[:, k, :], start=(n == 0), stop=(n == 7))
                            n += 1
                ins.then_inc(sig["pe_up"], 1)

            def down(u, e):
                wait(pe, "a_hh", u, e + 1)
                wait(pe, "d_hl", u, e + 1)
                if e == 0:
                    wait(pe, "d_y", u - 1, 4)
                for r in range(UB):
                    for part in (hh, hl):
                        ins = pe.matmul((A + B)[r][0:S, :], part[e % 2][:, r * S:(r + 1) * S], wf[:, 8 + e // 4, e % 4, :],
                                        start=(e == 0 and part is hh), stop=(e == ET - 1 and part is hl))
                ins.then_inc(sig["pe_dn"], 1)

            pe.wait_ge(d_tern, 12)
            x3_turn(0)

            def unit(u, last=False):
                up_gate(u, 0)
                for e in range(ET):
                    if e + 1 < ET:
                        up_gate(u, e + 1)
                    elif not last:
                        x3_turn(u + 1)
                    down(u, e)

            with pe.Fori(0, NB // UB - 1) as u:
                unit(u)
            unit(NB // UB - 1, last=True)


def kernel(**inputs):
    import concourse.bacc as _bacc
    from concourse import mybir as _mybir
    from concourse.bass_utils import run_bass_kernel_spmd as _run

    f = {k: np.asarray(v) for k, v in inputs.items()}
    tiles = lambda w: w.T.reshape(w.shape[1] // 128, 128, w.shape[0]).transpose(1, 0, 2)
    wqkv = f["L0_attn_w_qkv"]
    q, k, v = wqkv[:H * D], wqkv[H * D:(H + HKV) * D], wqkv[(H + HKV) * D:]
    wqkv = tiles(np.concatenate([k, q, v]))
    wqkv = wqkv.reshape(128, KT, 6, 512).transpose(0, 2, 1, 3)
    wo = tiles(f["L0_attn_w_o"]).reshape(128, 4, 4, DM)
    wkv = np.concatenate([f["L0_xattn_Wk"], f["L0_xattn_Wv"]])
    wx = tiles(np.concatenate([f["L0_xattn_Wq"], wkv[0::2], wkv[1::2]]))
    wx = wx.reshape(128, KT, 3, 512).transpose(0, 2, 1, 3)
    ctxt = f["ctx_2048"].transpose(0, 2, 1).reshape(NB, KT, 128, CTX).transpose(0, 2, 1, 3)
    updown = [tiles(f["L0_ffn_" + n]).reshape(128, KT, 4, 512).transpose(0, 2, 1, 3) for n in ("W_up", "W_gate")]
    wffn = np.concatenate(updown + [tiles(f["L0_ffn_W_down"]).reshape(128, 4, 4, DM)], 1)
    swap = lambda a: np.concatenate([a[HALF:], a[:HALF]])
    gq, gk, bq, bk = (f["L0_attn_" + n] for n in ("qn_g", "kn_g", "qn_b", "kn_b"))
    gains = np.broadcast_to(np.concatenate([gq, swap(gq), gk, swap(gk)]), (S, 4 * D))
    bcols = np.stack([bq, swap(bq), bk, swap(bk)], 1)
    arrays = {
        "x": f["x"].reshape(NB * S, DM), "wqkv": wqkv, "wo": wo, "wx": wx, "ctxt": ctxt, "wffn": wffn, "gains": gains, "bcols": bcols,
        "consts": constants(),
    }
    arrays = {f"in_{n}": np.ascontiguousarray(a) for n, a in arrays.items()}
    nc = _bacc.Bacc("TRN2", target_bir_lowering=False, num_devices=1)
    args = [nc.dram_tensor(n, a.shape, _mybir.dt.from_np(a.dtype), kind="ExternalInput").ap() for n, a in arrays.items()]
    out = nc.dram_tensor("out_x", (NB * S, DM), F32, kind="ExternalOutput").ap()
    build(nc, *args, out)
    r = _run(nc, [arrays], core_ids=[0])
    return r.results[0]["out_x"].reshape(NB, S, DM)
```

```python
from contextlib import ExitStack

import numpy as np
import concourse.bass as bass
from concourse import mybir

F32 = mybir.dt.float32
F16 = mybir.dt.float16
BF16 = mybir.dt.bfloat16
I32 = mybir.dt.int32
ALU = mybir.AluOpType
ACT = mybir.ActivationFunctionType
AX = mybir.AxisListType

NB, S, DM = 16, 100, 512
KT = DM // 128
H, HKV, D = 16, 4, 128
REP = H // HKV
ROPE_BASE = 1000000.0
EPS_LN = 1e-5
EPS_RMS = 1e-6
CTX = 361
XH, XD = 32, 16
KC = 122
NC = 3
CTXP = KC * NC
FE = 2048
HALF = D // 2

SX = 256.0
SW = 1024.0
SA = 512.0
SN = 1024.0
SV = 2.0 ** -10
SH = 8.0
VW = 2 * XD + 1
GH = 4
NG = XH // GH
UB = 4
ET = FE // 128

C_ID, C_COS, C_SIN, C_COST, C_SINT, C_MASK, C_ONE, C_END = 0, 128, 256, 384, 484, 584, 684, 687


def constants():
    inv = (np.float32(1.0) / np.float32(ROPE_BASE) ** (np.arange(0, D, 2, dtype=np.float32) / np.float32(D))).astype(np.float32)
    f = np.outer(np.arange(S, dtype=np.float32), inv).astype(np.float32)
    cos = np.concatenate([np.cos(f), np.cos(f)], -1).astype(np.float32)
    sin = np.concatenate([-np.sin(f), np.sin(f)], -1).astype(np.float32)
    c = np.zeros((128, C_END), np.float32)
    c[:, C_ID:C_ID + 128] = np.eye(128)
    c[:S, C_COS:C_COS + D] = cos
    c[:S, C_SIN:C_SIN + D] = sin
    c[:, C_COST:C_COST + S] = cos.T
    c[:, C_SINT:C_SINT + S] = sin.T
    c[:S, C_MASK:C_MASK + S] = np.where(np.triu(np.ones((S, S)), 1) > 0, np.float32(-1e30), np.float32(0))
    c[:KC, C_ONE:C_ONE + NC] = (np.arange(CTXP) < CTX).reshape(NC, KC).T
    return c


class Steps:

    def __init__(self, eng, sem):
        self.eng, self.sem, self.n, self.turn, self.per = eng, sem, 0, 0, 0

    def did(self, ins):
        ins.then_inc(self.sem, 1)
        self.n += 1

    def wait(self, back=0):
        self.eng.wait_ge(self.sem, self.turn + (self.n - back))

    def chain(self, ins):
        self.did(ins)
        self.wait()

    def begin(self, i, per):
        self.turn, self.per, self.first = i * per, per, self.n

    def end(self, turns):
        assert self.n - self.first == self.per, (self.n - self.first, self.per)
        self.n += (turns - 1) * self.per
        self.turn = 0


def build(nc, x, wqkv, wo, wx, ctxt, wffn, gains, bcols, consts, out):
    with ExitStack() as ctx:
        def sb(name, shape, dt=F32):
            return ctx.enter_context(nc.sbuf_tensor(name, shape, dt))

        def sem(name):
            return ctx.enter_context(nc.semaphore(name))

        xres = sb("xres", [S, NB, DM])
        cst = sb("cst", [128, C_END])
        idb = sb("idb", [S, S], BF16)
        maskb = sb("maskb", [S, REP, S], BF16)
        gain = sb("gain", [S, 4 * D])
        bcol = sb("bcol", [128, 4])
        stageb = sb("stageb", [128, 2 * KT * 512])
        stage = stageb[:, :].rearrange("p (t k n) -> p t k n", t=2, k=KT)
        ropeA = sb("ropeA", [S, 2, D])
        ropeB = sb("ropeB", [S, 2, D])
        ropeC = sb("ropeC", [128, 2, S])
        wmean = sb("wmean", [128, KT * 4])
        wxh = sb("wxh", [128, 3, KT, 512], F16)
        wxl = sb("wxl", [128, 3, KT, 512], F16)
        arena = sb("arena", [128, 20480])

        region2 = sb("region2", [128, 5 * 512])
        region3 = sb("region3", [128, H * S])

        def carver(region=arena):
            at = [0]

            def carve(shape, dt=F32):
                n = int(np.prod(shape[1:]))
                words = n * (2 if dt in (F16, BF16) else 4) // 4
                v = region[0:shape[0], at[0]:at[0] + words]
                at[0] += words
                if dt != F32:
                    v = v.bitcast(dt)
                names = "abcd"[:len(shape) - 1]
                if len(names) > 1:
                    v = v.rearrange(f"p ({' '.join(names)}) -> p {' '.join(names)}",
                                    **{k: n for k, n in zip(names[1:], shape[2:])})
                return v
            return carve

        carve = carver()
        wqh = carve([128, 6, KT, 512], F16)
        wql = carve([128, 6, KT, 512], F16)
        woh = carve([128, H, DM], F16)
        wol = carve([128, H, DM], F16)
        carve = carver()
        raw = [carve([KC, 4, 512]) for _ in range(2)]
        ctxs = carve([128, KT, CTXP])
        ch = carve([128, KT, CTXP], F16)
        cl = carve([128, KT, CTXP], F16)
        kn = [carve([KC, NC * GH, XD]) for _ in range(2)]
        kst = [carve([KC, NC, GH * 4 * XD], F16) for _ in range(2)]
        kT = [carve([128, 2 * NC, KC], F16) for _ in range(2)]
        qbd = [carve([128, 2, 2 * S], F16) for _ in range(2)]
        qn = carve([S, 512])
        qst1, vst1 = carve([S, XH, 4, XD], F16), carve([KC, NC, XH * VW], F16)
        qst = [carve([S, XH, 4, XD], F16), qst1]
        vst = [carve([KC, NC, XH * VW], F16), vst1]
        eb = [carve([KC, NC, GH * S]) for _ in range(2)]
        eh = [carve([KC, NC, GH * S], F16) for _ in range(2)]
        el = [carve([KC, NC, GH * S], F16) for _ in range(2)]
        carve = carver(stageb)
        pT = carve([S, H * S])
        ah = carve([128, H, S], F16)
        al = carve([128, H, S], F16)
        carve = carver(region3)
        pr = carve([S, H * S])
        carve = carver(region3)
        ob = carve([S, XH, VW])
        osum = carve([S, DM])
        carve = carver(region2)
        zb = carve([S, 5, 512])
        carve = carver(region2)
        xsq = carve([KC, 2, 512])
        xssq = carve([KC, 129])
        xrstd = [carve([KC, 129]) for _ in range(2)]
        xnw = carve([KC, 2, 129])
        oinv = carve([S, XH])
        carve = carver()
        wf = carve([128, 12, 4, 512], BF16)
        carve([128, 140])
        fh = carve([128, KT, UB * S], F16)
        fl = carve([128, KT, UB * S], F16)
        sg = [carve([128, UB * S]) for _ in range(2)]
        hd = [carve([128, UB * S]) for _ in range(2)]
        hh = [carve([128, UB * S], F16) for _ in range(2)]
        hl = [carve([128, UB * S], F16) for _ in range(2)]
        asum = sb("asum", [128, 3, NB, 1])
        fsc = sb("fsc", [128, 16])
        idh = sb("idh", [128, 128], F16)
        statc = sb("statc", [S, 6])
        stats = sb("stats", [S, 6])
        mv = sb("mv", [S, 2])
        stats3 = sb("stats3", [S, UB, 6])
        statc3 = sb("statc3", [S, UB, 6])
        mv3 = sb("mv3", [S, UB, 2])
        ms3 = sb("ms3", [S, UB])
        rs3 = sb("rs3", [S, UB])
        ms1 = sb("ms1", [S, 1])
        nwt = sb("nwt", [128, 3, 32])
        rs1 = sb("rs1", [S, 1])
        xn = sb("xn", [S, DM])
        xh = sb("xh", [128, KT, S], F16)
        xl = sb("xl", [128, KT, S], F16)
        sq = sb("sq", [S, 2, 512])
        tb = sb("tb", [S, 2, 512])
        ub = sb("ub", [S, 2, 512])
        ssq = sb("ssq", [S, 5 * 4 + 1])
        rstd = sb("rstd", [S, 5 * 4 + 1])
        qk = sb("qk", [128, 5, REP, S])
        vv = sb("vv", [S, HKV * D])
        xn3 = [tb[:, 0], tb[:, 1], ub[:, 0], ub[:, 1]]
        wgt = qk[:, :].rearrange("p g h s -> p (g h s)")[:, 0:1024].bitcast(BF16)
        smax = sb("smax", [S, H])
        negm = sb("negm", [S, H])
        rsum = sb("rsum", [S, H])
        rinv = sb("rinv", [S, H])

        A = [ctx.enter_context(nc.psum_tensor(f"A{i}", [128, 512], F32)) for i in range(2)]
        B = [ctx.enter_context(nc.psum_tensor(f"B{i}", [128, 512], F32)) for i in range(2)]
        C = [ctx.enter_context(nc.psum_tensor(f"C{i}", [128, 512], F32)) for i in range(4)]

        ld_c = sem("ld_c")
        ld_x0 = sem("ld_x0")
        ld_x = sem("ld_x")
        ld_w = [sem("ld_w0"), sem("ld_w1")]
        g_setup = sem("g_setup")
        d_tab = sem("d_tab")
        d_wmean, g_wcen, a_whi, d_wlo = sem("d_wmean"), sem("g_wcen"), sem("a_whi"), sem("d_wlo")
        d_step = sem("d_step")
        g_step = sem("g_step")
        PER = dict(pe_xT=1, pe_qkv=6, pe_zT=5, pe_s=4, pe_pT=4, pe_av=4, pe_o=1,
                   a_xhi=1, a_sq=5, a_v=1, a_exp=16, a_pT=4, a_ahi=4,
                   d_xn=1, d_zT=5, d_xlo=1, d_negm=4, d_t=5, d_u=5, d_ssq=5, d_rstd=1, d_rinv=4,
                   d_alo=4, d_x1=1, g_w=5, g_z=5, g_p=4,
                   pe_xT2=1, pe_proj=7, pe_T=8, pe_sc=24, pe_pv=8,
                   a_ctx=1, a_x2=1, a_raw=4, a_sq2=4, a_qst=1, a_v2=3, a_kst=8, a_T=8, a_e=24, a_ob=4, a_abs=3,
                   d_xn2=1, d_ctx=1, d_x2=1, d_ssq2=4, d_rstd2=1, d_qst=1, d_v2=3, d_kst=8, d_T=8,
                   d_eh=8, d_x2out=1,
                   g_kn=8, g_el=8, g_qn=1,
                   pe_xT3=4, pe_up=16, pe_dn=16, a_x3=4, a_sg=16, a_hh=16,
                   d_xn3=4, d_x3=4, d_hd=16, d_hl=16, d_y=4)
        sig = {n: sem(n) for n in PER}
        OWNER = {"p": "tensor", "a": "scalar", "d": "vector", "g": "gpsimd"}

        def credit(eng, who):
            for n in PER:
                if n[0] == who:
                    eng.sem_inc(sig[n], PER[n])

        def wait(eng, name, b, n):
            eng.wait_ge(sig[name], (b + 1) * PER[name] + n)

        wchunks = 6 + 4 + 3
        ld_ctx, g_zero, st_y = sem("ld_ctx"), sem("g_zero"), sem("st_y")
        ld_f = [sem("ld_f0"), sem("ld_f1")]
        g_sum, d_fsc, d_tern = sem("g_sum"), sem("d_fsc"), sem("d_tern")

        def later(b, m, k):
            return b + (m + k) // NG, (m + k) % NG

        def two_ways(eng, turn, st=None, per=0):
            with eng.Fori(0, NB // 2 - 1) as i:
                if st:
                    st.begin(i, per)
                turn(i * 2, 0, 0)
                turn(i * 2 + 1, 1, 0)
            if st:
                st.end(NB // 2 - 1)
            turn(NB - 2, 0, 1)
            turn(NB - 1, 1, 2)

        block = ctx.enter_context(nc.Block())

        @block.sync
        def _(sp):
            sp.dma_start(cst[:], consts).then_inc(ld_c, 16)
            sp.dma_start(gain[:], gains).then_inc(ld_c, 16)
            sp.dma_start(bcol[:], bcols).then_inc(ld_c, 16)
            xt = x.rearrange("(b p) f -> p b f", b=NB)
            sp.dma_start(xres[:, 0, :], xt[:, 0, :]).then_inc(ld_x0, 16)
            for j in range(wchunks):
                if j >= 2:
                    sp.wait_ge(a_whi, j - 1)
                    sp.wait_ge(d_wlo, j - 1)
                src = wqkv[:, j] if j < 6 else wo[:, j - 6] if j < 10 else wx[:, j - 10]
                sp.dma_start(stage[:, j % 2], src).then_inc(ld_w[j % 2], 16)
                if j == 1:
                    sp.dma_start(xres[:, 1:NB, :], xt[:, 1:NB, :]).then_inc(ld_x, 16)
            sp.wait_ge(sig["d_x1"], NB + 1)
            sp.wait_ge(g_zero, 1)
            wsum = wffn.rearrange("p (w c) k n -> p w (c k) n", w=3)
            with sp.Fori(0, NB // 2) as i:
                for par in range(2):
                    b = i * 2 + par
                    wait(sp, "a_ctx", b - 1, 1)
                    wait(sp, "d_ctx", b - 1, 1)
                    sp.dma_start(ctxs[:, :, 0:CTX], ctxt[b]).then_inc(ld_ctx, 16)
                    wait(sp, "a_abs", b - 2, 3)
                    sp.dma_start(stage[:, par, 0:3], wsum[:, :, b]).then_inc(ld_f[par], 16)
            for n in range(12):
                if n < 2:
                    wait(sp, "a_abs", NB - 2 + n, 3)
                else:
                    sp.wait_ge(d_tern, n - 1)
                sp.dma_start(stage[:, n % 2], wffn[:, 4 * (n % 3) + n // 3]).then_inc(ld_f[n % 2], 16)
            with sp.Fori(0, NB // UB) as u:
                for r in range(UB):
                    wait(sp, "d_y", u, r + 1)
                    sp.dma_start(out.rearrange("(b p) f -> p b f", b=NB)[:, u * UB + r, :],
                                 xres[:, u * UB + r, :]).then_inc(st_y, 16)
            sp.wait_ge(st_y, 16 * NB)

        @block.gpsimd
        def _(pool):
            credit(pool, "g")
            pool.wait_ge(ld_c, 48)
            pool.tensor_copy(idh[:], cst[:, C_ID:C_ID + 128]).then_inc(g_setup, 1)
            pool.tensor_copy(idb[:], cst[0:S, C_ID:C_ID + S]).then_inc(g_setup, 1)
            m = cst[0:S, C_MASK:C_MASK + S].unsqueeze(1).broadcast_to([S, REP, S])
            pool.tensor_copy(maskb[:], m).then_inc(g_setup, 1)
            for j in range(5):
                pool.wait_ge(d_wmean, j + 1)
                w = stage[:, j % 2].rearrange("p k (h d) -> p (k h) d", h=4)
                pool.tensor_tensor(w, w, wmean[:].unsqueeze(2).broadcast_to([128, KT * 4, D]),
                                   ALU.subtract).then_inc(g_wcen, 1)

            def w_of(b, j):
                wait(pool, "d_t", b, j + 1)
                wait(pool, "d_u", b, j + 1)
                if j == 0:
                    wait(pool, "pe_zT", b - 1, 5)
                pool.tensor_tensor(zb[:, j], tb[:, j % 2], ub[:, j % 2], ALU.add).then_inc(sig["g_w"], 1)

            def z_of(b, j):
                wait(pool, "d_rstd", b, 1)
                wait(pool, "g_w", b, j + 1)
                r = rstd[:, 4 * j:4 * j + 4].unsqueeze(2).broadcast_to([S, 4, D])
                z = zb[:, j].rearrange("p (h d) -> p h d", h=4)
                pool.tensor_tensor(z, z, r, ALU.mult).then_inc(sig["g_z"], 1)

            def p_of(b, g):
                wait(pool, "d_rinv", b, g + 1)
                p = pr[:, g * 400:(g + 1) * 400].rearrange("p (h k) -> p h k", h=4)
                r = rinv[:, 4 * g:4 * g + 4].unsqueeze(2).broadcast_to([S, 4, S])
                pool.tensor_tensor(p, p, r, ALU.mult).then_inc(sig["g_p"], 1)

            for j in range(5):
                w_of(0, j)
            for j in range(5):
                z_of(0, j)

            def turn(b, last=False):
                for what, j in (("w", 0), ("w", 1), ("p", 0), ("w", 2), ("p", 1), ("p", 2), ("w", 3), ("p", 3), ("w", 4)):
                    if what == "p":
                        p_of(b, j)
                    elif not last:
                        w_of(b + 1, j)
                if not last:
                    for j in range(5):
                        z_of(b + 1, j)

            with pool.Fori(0, NB - 1) as b:
                turn(b)
            turn(NB - 1, last=True)

            pool.wait_ge(sig["d_x1"], NB + 1)
            pool.memset(ctxs[:, :, CTX:CTXP], 0.0).then_inc(g_zero, 1)
            for p in range(2):
                one = cst[0:KC, C_ONE:C_ONE + NC].unsqueeze(2).broadcast_to([KC, NC, XH])
                pool.tensor_copy(vst[p].rearrange("p c (h v) -> p c h v", h=XH)[:, :, :, 2 * XD], one)\
                    .then_inc(g_zero, 1)
                pool.memset(qbd[p], 0.0).then_inc(g_zero, 1)
            pool.memset(xssq[:], 1.0).then_inc(g_zero, 1)

            def q_normed(b, par):
                wait(pool, "d_rstd2", b, 1)
                wait(pool, "d_qst", b - 1, 1)
                wait(pool, "a_qst", b - 1, 1)
                r = xrstd[par][0:S, 96:128].unsqueeze(2).broadcast_to([S, XH, XD])
                pool.tensor_tensor(qn.rearrange("p (h d) -> p h d", h=XH),
                                   raw[par][0:S, 3].rearrange("p (h d) -> p h d", h=XH), r,
                                   ALU.mult).then_inc(sig["g_qn"], 1)

            def k_normed(b, m, par):
                wait(pool, "d_rstd2", b, 1)
                bb, mm = later(b, m, -2)
                wait(pool, "a_kst", bb, mm + 1)
                wait(pool, "d_kst", bb, mm + 1)
                for c in range(NC):
                    r = xrstd[par][:, c * XH + m * GH:c * XH + (m + 1) * GH].unsqueeze(2).broadcast_to([KC, GH, XD])
                    ins = pool.tensor_tensor(kn[m % 2][:, c * GH:(c + 1) * GH, :],
                                             raw[par][:, c, m * GH * XD:(m + 1) * GH * XD]
                                             .rearrange("p (h d) -> p h d", h=GH), r, ALU.mult)
                ins.then_inc(sig["g_kn"], 1)

            def e_low(b, m):
                wait(pool, "d_eh", b, m + 1)
                bb, mm = later(b, m, -2)
                wait(pool, "pe_pv", bb, mm + 1)
                pool.tensor_tensor(el[m % 2], eb[m % 2], eh[m % 2], ALU.subtract)\
                    .then_inc(sig["g_el"], 1)

            q_normed(0, 0)
            for m in range(4):
                k_normed(0, m, 0)
            e_low(0, 0)

            def turn(b, par, end):
                for m in range(NG):
                    bb, mm = later(b, m, 4)
                    if mm > 3 or end < 2:
                        k_normed(bb, mm, par if mm > 3 else 1 - par)
                    bb, mm = later(b, m, 1)
                    if mm > 0 or end < 2:
                        e_low(bb, mm)
                    if m == 4 and end < 2:
                        q_normed(b + 1, 1 - par)
                    if m == 1 and end == 2:
                        pool.wait_ge(d_fsc, 1)
                        pool.partition_all_reduce(fsc[:, 3:6], fsc[:, 0:3], 128, bass.bass_isa.ReduceOp.add)\
                            .then_inc(g_sum, 1)

            two_ways(pool, turn)

        @block.scalar
        def _(act):
            credit(act, "a")

            def w_hi(j):
                if j < 5:
                    act.wait_ge(g_wcen, j + 1)
                else:
                    act.wait_ge(ld_w[j % 2], 16 * (j // 2 + 1))
                dst = wqh[:, j] if j < 6 else woh[:, 4 * (j - 6):4 * (j - 5), :] if j < 10 else wxh[:, j - 10]
                act.activation(dst, stage[:, j % 2], ACT.Copy, scale=SW).then_inc(a_whi, 1)

            def x_hi(b):
                wait(act, "pe_xT", b, 1)
                wait(act, "pe_qkv", b - 1, 6)
                act.activation(xh[:], B[1][:, 0:KT * S].rearrange("p (k s) -> p k s", k=KT), ACT.Copy)\
                   .then_inc(sig["a_xhi"], 1)

            def square(b, j):
                wait(act, "pe_qkv", b, j + 1)
                if j >= 2:
                    wait(act, "d_ssq", b, j - 1)
                else:
                    wait(act, "d_ssq", b - 1, 4 + j)
                act.activation(sq[:, j % 2], A[j % 2][0:S, :], ACT.Square).then_inc(sig["a_sq"], 1)

            def v_of(b):
                wait(act, "pe_qkv", b, 6)
                wait(act, "pe_av", b - 1, 4)
                act.activation(vv[:], A[1][0:S, :], ACT.Copy, scale=1.0 / (SX * SW)).then_inc(sig["a_v"], 1)

            def exps(b, g):
                wait(act, "d_negm", b, g + 1)
                if g == 0:
                    wait(act, "pe_pT", b - 1, 4)
                    wait(act, "d_rinv", b - 1, 4)
                for h in range(4):
                    n = 4 * g + h
                    act.activation(pr[:, n * S:(n + 1) * S], C[g][0:S, h * S:(h + 1) * S], ACT.Exp,
                                   bias=negm[:, n:n + 1], scale=float(D) ** -0.5,
                                   accum_out=rsum[:, n:n + 1]).then_inc(sig["a_exp"], 1)

            def p_back(b, g):
                wait(act, "pe_pT", b, g + 1)
                wait(act, "pe_av", b - 1, g + 1)
                act.activation(pT[:, g * 400:(g + 1) * 400], B[g % 2][0:S, 0:400], ACT.Copy)\
                   .then_inc(sig["a_pT"], 1)

            def a_hi(b, g):
                wait(act, "pe_av", b, g + 1)
                wait(act, "pe_o", b - 1, 1)
                act.activation(ah[:, 4 * g:4 * g + 4, :], C[g][:, 0:400].rearrange("p (h s) -> p h s", h=4),
                               ACT.Copy, scale=SA).then_inc(sig["a_ahi"], 1)

            for j in range(6):
                w_hi(j)
            x_hi(0)
            for j in range(5):
                square(0, j)
            v_of(0)
            for j in range(6, wchunks):
                w_hi(j)

            def turn(b, last=False):
                if not last:
                    x_hi(b + 1)
                for g in range(4):
                    exps(b, g)
                    if not last:
                        square(b + 1, g)
                if not last:
                    square(b + 1, 4)
                for g in range(4):
                    p_back(b, g)
                for g in range(4):
                    a_hi(b, g)
                if not last:
                    v_of(b + 1)

            with act.Fori(0, NB - 1) as b:
                turn(b)
            turn(NB - 1, last=True)

            act.wait_ge(sig["d_x1"], NB + 1)
            act.wait_ge(g_zero, 6)

            def ctx_hi(b):
                act.wait_ge(ld_ctx, (b + 1) * 16)
                wait(act, "pe_proj", b - 1, 7)
                act.activation(ch, ctxs, ACT.Copy, scale=SX).then_inc(sig["a_ctx"], 1)

            def x2_hi(b):
                wait(act, "pe_xT2", b, 1)
                wait(act, "pe_proj", b - 1, 1)
                act.activation(xh[:], A[0][:, 0:KT * S].rearrange("p (k s) -> p k s", k=KT), ACT.Copy)\
                   .then_inc(sig["a_x2"], 1)

            def keep_raw(b, n, par):
                wait(act, "pe_proj", b, n + 1)
                rows, slot = (S, 3) if n == 0 else (KC, n - 1)
                if n == 0:
                    wait(act, "g_kn", b - 2, 8)
                    wait(act, "g_qn", b - 2, 1)
                act.activation(raw[par][0:rows, slot], A[(n + 1) % 2][0:rows, :], ACT.Copy).then_inc(sig["a_raw"], 1)
                if n >= 2:
                    wait(act, "d_ssq2", b, n - 1)
                else:
                    wait(act, "d_ssq2", b - 1, n + 3)
                act.activation(xsq[0:rows, n % 2], A[(n + 1) % 2][0:rows, :], ACT.Square).then_inc(sig["a_sq2"], 1)

            def v2_hi(b, c, par):
                wait(act, "pe_proj", b, 5 + c)
                if c == 0:
                    wait(act, "pe_pv", b - 2, 8)
                act.activation(vst[par][:, c].rearrange("p (h v) -> p h v", h=XH)[:, :, 0:XD],
                               A[(c + 1) % 2][0:KC, :].rearrange("p (h d) -> p h d", h=XH), ACT.Copy, scale=SV)\
                   .then_inc(sig["a_v2"], 1)

            def q_stack(b, par):
                wait(act, "g_qn", b, 1)
                wait(act, "pe_T", b - 2, 8)
                act.activation(qst[par].rearrange("p h (u w) d -> p h u w d", u=2)[:, :, :, 0, :],
                               qn.rearrange("p (h d) -> p h d", h=XH).unsqueeze(2).broadcast_to([S, XH, 2, XD]),
                               ACT.Copy).then_inc(sig["a_qst"], 1)

            def k_stack(b, m):
                wait(act, "g_kn", b, m + 1)
                bb, mm = later(b, m, -2)
                wait(act, "pe_T", bb, mm + 1)
                act.activation(kst[m % 2].rearrange("p c (h u d) -> p (c h) u d", h=GH, u=4)[:, :, 0:2, :],
                               kn[m % 2].unsqueeze(2).broadcast_to([KC, NC * GH, 2, XD]), ACT.Copy)\
                   .then_inc(sig["a_kst"], 1)

            def exp2(b, m):
                for c in range(NC):
                    wait(act, "pe_sc", b, m * NC + c + 1)
                    if c == 0:
                        bb, mm = later(b, m, -2)
                        wait(act, "g_el", bb, mm + 1)
                    act.activation(eb[m % 2][:, c], C[(m * NC + c) % 4][0:KC, 0:GH * S], ACT.Exp,
                                   scale=float(XD) ** -0.5 / SN ** 2).then_inc(sig["a_e"], 1)

            def keys_back(b, m):
                wait(act, "d_T", b, m + 1)
                bb, mm = later(b, m, -2)
                wait(act, "pe_sc", bb, mm * NC + NC)
                act.activation(kT[m % 2], B[0][:, :].bitcast(F16)[:, 0:2 * NC * KC].rearrange("p (n k) -> p n k", n=2 * NC),
                               ACT.Copy).then_inc(sig["a_T"], 1)

            def magnitudes(b, w, par):
                if w == 0:
                    act.wait_ge(ld_f[par], (b - par) * 8 + 16)
                act.activation(stage[:, par, w], stage[:, par, w], ACT.Abs, accum_out=asum[:, w, b, :])\
                   .then_inc(sig["a_abs"], 1)

            def x3_hi(u, r, bank):
                wait(act, "pe_xT3", u, r + 1)
                wait(act, "pe_up", u - 1, 16)
                act.activation(fh[:, :, r * S:(r + 1) * S], bank[:, 0:KT * S].rearrange("p (k s) -> p k s", k=KT),
                               ACT.Copy).then_inc(sig["a_x3"], 1)

            def out_back(b, n):
                wait(act, "pe_pv", b, 2 * n + 2)
                if n == 0:
                    wait(act, "d_x2out", b - 1, 1)
                act.activation(ob[:, 8 * n:8 * n + 8, :], B[1][0:S, 0:8 * VW].rearrange("p (h v) -> p h v", h=8),
                               ACT.Copy).then_inc(sig["a_ob"], 1)

            ctx_hi(0)
            x2_hi(0)
            for n in range(4):
                keep_raw(0, n, 0)
            for c in range(NC):
                v2_hi(0, c, 0)
            x2_hi(1)
            ctx_hi(1)
            q_stack(0, 0)
            for m in range(3):
                k_stack(0, m)
                if m < 2:
                    keys_back(0, m)
            exp2(0, 0)
            keep_raw(1, 0, 1)

            def turn(b, par, end):
                for m in range(NG):
                    bb, mm = later(b, m, 1)
                    if mm > 0 or end < 2:
                        exp2(bb, mm)
                    if m in (2, 4, 6):
                        out_back(b, m // 2 - 1)
                    bb, mm = later(b, m, 2)
                    if mm > 1 or end < 2:
                        keys_back(bb, mm)
                    if m == 5 and end < 2:
                        q_stack(b + 1, 1 - par)
                    bb, mm = later(b, m, 3)
                    if mm > 2 or end < 2:
                        k_stack(bb, mm)
                    if end < 2 and m < 3:
                        keep_raw(b + 1, m + 1, 1 - par)
                    elif end < 2 and m < 6:
                        v2_hi(b + 1, m - 3, 1 - par)
                    elif end < 1 and m == 6:
                        x2_hi(b + 2)
                        ctx_hi(b + 2)
                    elif end < 1 and m == 7:
                        keep_raw(b + 2, 0, par)
                    if end < 2 and 3 <= m < 6:
                        magnitudes(b, m - 3, par)
                    elif end == 1 and m == 6:
                        for w in range(3):
                            magnitudes(b + 1, w, 1 - par)
                    if end == 2 and m == 2:
                        wait(act, "pe_pv", b - 1, 8)
                    if end == 2 and 2 <= m < 6:
                        x3_hi(0, m - 2, A[m % 2])
                out_back(b, 3)

            two_ways(act, turn)

            def silu(u, e):
                wait(act, "pe_up", u, e + 1)
                if e >= 2:
                    wait(act, "d_hd", u, e - 1)
                else:
                    wait(act, "d_hd", u - 1, 15 + e)
                act.activation(sg[e % 2], C[2 * (e % 2)][:, 0:UB * S], ACT.Silu, scale=fsc[:, 6:7])\
                   .then_inc(sig["a_sg"], 1)

            def hidden_hi(u, e):
                wait(act, "d_hd", u, e + 1)
                if e >= 2:
                    wait(act, "pe_dn", u, e - 1)
                else:
                    wait(act, "pe_dn", u - 1, 15 + e)
                act.activation(hh[e % 2], hd[e % 2], ACT.Copy).then_inc(sig["a_hh"], 1)

            def unit(u, last=False):
                silu(u, 0)
                for e in range(ET):
                    hidden_hi(u, e)
                    if e + 1 < ET:
                        silu(u, e + 1)
                    if e == ET - 2 and not last:
                        x3_hi(u + 1, 0, C[0])
                        x3_hi(u + 1, 1, C[1])
                if not last:
                    x3_hi(u + 1, 2, C[0])
                    x3_hi(u + 1, 3, C[1])

            wait(act, "pe_pv", NB - 1, 8)
            unit(0)
            with act.Fori(0, NB // UB - 2) as i:
                unit(i + 1)
            unit(NB // UB - 1, last=True)

        @block.vector
        def _(dve):
            credit(dve, "d")
            st = Steps(dve, d_step)

            def rsqrt(y, v, n, p=S):
                a, c = nwt[0:p, 0, 0:n], nwt[0:p, 1, 0:n]
                st.chain(dve.tensor_scalar(y.bitcast(I32), v.bitcast(I32), 1, None, ALU.logical_shift_right))
                st.chain(dve.tensor_scalar(y.bitcast(I32), y.bitcast(I32), -1, 0x5f3759df, ALU.mult, ALU.add))
                for _ in range(3):
                    st.chain(dve.scalar_tensor_tensor(a, y, -0.5, y, ALU.mult, ALU.mult))
                    st.chain(dve.tensor_tensor(c, a, v, ALU.mult))
                    ins = dve.scalar_tensor_tensor(y, c, 1.5, y, ALU.add, ALU.mult)
                    if _ < 2:
                        st.chain(ins)
                return ins

            def row_stats(b, var):
                st.chain(dve.bn_stats(stats[:], xres[:, b, :]))
                st.did(dve.tensor_copy(statc[:], stats[:]))
                st.chain(dve.bn_aggr(mv[:], stats[:]))
                st.did(dve.tensor_scalar(var, mv[:, 1:2], EPS_LN, SX ** -2, ALU.add, ALU.mult))

            def normed(b, rs):
                wait(dve, "pe_xT", b - 1, 1)
                dve.tensor_scalar(xn[:], xres[:, b, :], mv[:, 0:1], rs, ALU.subtract, ALU.mult)\
                   .then_inc(sig["d_xn"], 1)

            def x_lo(b):
                wait(dve, "a_xhi", b, 1)
                wait(dve, "pe_qkv", b - 1, 6)
                dve.tensor_tensor(xl[:], B[1][:, 0:KT * S].rearrange("p (k s) -> p k s", k=KT), xh[:],
                                  ALU.subtract).then_inc(sig["d_xlo"], 1)

            def proj(b, j):
                wait(dve, "pe_qkv", b, j + 1)
                wait(dve, "a_sq", b, j + 1)
                if j >= 2:
                    wait(dve, "g_w", b, j - 1)
                else:
                    wait(dve, "g_w", b - 1, 4 + j)
                which = 0 if j == 0 else 1
                bank = A[j % 2][0:S, :].rearrange("p (h d) -> p h d", h=4)
                t = tb[:, j % 2].rearrange("p (h d) -> p h d", h=4)
                u = ub[:, j % 2].rearrange("p (h d) -> p h d", h=4)

                def table(tab, lo, hi):
                    return tab[:, which, lo:hi].unsqueeze(1).broadcast_to([S, 4, hi - lo])

                dve.tensor_tensor(t, bank, table(ropeA, 0, D), ALU.mult).then_inc(sig["d_t"], 1)
                st.did(dve.tensor_tensor(u[:, :, 0:HALF], bank[:, :, HALF:D], table(ropeB, 0, HALF), ALU.mult))
                dve.tensor_tensor(u[:, :, HALF:D], bank[:, :, 0:HALF], table(ropeB, HALF, D), ALU.mult)\
                   .then_inc(sig["d_u"], 1)
                if j == 0:
                    wait(dve, "d_rstd", b - 1, 1)
                dve.tensor_reduce(ssq[:, 4 * j:4 * j + 4], sq[:, j % 2].rearrange("p (h d) -> p h d", h=4),
                                  AX.X, ALU.add).then_inc(sig["d_ssq"], 1)

            def head_norm(b):
                wait(dve, "d_ssq", b, 5)
                st.chain(dve.tensor_scalar(ssq[:, 0:20], ssq[:, 0:20], 1.0 / D, EPS_LN * (SX * SW) ** 2,
                                           ALU.mult, ALU.add))
                wait(dve, "g_z", b - 1, 5)
                rsqrt(rstd[:], ssq[:], 21).then_inc(sig["d_rstd"], 1)
                wait(dve, "d_rstd", b, 1)

            def z_back(b, g):
                wait(dve, "pe_zT", b, g + 1)
                if g == 0:
                    wait(dve, "pe_s", b - 1, 4)
                c = ropeC[:, 0 if g == 0 else 1, :].unsqueeze(1).broadcast_to([128, 4, S])
                dve.tensor_tensor(qk[:, g], B[g % 2][:, 0:400].rearrange("p (h s) -> p h s", h=4), c,
                                  ALU.add).then_inc(sig["d_zT"], 1)

            def row_max(b, g):
                wait(dve, "pe_s", b, g + 1)
                if g == 0:
                    wait(dve, "a_exp", b - 1, 16)
                st.chain(dve.tensor_reduce(smax[:, 4 * g:4 * g + 4],
                                           C[g][0:S, 0:400].rearrange("p (h k) -> p h k", h=4), AX.X, ALU.max))
                dve.tensor_scalar(negm[:, 4 * g:4 * g + 4], smax[:, 4 * g:4 * g + 4], -float(D) ** -0.5, None,
                                  ALU.mult).then_inc(sig["d_negm"], 1)

            def sums(b, g):
                wait(dve, "a_exp", b, 4 * g + 4)
                if g == 0:
                    wait(dve, "g_p", b - 1, 4)
                dve.reciprocal(rinv[:, 4 * g:4 * g + 4], rsum[:, 4 * g:4 * g + 4]).then_inc(sig["d_rinv"], 1)

            def a_lo(b, g):
                wait(dve, "a_ahi", b, g + 1)
                dve.scalar_tensor_tensor(al[:, 4 * g:4 * g + 4, :],
                                         C[g][:, 0:400].rearrange("p (h s) -> p h s", h=4), SA,
                                         ah[:, 4 * g:4 * g + 4, :], ALU.mult, ALU.subtract)\
                   .then_inc(sig["d_alo"], 1)

            def add_attn(b):
                wait(dve, "pe_o", b, 1)
                dve.scalar_tensor_tensor(xres[:, b, :], A[0][0:S, :], 1.0 / (SA * SW), xres[:, b, :],
                                         ALU.mult, ALU.add).then_inc(sig["d_x1"], 1)

            dve.wait_ge(ld_x0, 16)
            row_stats(0, ms1[:])
            st.wait()
            st.chain(rsqrt(rs1[:], ms1[:], 1))
            normed(0, rs1[:, 0:1])
            dve.wait_ge(ld_c, 48)
            for w, g in ((0, 2), (1, 0)):
                dve.tensor_tensor(ropeA[:, w], gain[:, g * D:(g + 1) * D], cst[0:S, C_COS:C_COS + D],
                                  ALU.mult).then_inc(d_tab, 1)
                dve.tensor_tensor(ropeB[:, w], gain[:, (g + 1) * D:(g + 2) * D], cst[0:S, C_SIN:C_SIN + D],
                                  ALU.mult).then_inc(d_tab, 1)
                st.chain(dve.tensor_scalar(ropeC[:, w], cst[:, C_COST:C_COST + S], bcol[:, g:g + 1], None, ALU.mult))
                dve.scalar_tensor_tensor(ropeC[:, w], cst[:, C_SINT:C_SINT + S], bcol[:, g + 1:g + 2],
                                         ropeC[:, w], ALU.mult, ALU.add).then_inc(d_tab, 1)
            dve.wait_ge(d_tab, 6)

            def w_mean(j):
                dve.wait_ge(ld_w[j % 2], 16 * (j // 2 + 1))
                if j > 0:
                    dve.wait_ge(g_wcen, j)
                st.chain(dve.tensor_reduce(wmean[:], stage[:, j % 2].rearrange("p k (h d) -> p (k h) d", h=4),
                                           AX.X, ALU.add))
                dve.tensor_scalar(wmean[:], wmean[:], 1.0 / D, None, ALU.mult).then_inc(d_wmean, 1)

            def w_lo(j):
                dve.wait_ge(a_whi, j + 1)
                dst, hi = (wql[:, j], wqh[:, j]) if j < 6 else (
                    wol[:, 4 * (j - 6):4 * (j - 5), :], woh[:, 4 * (j - 6):4 * (j - 5), :]) if j < 10 else (
                    wxl[:, j - 10], wxh[:, j - 10])
                dve.scalar_tensor_tensor(dst.rearrange("p k n -> p (k n)"),
                                         stage[:, j % 2].rearrange("p k n -> p (k n)"), SW,
                                         hi.rearrange("p k n -> p (k n)"), ALU.mult, ALU.subtract)\
                   .then_inc(d_wlo, 1)

            w_mean(0)
            for j in range(6):
                if j + 1 < 5:
                    w_mean(j + 1)
                w_lo(j)
            x_lo(0)
            for j in range(5):
                proj(0, j)
            dve.wait_ge(ld_x, 16)
            row_stats(1, ssq[:, 20:21])
            head_norm(0)
            normed(1, rstd[:, 20:21])
            for j in range(6, wchunks):
                w_lo(j)
            for g in range(2):
                z_back(0, g)

            def turn(b, end=0):
                for g in range(2, 5):
                    z_back(b, g)
                row_max(b, 0)
                if end < 2:
                    x_lo(b + 1)
                for g in range(1, 4):
                    row_max(b, g)
                for g in range(4):
                    if end < 2:
                        proj(b + 1, g)
                    sums(b, g)
                if end < 1:
                    row_stats(b + 2, ssq[:, 20:21])
                if end < 2:
                    proj(b + 1, 4)
                    head_norm(b + 1)
                if end < 1:
                    normed(b + 2, rstd[:, 20:21])
                for g in range(4):
                    a_lo(b, g)
                if end < 2:
                    for g in range(2):
                        z_back(b + 1, g)
                add_attn(b)

            with dve.Fori(0, NB - 2) as b:
                st.begin(b, 24)
                turn(b)
            st.end(NB - 2)
            turn(NB - 2, 1)
            turn(NB - 1, 2)

            dve.wait_ge(g_zero, 6)

            def ctx_lo(b):
                wait(dve, "a_ctx", b, 1)
                wait(dve, "pe_proj", b - 1, 7)
                dve.scalar_tensor_tensor(cl.rearrange("p k n -> p (k n)"), ctxs.rearrange("p k n -> p (k n)"), SX,
                                         ch.rearrange("p k n -> p (k n)"), ALU.mult, ALU.subtract)\
                   .then_inc(sig["d_ctx"], 1)

            def layer_norm2(b):
                st.chain(dve.bn_stats(stats[:], xres[:, b, :]))
                st.did(dve.tensor_copy(statc[:], stats[:]))
                st.chain(dve.bn_aggr(mv[:], stats[:]))
                st.chain(dve.tensor_scalar(ms1[:], mv[:, 1:2], EPS_LN, SX ** -2, ALU.add, ALU.mult))
                st.chain(rsqrt(rs1[:], ms1[:], 1))

            def row_stats2(b):
                st.chain(dve.bn_stats(stats[:], xres[:, b, :]))
                st.did(dve.tensor_copy(statc[:], stats[:]))
                st.chain(dve.bn_aggr(mv[:], stats[:]))
                st.did(dve.tensor_scalar(xssq[0:S, 128:129], mv[:, 1:2], EPS_LN, SX ** -2, ALU.add, ALU.mult))

            def normed2(b, rs):
                wait(dve, "pe_xT2", b - 1, 1)
                dve.tensor_scalar(xn[:], xres[:, b, :], mv[:, 0:1], rs, ALU.subtract, ALU.mult)\
                   .then_inc(sig["d_xn2"], 1)

            def x2_lo(b):
                wait(dve, "a_x2", b, 1)
                wait(dve, "pe_proj", b - 1, 1)
                dve.tensor_tensor(xl[:], A[0][:, 0:KT * S].rearrange("p (k s) -> p k s", k=KT), xh[:],
                                  ALU.subtract).then_inc(sig["d_x2"], 1)

            def square_sums(b, n):
                wait(dve, "a_sq2", b, n + 1)
                rows, slot = (S, 3) if n == 0 else (KC, n - 1)
                if n == 0:
                    wait(dve, "d_rstd2", b - 1, 1)
                dve.tensor_reduce(xssq[0:rows, slot * XH:(slot + 1) * XH],
                                  xsq[0:rows, n % 2].rearrange("p (h d) -> p h d", h=XH), AX.X, ALU.add)\
                   .then_inc(sig["d_ssq2"], 1)

            def rms_start(b, par):
                wait(dve, "d_ssq2", b, 4)
                wait(dve, "g_kn", b - 2, 8)
                wait(dve, "g_qn", b - 2, 1)
                wait(dve, "d_xn2", b, 1)
                st.chain(dve.tensor_scalar(xssq[:, 0:128], xssq[:, 0:128], SN ** -2 / XD,
                                           EPS_RMS * (SX * SW / SN) ** 2, ALU.mult, ALU.add))
                y = xrstd[par].bitcast(I32)
                st.chain(dve.tensor_scalar(y, xssq.bitcast(I32), 1, None, ALU.logical_shift_right))
                st.did(dve.tensor_scalar(y, y, -1, 0x5f3759df, ALU.mult, ALU.add))

            def rms_step(par, last=False):
                y = xrstd[par]
                a, c = xnw[:, 0, :], xnw[:, 1, :]
                st.wait()
                st.chain(dve.scalar_tensor_tensor(a, y, -0.5, y, ALU.mult, ALU.mult))
                st.chain(dve.tensor_tensor(c, a, xssq, ALU.mult))
                ins = dve.scalar_tensor_tensor(y, c, 1.5, y, ALU.add, ALU.mult)
                if last:
                    ins.then_inc(sig["d_rstd2"], 1)
                else:
                    st.did(ins)

            def v2_lo(b, c, par):
                wait(dve, "a_v2", b, c + 1)
                v = vst[par][:, c].rearrange("p (h v) -> p h v", h=XH)
                dve.scalar_tensor_tensor(v[:, :, XD:2 * XD], A[(c + 1) % 2][0:KC, :].rearrange("p (h d) -> p h d", h=XH), SV,
                                         v[:, :, 0:XD], ALU.mult, ALU.subtract).then_inc(sig["d_v2"], 1)

            def q_stack_lo(b, par):
                wait(dve, "a_qst", b, 1)
                q = qst[par].rearrange("p h (u w) d -> p h u w d", u=2)
                dve.tensor_tensor(q[:, :, :, 1, :],
                                  qn.rearrange("p (h d) -> p h d", h=XH).unsqueeze(2).broadcast_to([S, XH, 2, XD]),
                                  q[:, :, :, 0, :], ALU.subtract).then_inc(sig["d_qst"], 1)

            def k_stack_lo(b, m):
                wait(dve, "a_kst", b, m + 1)
                k = kst[m % 2].rearrange("p c (h u d) -> p (c h) u d", h=GH, u=4)
                dve.tensor_tensor(k[:, :, 2:4, :], kn[m % 2].unsqueeze(2).broadcast_to([KC, NC * GH, 2, XD]),
                                  k[:, :, 0:2, :], ALU.subtract).then_inc(sig["d_kst"], 1)

            def queries_back(b, m):
                wait(dve, "pe_T", b, m + 1)
                bb, mm = later(b, m, -2)
                wait(dve, "pe_sc", bb, mm * NC + NC)
                q = B[0][:, :].bitcast(F16)[:, 2 * NC * KC:2 * NC * KC + 2 * S].rearrange("p (n s) -> p n s", n=2)
                st.did(dve.tensor_copy(qbd[m % 2][0:64, :, 0:S], q[0:64]))
                dve.tensor_copy(qbd[m % 2][64:128, :, S:2 * S], q[64:128]).then_inc(sig["d_T"], 1)

            def e_high(b, m):
                wait(dve, "a_e", b, NC * (m + 1))
                bb, mm = later(b, m, -2)
                wait(dve, "pe_pv", bb, mm + 1)
                dve.tensor_copy(eh[m % 2], eb[m % 2]).then_inc(sig["d_eh"], 1)

            def scales3():
                dve.wait_ge(g_sum, 1)
                st.chain(dve.tensor_scalar(fsc[:, 3:6], fsc[:, 3:6], 1.0 / (FE * DM), 1e-8, ALU.mult, ALU.add))
                st.did(dve.tensor_scalar(fsc[:, 9:12], fsc[:, 3:6], 0.5, None, ALU.mult))
                st.did(dve.tensor_scalar(fsc[:, 12:15], fsc[:, 3:6], -0.5, None, ALU.mult))
                st.did(dve.tensor_scalar(fsc[:, 6:7], fsc[:, 3:4], -1.0 / SX, None, ALU.mult))
                st.chain(dve.reciprocal(fsc[:, 7:8], fsc[:, 3:4]))
                st.did(dve.tensor_scalar(fsc[:, 7:8], fsc[:, 7:8], 1.0 / (SX * SH), None, ALU.mult))
                st.chain(dve.tensor_tensor(fsc[:, 8:9], fsc[:, 3:4], fsc[:, 4:5], ALU.mult))
                st.chain(dve.scalar_tensor_tensor(fsc[:, 8:9], fsc[:, 8:9], SH, fsc[:, 5:6], ALU.mult, ALU.mult))

            def ternary(n):
                dve.wait_ge(ld_f[n % 2], 16 * (NB // 2 + n // 2 + 1))
                if n > 0:
                    dve.wait_ge(d_tern, n)
                w = stage[:, n % 2].rearrange("p k n -> p (k n)")
                st.chain(dve.tensor_scalar(wgt, w, fsc[:, 9 + n % 3:10 + n % 3], None, ALU.is_gt))
                dve.scalar_tensor_tensor(wf[:, n].rearrange("p k n -> p (k n)"), w, fsc[:, 12 + n % 3:13 + n % 3],
                                         wgt, ALU.is_lt, ALU.subtract).then_inc(d_tern, 1)

            def row_stats3(u):
                for r in range(UB):
                    st.did(dve.bn_stats(stats3[:, r], xres[:, u * UB + r, :]))
                st.wait()
                st.did(dve.tensor_copy(statc3[:], stats3[:]))
                for r in range(UB):
                    st.did(dve.bn_aggr(mv3[:, r], stats3[:, r]))
                st.wait()
                st.chain(dve.tensor_scalar(ms3[:], mv3[:, :, 1], EPS_LN, SX ** -2, ALU.add, ALU.mult))
                st.chain(rsqrt(rs3[:], ms3[:], UB))

            def normed3(u, r):
                wait(dve, "pe_xT3", u - 1, 4)
                dve.tensor_scalar(xn3[r], xres[:, u * UB + r, :], mv3[:, r, 0:1], rs3[:, r:r + 1],
                                  ALU.subtract, ALU.mult).then_inc(sig["d_xn3"], 1)

            def x3_lo(u, r, bank):
                wait(dve, "a_x3", u, r + 1)
                wait(dve, "pe_up", u - 1, 16)
                dve.tensor_tensor(fl[:, :, r * S:(r + 1) * S],
                                  bank[:, 0:KT * S].rearrange("p (k s) -> p k s", k=KT),
                                  fh[:, :, r * S:(r + 1) * S], ALU.subtract).then_inc(sig["d_x3"], 1)

            def add_cross(b):
                wait(dve, "a_ob", b, 4)
                st.did(dve.reciprocal(oinv, ob[:, :, 2 * XD]))
                st.chain(dve.tensor_tensor(osum.rearrange("p (h d) -> p h d", h=XH), ob[:, :, 0:XD],
                                           ob[:, :, XD:2 * XD], ALU.add))
                o = osum.rearrange("p (h d) -> p h d", h=XH)
                st.chain(dve.tensor_tensor(o, o, oinv.unsqueeze(2).broadcast_to([S, XH, XD]), ALU.mult))
                dve.scalar_tensor_tensor(xres[:, b, :], osum, 1.0 / (SX * SW * SV), xres[:, b, :],
                                         ALU.mult, ALU.add).then_inc(sig["d_x2out"], 1)

            dve.wait_ge(sig["d_x1"], NB + 1)
            layer_norm2(0)
            normed2(0, rs1[:, 0:1])
            x2_lo(0)
            ctx_lo(0)
            row_stats2(1)
            for n in range(4):
                square_sums(0, n)
            rms_start(0, 0)
            for n in range(3):
                rms_step(0, n == 2)
            wait(dve, "d_rstd2", 0, 1)
            normed2(1, xrstd[0][0:S, 128:129])
            for c in range(NC):
                v2_lo(0, c, 0)
            x2_lo(1)
            ctx_lo(1)
            q_stack_lo(0, 0)
            for m in range(3):
                k_stack_lo(0, m)
                if m < 2:
                    queries_back(0, m)
            e_high(0, 0)
            square_sums(1, 0)

            def turn(b, par, end):
                for m in range(NG):
                    bb, mm = later(b, m, 2)
                    if mm > 1 or end < 2:
                        queries_back(bb, mm)
                    if m == 3 and end < 2:
                        rms_start(b + 1, 1 - par)
                    bb, mm = later(b, m, 1)
                    if mm > 0 or end < 2:
                        e_high(bb, mm)
                    if m == 3 and end < 2:
                        rms_step(1 - par)
                    if m == 5 and end < 2:
                        q_stack_lo(b + 1, 1 - par)
                    bb, mm = later(b, m, 3)
                    if mm > 2 or end < 2:
                        k_stack_lo(bb, mm)
                    if m == 3 and end < 2:
                        rms_step(1 - par)
                    if end < 2 and m < 3:
                        square_sums(b + 1, m + 1)
                    elif end < 2 and m < 6:
                        v2_lo(b + 1, m - 3, 1 - par)
                    elif end < 1 and m == 6:
                        x2_lo(b + 2)
                        ctx_lo(b + 2)
                    elif end < 1 and m == 7:
                        square_sums(b + 2, 0)
                    if end < 1 and m == 1:
                        row_stats2(b + 2)
                    if m == 3 and end < 2:
                        rms_step(1 - par, last=True)
                    if m == 4 and end < 1:
                        wait(dve, "d_rstd2", b + 1, 1)
                        normed2(b + 2, xrstd[1 - par][0:S, 128:129])
                    if end == 2:
                        if m == 0:
                            wait(dve, "a_abs", NB - 1, 3)
                            dve.tensor_reduce(fsc[:, 0:3], asum[:, :, :, 0], AX.X, ALU.add).then_inc(d_fsc, 1)
                            wait(dve, "d_x2out", UB - 1, 1)
                            row_stats3(0)
                        elif m == 1:
                            for r in range(UB):
                                normed3(0, r)
                            scales3()
                        if m == 2:
                            wait(dve, "pe_proj", b, 7)
                            wait(dve, "pe_pv", b - 1, 8)
                        if m == 4:
                            wait(dve, "g_kn", b, 8)
                        if m >= 2:
                            ternary(m - 2)
                        if 2 <= m < 6:
                            x3_lo(0, m - 2, A[m % 2])
                add_cross(b)

            two_ways(dve, turn, st, 52)

            def hidden(u, e):
                wait(dve, "a_sg", u, e + 1)
                if e >= 2:
                    wait(dve, "a_hh", u, e - 1)
                    wait(dve, "d_hl", u, e - 1)
                else:
                    wait(dve, "a_hh", u - 1, 15 + e)
                    wait(dve, "d_hl", u - 1, 15 + e)
                dve.scalar_tensor_tensor(hd[e % 2], C[2 * (e % 2) + 1][:, 0:UB * S], fsc[:, 7:8], sg[e % 2],
                                         ALU.mult, ALU.mult).then_inc(sig["d_hd"], 1)

            def hidden_lo(u, e):
                wait(dve, "a_hh", u, e + 1)
                if e >= 2:
                    wait(dve, "pe_dn", u, e - 1)
                else:
                    wait(dve, "pe_dn", u - 1, 15 + e)
                dve.tensor_tensor(hl[e % 2], hd[e % 2], hh[e % 2], ALU.subtract).then_inc(sig["d_hl"], 1)

            def unit(u, first=False, last=False):
                hidden(u, 0)
                for e in range(ET):
                    hidden_lo(u, e)
                    if e + 1 < ET:
                        hidden(u, e + 1)
                    if first and e % 4 < 3 and 3 * (e // 4) + e % 4 + 6 < 12:
                        ternary(3 * (e // 4) + e % 4 + 6)
                    if e == 9 and not last:
                        row_stats3(u + 1)
                    elif 10 <= e < 14 and not last:
                        normed3(u + 1, e - 10)
                    elif e == ET - 2 and not last:
                        x3_lo(u + 1, 0, C[0])
                        x3_lo(u + 1, 1, C[1])
                if not last:
                    x3_lo(u + 1, 2, C[0])
                    x3_lo(u + 1, 3, C[1])
                for r in range(UB):
                    wait(dve, "pe_dn", u, 16)
                    dve.scalar_tensor_tensor(xres[:, u * UB + r, :], (A + B)[r][0:S, :], fsc[0:S, 8:9],
                                             xres[:, u * UB + r, :], ALU.mult, ALU.add).then_inc(sig["d_y"], 1)

            wait(dve, "pe_pv", NB - 1, 8)
            wait(dve, "d_x2out", NB - 1, 1)
            unit(0, first=True)
            with dve.Fori(0, NB // UB - 2) as i:
                st.begin(i, 21)
                unit(i + 1)
            st.end(NB // UB - 2)
            unit(NB // UB - 1, last=True)

        @block.tensor
        def _(pe):
            credit(pe, "p")
            ident = cst[0:128, C_ID:C_ID + 128]

            def x_turn(b):
                wait(pe, "d_xn", b, 1)
                wait(pe, "d_zT", b - 1, 4)
                for k in range(KT):
                    ins = pe.transpose(B[1][:, k * S:(k + 1) * S], xn[:, k * 128:(k + 1) * 128], ident[0:S, 0:S])
                ins.then_inc(sig["pe_xT"], 1)

            def project(b, j):
                if j == 0:
                    wait(pe, "a_xhi", b, 1)
                    wait(pe, "d_xlo", b, 1)
                    wait(pe, "d_x1", b - 2, 1)
                elif j == 1:
                    wait(pe, "a_v", b - 1, 1)
                else:
                    wait(pe, "a_sq", b, j - 1)
                    wait(pe, "d_t", b, j - 1)
                    wait(pe, "d_u", b, j - 1)
                n = 0
                for xp, wp in ((xh, wqh), (xh, wql), (xl, wqh)):
                    for k in range(KT):
                        ins = pe.matmul(A[j % 2][0:S, :], xp[:, k, :], wp[:, j, k, :], start=(n == 0), stop=(n == 11))
                        n += 1
                ins.then_inc(sig["pe_qkv"], 1)

            def z_turn(b, g):
                wait(pe, "g_z", b, g + 1)
                if g < 2:
                    wait(pe, "a_pT", b - 1, 3 + g)
                else:
                    wait(pe, "d_zT", b, g - 1)
                for h in range(4):
                    ins = pe.transpose(B[g % 2][:, h * S:(h + 1) * S], zb[:, g, h * D:(h + 1) * D], ident[0:S, 0:S])
                ins.then_inc(sig["pe_zT"], 1)

            def scores(b, g):
                wait(pe, "d_zT", b, g + 2)
                wait(pe, "d_alo", b - 1, g + 1)
                bank = C[g][0:S, 0:400]
                pe.matmul(bank, idb[:], maskb[:].rearrange("p h k -> p (h k)"), start=True, stop=True)
                for h in range(4):
                    ins = pe.matmul(bank[:, h * S:(h + 1) * S], qk[:, g + 1, h, :], qk[:, 0, g, :],
                                    start=False, stop=True, skip_group_check=True)
                ins.then_inc(sig["pe_s"], 1)

            def p_turn(b, g):
                wait(pe, "g_p", b, g + 1)
                if g == 0:
                    wait(pe, "d_zT", b, 5)
                elif g >= 2:
                    wait(pe, "a_pT", b, g - 1)
                for h in range(4):
                    n = 4 * g + h
                    ins = pe.transpose(B[g % 2][0:S, h * S:(h + 1) * S], pr[:, n * S:(n + 1) * S], ident[0:S, 0:S])
                ins.then_inc(sig["pe_pT"], 1)

            def attend(b, g):
                wait(pe, "a_pT", b, g + 1)
                if g == 0:
                    wait(pe, "a_v", b, 1)
                pe.matmul(C[g][:, 0:400], vv[:, g * D:(g + 1) * D], pT[:, g * 400:(g + 1) * 400],
                          start=True, stop=True).then_inc(sig["pe_av"], 1)

            def project_out(b):
                n = 0
                for g in range(4):
                    wait(pe, "a_ahi", b, g + 1)
                    wait(pe, "d_alo", b, g + 1)
                    for h in range(4 * g, 4 * g + 4):
                        for ap, wp in ((ah, woh), (ah, wol), (al, woh)):
                            ins = pe.matmul(A[0][0:S, :], ap[:, h, :], wp[:, h, :], start=(n == 0), stop=(n == 47))
                            n += 1
                ins.then_inc(sig["pe_o"], 1)

            pe.wait_ge(ld_c, 48)
            pe.wait_ge(g_setup, 3)
            x_turn(0)
            for j in range(6):
                pe.wait_ge(a_whi, j + 1)
                pe.wait_ge(d_wlo, j + 1)
                project(0, j)

            def turn(b, last=False):
                z_turn(b, 2)
                z_turn(b, 3)
                scores(b, 0)
                z_turn(b, 4)
                scores(b, 1)
                if not last:
                    x_turn(b + 1)
                scores(b, 2)
                scores(b, 3)
                if not last:
                    for j in range(5):
                        project(b + 1, j)
                p_turn(b, 0)
                p_turn(b, 1)
                attend(b, 0)
                p_turn(b, 2)
                attend(b, 1)
                p_turn(b, 3)
                attend(b, 2)
                attend(b, 3)
                if not last:
                    project(b + 1, 5)
                    z_turn(b + 1, 0)
                    z_turn(b + 1, 1)
                project_out(b)

            z_turn(0, 0)
            z_turn(0, 1)
            pe.wait_ge(a_whi, wchunks)
            pe.wait_ge(d_wlo, wchunks)
            with pe.Fori(0, NB - 1) as b:
                turn(b)
            turn(NB - 1, last=True)

            pe.wait_ge(sig["d_x1"], NB + 1)
            pe.wait_ge(g_zero, 6)

            def x2_turn(b):
                wait(pe, "d_xn2", b, 1)
                wait(pe, "d_v2", b - 1, 2)
                for k in range(KT):
                    ins = pe.transpose(A[0][:, k * S:(k + 1) * S], xn[:, k * 128:(k + 1) * 128], ident[0:S, 0:S])
                ins.then_inc(sig["pe_xT2"], 1)

            def project2(b, n):
                if n == 0:
                    wait(pe, "a_x2", b, 1)
                    wait(pe, "d_x2", b, 1)
                    wait(pe, "d_v2", b - 1, 3)
                elif n == 1:
                    wait(pe, "a_ctx", b, 1)
                    wait(pe, "d_ctx", b, 1)
                elif n <= 5:
                    wait(pe, "a_sq2", b, n - 1)
                else:
                    wait(pe, "d_v2", b, 1)
                i = 0
                for hi, wp in ((1, wxh), (1, wxl), (0, wxh)):
                    for k in range(KT):
                        if n == 0:
                            rows, lhs = S, (xh if hi else xl)[:, k, :]
                        else:
                            c = (n - 1) % 3
                            rows, lhs = KC, (ch if hi else cl)[:, k, c * KC:(c + 1) * KC]
                        ins = pe.matmul(A[(n + 1) % 2][0:rows, :], lhs, wp[:, 0 if n == 0 else 1 if n < 4 else 2, k, :],
                                        start=(i == 0), stop=(i == 11))
                        i += 1
                ins.then_inc(sig["pe_proj"], 1)

            def turn_heads(b, m, par):
                wait(pe, "d_kst", b, m + 1)
                wait(pe, "a_kst", b, m + 1)
                wait(pe, "d_qst", b, 1)
                bb, mm = later(b, m, -1)
                wait(pe, "d_T", bb, mm + 1)
                wait(pe, "a_T", bb, mm + 1)
                bank = B[0][:, :].bitcast(F16)
                for j in range(2):
                    for c in range(NC):
                        n = j * NC + c
                        pe.transpose(bank[:, n * KC:(n + 1) * KC], kst[m % 2][:, c, j * 128:(j + 1) * 128],
                                     idh[0:KC, 0:KC])
                at = 2 * NC * KC
                for j in range(2):
                    h = m * GH + 2 * j
                    ins = pe.transpose(bank[:, at + j * S:at + (j + 1) * S],
                                       qst[par][:, h:h + 2].rearrange("p h u d -> p (h u d)"), idh[0:S, 0:S])
                ins.then_inc(sig["pe_T"], 1)

            def scores2(b, m):
                wait(pe, "d_T", b, m + 1)
                wait(pe, "a_T", b, m + 1)
                for c in range(NC):
                    n = m * NC + c
                    bb, mm = (b, n) if n >= 4 else (b - 1, n + 24)
                    wait(pe, "a_e", bb, mm - 3)
                    for j in range(2):
                        ins = pe.matmul(C[n % 4][0:KC, j * 2 * S:(j + 1) * 2 * S], kT[m % 2][:, j * NC + c, :],
                                        qbd[m % 2][:, j, :], start=True, stop=True)
                    ins.then_inc(sig["pe_sc"], 1)

            def attend2(b, m, par):
                wait(pe, "d_eh", b, m + 1)
                wait(pe, "g_el", b, m + 1)
                if m == 0:
                    wait(pe, "a_v2", b, 3)
                    wait(pe, "d_v2", b, 3)
                if m % 2 == 0:
                    bb, mm = (b, m // 2) if m else (b - 1, 4)
                    wait(pe, "a_ob", bb, mm)
                for h in range(GH):
                    n = 0
                    at = ((m % 2) * GH + h) * VW
                    for c in range(NC):
                        for e in (eh, el):
                            ins = pe.matmul(B[1][0:S, at:at + VW], e[m % 2][:, c, h * S:(h + 1) * S],
                                            vst[par][:, c, (m * GH + h) * VW:(m * GH + h + 1) * VW],
                                            start=(n == 0), stop=(n == 5))
                            n += 1
                ins.then_inc(sig["pe_pv"], 1)

            def x3_turn(u, r, bank):
                wait(pe, "d_xn3", u, r + 1)
                if r >= 2:
                    wait(pe, "d_x3", u, r - 1)
                for k in range(KT):
                    ins = pe.transpose(bank[:, k * S:(k + 1) * S], xn3[r][:, k * 128:(k + 1) * 128], ident[0:S, 0:S])
                ins.then_inc(sig["pe_xT3"], 1)

            x2_turn(0)
            for n in range(7):
                project2(0, n)
            x2_turn(1)
            turn_heads(0, 0, 0)
            turn_heads(0, 1, 0)
            scores2(0, 0)
            project2(1, 0)

            def turn(b, par, end):
                for m in range(NG):
                    bb, mm = later(b, m, 1)
                    if mm > 0 or end < 2:
                        scores2(bb, mm)
                    bb, mm = later(b, m, 2)
                    if mm > 1 or end < 2:
                        turn_heads(bb, mm, par if mm > 1 else 1 - par)
                    if end < 2 and m < 6:
                        project2(b + 1, m + 1)
                    elif end < 1 and m == 6:
                        x2_turn(b + 2)
                    elif end < 1 and m == 7:
                        project2(b + 2, 0)
                    elif end == 2 and 2 <= m < 6:
                        if m == 2:
                            wait(pe, "d_v2", b, 3)
                        x3_turn(0, m - 2, A[m % 2])
                    attend2(b, m, par)

            two_ways(pe, turn)

            def up_gate(u, e, first=False):
                if e == 0:
                    wait(pe, "d_x3", u, 4)
                if e >= 2:
                    wait(pe, "d_hd", u, e - 1)
                if first and e % 4 == 0:
                    pe.wait_ge(d_tern, 3 * (e // 4) + 2)
                for half in range(2):
                    n = 0
                    for part in (fh, fl):
                        for k in range(KT):
                            ins = pe.matmul(C[2 * (e % 2) + half][:, 0:UB * S],
                                            wf[:, 3 * (e // 4) + half, k, (e % 4) * 128:(e % 4 + 1) * 128],
                                            part[:, k, :], start=(n == 0), stop=(n == 7))
                            n += 1
                ins.then_inc(sig["pe_up"], 1)

            def down(u, e, first=False):
                wait(pe, "a_hh", u, e + 1)
                wait(pe, "d_hl", u, e + 1)
                if e == 0:
                    wait(pe, "d_y", u - 1, 4)
                if first and e % 4 == 0:
                    pe.wait_ge(d_tern, 3 * (e // 4) + 3)
                for r in range(UB):
                    for part in (hh, hl):
                        ins = pe.matmul((A + B)[r][0:S, :], part[e % 2][:, r * S:(r + 1) * S], wf[:, 3 * (e // 4) + 2, e % 4, :],
                                        start=(e == 0 and part is hh), stop=(e == ET - 1 and part is hl))
                ins.then_inc(sig["pe_dn"], 1)

            def unit(u, first=False, last=False):
                up_gate(u, 0, first)
                for e in range(ET):
                    if e + 1 < ET:
                        up_gate(u, e + 1, first)
                    if not last and e == ET - 2:
                        wait(pe, "d_hd", u, ET - 1)
                        x3_turn(u + 1, 0, C[0])
                        x3_turn(u + 1, 1, C[1])
                    elif not last and e == ET - 1:
                        x3_turn(u + 1, 2, C[0])
                        x3_turn(u + 1, 3, C[1])
                    down(u, e, first)

            wait(pe, "a_e", NB - 1, 24)
            wait(pe, "a_ob", NB - 1, 4)
            unit(0, first=True)
            with pe.Fori(0, NB // UB - 2) as i:
                unit(i + 1)
            unit(NB // UB - 1, last=True)


def kernel(**inputs):
    import concourse.bacc as _bacc
    from concourse import mybir as _mybir
    from concourse.bass_utils import run_bass_kernel_spmd as _run

    f = {k: np.asarray(v) for k, v in inputs.items()}
    tiles = lambda w: w.T.reshape(w.shape[1] // 128, 128, w.shape[0]).transpose(1, 0, 2)
    wqkv = f["L0_attn_w_qkv"]
    q, k, v = wqkv[:H * D], wqkv[H * D:(H + HKV) * D], wqkv[(H + HKV) * D:]
    wqkv = tiles(np.concatenate([k, q, v]))
    wqkv = wqkv.reshape(128, KT, 6, 512).transpose(0, 2, 1, 3)
    wo = tiles(f["L0_attn_w_o"]).reshape(128, 4, 4, DM)
    wkv = np.concatenate([f["L0_xattn_Wk"], f["L0_xattn_Wv"]])
    wx = tiles(np.concatenate([f["L0_xattn_Wq"], wkv[0::2], wkv[1::2]]))
    wx = wx.reshape(128, KT, 3, 512).transpose(0, 2, 1, 3)
    ctxt = f["ctx_2048"].transpose(0, 2, 1).reshape(NB, KT, 128, CTX).transpose(0, 2, 1, 3)
    updown = [tiles(f["L0_ffn_" + n]).reshape(128, KT, 4, 512).transpose(0, 2, 1, 3) for n in ("W_up", "W_gate")]
    wffn = np.concatenate(updown + [tiles(f["L0_ffn_W_down"]).reshape(128, 4, 4, DM)], 1)
    swap = lambda a: np.concatenate([a[HALF:], a[:HALF]])
    gq, gk, bq, bk = (f["L0_attn_" + n] for n in ("qn_g", "kn_g", "qn_b", "kn_b"))
    gains = np.broadcast_to(np.concatenate([gq, swap(gq), gk, swap(gk)]), (S, 4 * D))
    bcols = np.stack([bq, swap(bq), bk, swap(bk)], 1)
    arrays = {
        "x": f["x"].reshape(NB * S, DM), "wqkv": wqkv, "wo": wo, "wx": wx, "ctxt": ctxt, "wffn": wffn, "gains": gains, "bcols": bcols,
        "consts": constants(),
    }
    arrays = {f"in_{n}": np.ascontiguousarray(a) for n, a in arrays.items()}
    nc = _bacc.Bacc("TRN2", target_bir_lowering=False, num_devices=1)
    args = [nc.dram_tensor(n, a.shape, _mybir.dt.from_np(a.dtype), kind="ExternalInput").ap() for n, a in arrays.items()]
    out = nc.dram_tensor("out_x", (NB * S, DM), F32, kind="ExternalOutput").ap()
    build(nc, *args, out)
    r = _run(nc, [arrays], core_ids=[0])
    return r.results[0]["out_x"].reshape(NB, S, DM)
```

```python
from contextlib import ExitStack

import numpy as np
import concourse.bass as bass
from concourse import mybir

F32 = mybir.dt.float32
F16 = mybir.dt.float16
BF16 = mybir.dt.bfloat16
I32 = mybir.dt.int32
ALU = mybir.AluOpType
ACT = mybir.ActivationFunctionType
AX = mybir.AxisListType

NB, S, DM = 16, 100, 512
KT = DM // 128
H, HKV, D = 16, 4, 128
REP = H // HKV
ROPE_BASE = 1000000.0
EPS_LN = 1e-5
EPS_RMS = 1e-6
CTX = 361
XH, XD = 32, 16
KC = 122
NC = 3
CTXP = KC * NC
FE = 2048
HALF = D // 2

SX = 64.0
SW = 256.0
SA = 32.0
SN = 1024.0
SV = 2.0 ** -9
SH = 8.0
VW = 2 * XD + 1
GH = 4
NG = XH // GH
UB = 4
ET = FE // 128
TERNARY_AT = (0, 1, 2, 4, 5, 7, 8, 9, 11)

C_ID, C_COS, C_SIN, C_COST, C_SINT, C_MASK, C_ONE, C_END = 0, 128, 256, 384, 484, 584, 684, 687


def constants():
    inv = (np.float32(1.0) / np.float32(ROPE_BASE) ** (np.arange(0, D, 2, dtype=np.float32) / np.float32(D))).astype(np.float32)
    f = np.outer(np.arange(S, dtype=np.float32), inv).astype(np.float32)
    cos = np.concatenate([np.cos(f), np.cos(f)], -1).astype(np.float32)
    sin = np.concatenate([-np.sin(f), np.sin(f)], -1).astype(np.float32)
    c = np.zeros((128, C_END), np.float32)
    c[:, C_ID:C_ID + 128] = np.eye(128)
    c[:S, C_COS:C_COS + D] = cos
    c[:S, C_SIN:C_SIN + D] = sin
    c[:, C_COST:C_COST + S] = cos.T
    c[:, C_SINT:C_SINT + S] = sin.T
    c[:S, C_MASK:C_MASK + S] = np.where(np.triu(np.ones((S, S)), 1) > 0, np.float32(-1e30), np.float32(0))
    c[:KC, C_ONE:C_ONE + NC] = (np.arange(CTXP) < CTX).reshape(NC, KC).T
    return c


class Steps:

    def __init__(self, eng, sem):
        self.eng, self.sem, self.n, self.turn, self.per = eng, sem, 0, 0, 0

    def did(self, ins):
        ins.then_inc(self.sem, 1)
        self.n += 1

    def wait(self, back=0):
        self.eng.wait_ge(self.sem, self.turn + (self.n - back))

    def chain(self, ins):
        self.did(ins)
        self.wait()

    def begin(self, i, per):
        self.turn, self.per, self.first = i * per, per, self.n

    def end(self, turns):
        assert self.n - self.first == self.per, (self.n - self.first, self.per)
        self.n += (turns - 1) * self.per
        self.turn = 0


def build(nc, x, wqkv, wo, wx, ctxt, wffn, gains, bcols, consts, out):
    with ExitStack() as ctx:
        def sb(name, shape, dt=F32):
            return ctx.enter_context(nc.sbuf_tensor(name, shape, dt))

        def sem(name):
            return ctx.enter_context(nc.semaphore(name))

        xres = sb("xres", [S, NB, DM])
        cst = sb("cst", [128, C_END])
        gain = sb("gain", [S, 4 * D])
        bcol = sb("bcol", [128, 4])
        stageb = sb("stageb", [128, 2 * KT * 512])
        stage = stageb[:, :].rearrange("p (t k n) -> p t k n", t=2, k=KT)
        ropeA = sb("ropeA", [S, 2, D])
        ropeB = sb("ropeB", [S, 2, D])
        ropeC = sb("ropeC", [128, 2, S])
        wmean = sb("wmean", [128, 5, KT * 4])
        wxh = sb("wxh", [128, 3, KT, 512], F16)
        wxl = sb("wxl", [128, 3, KT, 512], F16)
        arena = sb("arena", [128, 20480])

        region2 = sb("region2", [128, 5 * 512])
        region3 = sb("region3", [128, H * S])

        def carver(region=arena):
            at = [0]

            def carve(shape, dt=F32):
                n = int(np.prod(shape[1:]))
                words = n * (2 if dt in (F16, BF16) else 4) // 4
                v = region[0:shape[0], at[0]:at[0] + words]
                at[0] += words
                if dt != F32:
                    v = v.bitcast(dt)
                names = "abcd"[:len(shape) - 1]
                if len(names) > 1:
                    v = v.rearrange(f"p ({' '.join(names)}) -> p {' '.join(names)}",
                                    **{k: n for k, n in zip(names[1:], shape[2:])})
                return v
            return carve

        carve = carver()
        wqh = carve([128, 6, KT, 512], F16)
        wql = carve([128, 6, KT, 512], F16)
        wohl = carve([128, 4, 2, 4, DM], F16)
        carve = carver()
        raw = [carve([KC, 4, 512]) for _ in range(2)]
        ctxs = carve([128, KT, CTXP])
        ch = carve([128, KT, CTXP], F16)
        cl = carve([128, KT, CTXP], F16)
        qst0 = carve([S, XH, 4, XD], F16)
        vst0 = carve([KC, NC, XH * VW], F16)
        kn = [carve([KC, NC * GH, XD]) for _ in range(2)]
        kst = [carve([KC, NC, GH * 4 * XD], F16) for _ in range(2)]
        kT = [carve([128, 2 * NC, KC], F16) for _ in range(2)]
        qbd = [carve([128, 2, 2 * S], F16) for _ in range(2)]
        carve([128, 372])
        qst = [qst0, carve([S, XH, 4, XD], F16)]
        vst = [vst0, carve([KC, NC, XH * VW], F16)]
        eb = [carve([KC, NC, GH * S]) for _ in range(2)]
        eh = [carve([KC, NC, GH * S], F16) for _ in range(2)]
        el = [carve([KC, NC, GH * S], F16) for _ in range(2)]
        carve = carver()
        xstage = [carve([128, KT, 512]) for _ in range(2)]
        carve([128, ctxs.shape[1] * CTXP * 2])
        xstage.append(carve([128, KT, 512]))
        carve = carver()
        carve([128, 2 * 6 * KT * 256])
        wstage = [stage[:, 0], stage[:, 1]] + [carve([128, KT, 512]) for _ in range(4)]
        ostage = [w[:, :].rearrange("p a k n -> p (a k n)").bitcast(F32)[:, 0:2048].rearrange("p (k n) -> p k n", k=KT)
                  for w in (wxh, wxl)]
        carve = carver(stageb)
        pT = carve([S, H * S])
        ah = carve([128, H, S], F16)
        al = carve([128, H, S], F16)
        carve = carver(region3)
        pr = carve([S, H * S])
        carve = carver(region3)
        ob = carve([S, XH, VW])
        osum = carve([S, DM])
        carve = carver(region2)
        zb = carve([S, 5, 512])
        carve = carver(region2)
        xsq = carve([KC, 2, 512])
        xssq = carve([KC, 129])
        xrstd = [carve([KC, 129]) for _ in range(2)]
        xnw = carve([KC, 2, 129])
        oinv = carve([S, XH])
        qn = carve([S, 512])
        carve = carver()
        fh = carve([128, KT, UB * S], F16)
        fl = carve([128, KT, UB * S], F16)
        sg = [carve([128, UB * S]) for _ in range(2)]
        hd = [carve([128, UB * S]) for _ in range(2)]
        hh = [carve([128, UB * S], F16) for _ in range(2)]
        hl = [carve([128, UB * S], F16) for _ in range(2)]
        carve([128, 96])
        wf = carve([128, 12, 4, 512], BF16)
        fstages = [stage[:, 0], stage[:, 1]] + [carve([128, 4, 512]) for _ in range(2)]
        yT = region3[:, :].rearrange("p (k s) -> p k s", k=KT)
        asum = sb("asum", [128, 3, NB, 1])
        fsc = sb("fsc", [128, 16])
        idh = sb("idh", [128, 128], F16)
        statc = sb("statc", [S, 6])
        stats = sb("stats", [S, 6])
        mv = sb("mv", [S, 2])
        stats3 = sb("stats3", [S, UB, 6])
        statc3 = sb("statc3", [S, UB, 6])
        mv3 = sb("mv3", [S, UB, 2])
        ms3 = sb("ms3", [S, UB])
        rs3 = sb("rs3", [S, UB])
        ms1 = sb("ms1", [S, 1])
        nwt = sb("nwt", [128, 3, 32])
        rs1 = sb("rs1", [S, 1])
        xn = sb("xn", [S, DM])
        xh = sb("xh", [128, KT, S], F16)
        xl = sb("xl", [128, KT, S], F16)
        sq = sb("sq", [S, 2, 512])
        tb = sb("tb", [S, 2, 512])
        ub = sb("ub", [S, 2, 512])
        ssq = sb("ssq", [S, 5 * 4 + 1])
        rstd = sb("rstd", [S, 5 * 4 + 1])
        qk = sb("qk", [128, 5, REP, S])
        vv = sb("vv", [S, HKV * D])
        xn3 = [tb[:, 0], tb[:, 1], ub[:, 0], ub[:, 1]]
        wgt = [qk[:, :].rearrange("p g h s -> p (g h s)")[:, 0:1024].bitcast(BF16),
               region2[:, 0:1024].bitcast(BF16)]
        smax = sb("smax", [S, H])
        negm = sb("negm", [S, H])
        rsum = sb("rsum", [S, H])
        rinv = sb("rinv", [S, H])

        A = [ctx.enter_context(nc.psum_tensor(f"A{i}", [128, 512], F32)) for i in range(2)]
        B = [ctx.enter_context(nc.psum_tensor(f"B{i}", [128, 512], F32)) for i in range(2)]
        C = [ctx.enter_context(nc.psum_tensor(f"C{i}", [128, 512], F32)) for i in range(4)]

        ld_c = sem("ld_c")
        ld_x0 = sem("ld_x0")
        ld_x = sem("ld_x")
        ld_w = [sem(f"ld_w{j}") for j in range(8)]
        ld_wx = [sem(f"ld_wx{j}") for j in range(3)]
        g_setup = sem("g_setup")
        d_tab = sem("d_tab")
        d_wmean, g_wcen, a_whi, d_wlo = sem("d_wmean"), sem("g_wcen"), sem("a_whi"), sem("d_wlo")
        d_step = sem("d_step")
        PER = dict(pe_xT=1, pe_qkv=6, pe_zT=5, pe_s=4, pe_pT=4, pe_av=4, pe_o=1,
                   a_xhi=1, a_sq=5, a_v=1, a_exp=16, a_pT=4, a_ahi=4,
                   d_xn=1, d_zT=5, d_xlo=1, d_negm=4, d_t=5, d_u=5, d_ssq=5, d_rstd=1, d_rinv=4,
                   d_alo=4, d_x1=1, g_w=5, g_z=5, g_p=4,
                   pe_xT2=1, pe_proj=7, pe_T=8, pe_sc=24, pe_pv=8,
                   a_ctx=1, a_x2=1, a_sq2=4, a_qst=1, a_v2=3, a_kst=8, a_T=8, a_e=24, a_ob=4, a_abs=3,
                   d_xn2=1, d_ctx=1, d_x2=1, d_ssq2=4, d_rstd2=1, d_qst=1, d_v2=3, d_kst=8, d_T=8,
                   d_eh=8, d_x2out=1,
                   g_kn=8, g_el=8, g_qn=1,
                   pe_xT3=4, pe_up=16, pe_dn=16, a_x3=4, a_sg=16, a_hh=16,
                   d_xn3=4, d_x3=4, d_hd=16, d_hl=16, d_y=4, pe_yT=4, a_y=1, d_yc=1)
        sig = {n: sem(n) for n in PER}

        def credit(eng, who):
            for n in PER:
                if n[0] == who:
                    eng.sem_inc(sig[n], PER[n])

        def wait(eng, name, b, n):
            eng.wait_ge(sig[name], (b + 1) * PER[name] + n)

        def staged(j):
            if j < 6:
                return wstage[j], ld_w[j], 16
            if j < 8:
                return ostage[j - 6], ld_w[j], 16
            if j < 10:
                return wstage[j - 8], ld_w[j - 8], 32
            return xstage[j - 10], ld_wx[j - 10], 16

        ld_ctx, g_zero, st_y = sem("ld_ctx"), sem("g_zero"), sem("st_y")
        g_ones, g_gt = sem("g_ones"), sem("g_gt")
        ld_f = [sem(f"ld_f{j}") for j in range(4)]

        def fstaged(n):
            slot = n % 2 if n < 4 else (n - 2) % 4
            turn = n // 2 if n < 4 else (n + 2) // 4
            return fstages[slot], ld_f[slot], 16 * (NB // 2 + turn + 1 if slot < 2 else turn)

        g_sum, d_fsc, d_tern = sem("g_sum"), sem("d_fsc"), sem("d_tern")

        def later(b, m, k):
            return b + (m + k) // NG, (m + k) % NG

        def two_ways(eng, turn, st=None, per=0):
            with eng.Fori(0, NB // 2 - 1) as i:
                if st:
                    st.begin(i, per)
                turn(i * 2, 0, 0)
                turn(i * 2 + 1, 1, 0)
            if st:
                st.end(NB // 2 - 1)
            turn(NB - 2, 0, 1)
            turn(NB - 1, 1, 2)

        block = ctx.enter_context(nc.Block())

        @block.sync
        def _(sp):
            sp.dma_start(cst[:], consts).then_inc(ld_c, 16)
            sp.dma_start(gain[:], gains).then_inc(ld_c, 16)
            sp.dma_start(bcol[:], bcols).then_inc(ld_c, 16)
            xt = x.rearrange("(b p) f -> p b f", b=NB)
            sp.dma_start(xres[:, 0, :], xt[:, 0, :]).then_inc(ld_x0, 16)
            for j in range(10):
                if j >= 8:
                    sp.wait_ge(a_whi, j - 7)
                    sp.wait_ge(d_wlo, j - 7)
                dst, loaded, _ = staged(j)
                sp.dma_start(dst, wqkv[:, j] if j < 6 else wo[:, j - 6]).then_inc(loaded, 16)
                if j == 5:
                    sp.dma_start(xres[:, 1:NB, :], xt[:, 1:NB, :]).then_inc(ld_x, 16)
            wait(sp, "pe_qkv", NB - 1, 6)
            for j in range(3):
                dst, loaded, _ = staged(10 + j)
                sp.dma_start(dst, wx[:, j]).then_inc(loaded, 16)

            def context(b):
                wait(sp, "a_ctx", b - 1, 1)
                wait(sp, "d_ctx", b - 1, 1)
                sp.dma_start(ctxs[:, :, 0:CTX], ctxt[b]).then_inc(ld_ctx, 16)

            wsum = wffn.rearrange("p (w c) k n -> p w (c k) n", w=3)

            def sixteenth(b, par):
                wait(sp, "a_abs", b - 2, 3)
                sp.dma_start(stage[:, par, 0:3], wsum[:, :, b]).then_inc(ld_f[par], 16)

            sp.wait_ge(g_zero, 1)
            context(0)
            context(1)
            wait(sp, "d_x1", NB - 1, 1)
            with sp.Fori(0, NB // 2 - 1) as i:
                for par in range(2):
                    sixteenth(i * 2 + par, par)
                    context(i * 2 + par + 2)
            for b in (NB - 2, NB - 1):
                sixteenth(b, b % 2)
            for n in range(12):
                if n < 2:
                    wait(sp, "a_abs", NB - 2 + n, 3)
                elif n < 4:
                    sp.wait_ge(d_tern, n - 1)
                elif n < 6:
                    wait(sp, "pe_pv", NB - 1, 8)
                else:
                    sp.wait_ge(d_tern, n - 3)
                dst, loaded, _ = fstaged(n)
                sp.dma_start(dst, wffn[:, 4 * (n % 3) + n // 3]).then_inc(loaded, 16)
            with sp.Fori(0, NB // UB) as u:
                for r in range(UB):
                    wait(sp, "d_y", u, r + 1)
                    sp.dma_start(out.rearrange("(b p) f -> p b f", b=NB)[:, u * UB + r, :],
                                 xres[:, u * UB + r, :]).then_inc(st_y, 16)
            sp.wait_ge(st_y, 16 * NB)

        @block.gpsimd
        def _(pool):
            credit(pool, "g")
            pool.wait_ge(ld_c, 48)
            pool.tensor_copy(idh[:], cst[:, C_ID:C_ID + 128]).then_inc(g_setup, 1)
            for j in range(5):
                pool.wait_ge(d_wmean, j + 1)
                w = staged(j)[0].rearrange("p k (h d) -> p (k h) d", h=4)
                pool.tensor_tensor(w, w, wmean[:, j].unsqueeze(2).broadcast_to([128, KT * 4, D]),
                                   ALU.subtract).then_inc(g_wcen, 1)

            def w_of(b, j):
                wait(pool, "d_t", b, j + 1)
                wait(pool, "d_u", b, j + 1)
                if j == 0:
                    wait(pool, "pe_zT", b - 1, 5)
                pool.tensor_tensor(zb[:, j], tb[:, j % 2], ub[:, j % 2], ALU.add).then_inc(sig["g_w"], 1)

            def z_of(b, j):
                wait(pool, "d_rstd", b, 1)
                wait(pool, "g_w", b, j + 1)
                r = rstd[:, 4 * j:4 * j + 4].unsqueeze(2).broadcast_to([S, 4, D])
                z = zb[:, j].rearrange("p (h d) -> p h d", h=4)
                pool.tensor_tensor(z, z, r, ALU.mult).then_inc(sig["g_z"], 1)

            def p_of(b, g):
                wait(pool, "d_rinv", b, g + 1)
                p = pr[:, g * 400:(g + 1) * 400].rearrange("p (h k) -> p h k", h=4)
                r = rinv[:, 4 * g:4 * g + 4].unsqueeze(2).broadcast_to([S, 4, S])
                pool.tensor_tensor(p, p, r, ALU.mult).then_inc(sig["g_p"], 1)

            def q_normed(b, par):
                wait(pool, "d_rstd2", b, 1)
                wait(pool, "d_qst", b - 1, 1)
                wait(pool, "a_qst", b - 1, 1)
                r = xrstd[par][0:S, 96:128].unsqueeze(2).broadcast_to([S, XH, XD])
                pool.tensor_tensor(qn.rearrange("p (h d) -> p h d", h=XH),
                                   raw[par][0:S, 3].rearrange("p (h d) -> p h d", h=XH), r,
                                   ALU.mult).then_inc(sig["g_qn"], 1)

            def k_normed(b, m, par):
                wait(pool, "d_rstd2", b, 1)
                bb, mm = later(b, m, -2)
                wait(pool, "a_kst", bb, mm + 1)
                wait(pool, "d_kst", bb, mm + 1)
                for c in range(NC):
                    r = xrstd[par][:, c * XH + m * GH:c * XH + (m + 1) * GH].unsqueeze(2).broadcast_to([KC, GH, XD])
                    ins = pool.tensor_tensor(kn[m % 2][:, c * GH:(c + 1) * GH, :],
                                             raw[par][:, c, m * GH * XD:(m + 1) * GH * XD]
                                             .rearrange("p (h d) -> p h d", h=GH), r, ALU.mult)
                ins.then_inc(sig["g_kn"], 1)

            def e_low(b, m):
                wait(pool, "d_eh", b, m + 1)
                bb, mm = later(b, m, -2)
                wait(pool, "pe_pv", bb, mm + 1)
                pool.tensor_tensor(el[m % 2], eb[m % 2], eh[m % 2], ALU.subtract)\
                    .then_inc(sig["g_el"], 1)

            for j in range(5):
                w_of(0, j)
            for j in range(5):
                z_of(0, j)

            def turn(b, last=False):
                for what, j in (("w", 0), ("w", 1), ("p", 0), ("w", 2), ("p", 1), ("p", 2), ("w", 3), ("p", 3), ("w", 4)):
                    if what == "p":
                        p_of(b, j)
                    elif not last:
                        w_of(b + 1, j)
                if not last:
                    for j in range(5):
                        z_of(b + 1, j)

            with pool.Fori(0, NB - 1) as b:
                turn(b)
            wait(pool, "pe_qkv", NB - 1, 6)
            pool.memset(ctxs[:, :, CTX:CTXP], 0.0).then_inc(g_zero, 1)
            for p in range(2):
                pool.memset(qbd[p], 0.0).then_inc(g_zero, 1)
            turn(NB - 1, last=True)

            def ones(par):
                one = cst[0:KC, C_ONE:C_ONE + NC].unsqueeze(2).broadcast_to([KC, NC, XH])
                pool.tensor_copy(vst[par].rearrange("p c (h v) -> p c h v", h=XH)[:, :, :, 2 * XD], one)\
                    .then_inc(g_ones, 1)

            pool.wait_ge(a_whi, 13)
            pool.wait_ge(d_wlo, 13)
            ones(0)

            q_normed(0, 0)
            for m in range(4):
                k_normed(0, m, 0)
            wait(pool, "pe_o", NB - 1, 1)
            ones(1)
            e_low(0, 0)

            def turn(b, par, end):
                for m in range(NG):
                    bb, mm = later(b, m, 4)
                    if mm > 3 or end < 2:
                        k_normed(bb, mm, par if mm > 3 else 1 - par)
                    if m == 4 and end < 2:
                        q_normed(b + 1, 1 - par)
                    bb, mm = later(b, m, 1)
                    if mm > 0 or end < 2:
                        e_low(bb, mm)
                    if m == 0 and end == 2:
                        pool.wait_ge(d_fsc, 1)
                        pool.partition_all_reduce(fsc[:, 3:6], fsc[:, 0:3], 128, bass.bass_isa.ReduceOp.add)\
                            .then_inc(g_sum, 1)

            two_ways(pool, turn)

            wait(pool, "d_x2out", NB - 1, 1)
            for n in range(3, 12):
                src, loaded, count = fstaged(n)
                pool.wait_ge(loaded, count)
                pool.wait_ge(d_tern, 3 if n < 5 else n - 1)
                pool.tensor_scalar(wgt[n % 2], src.rearrange("p k n -> p (k n)"),
                                   fsc[:, 9 + n % 3:10 + n % 3], None, ALU.is_gt).then_inc(g_gt, 1)

        @block.scalar
        def _(act):
            credit(act, "a")

            def w_hi(j):
                src, loaded, n = staged(j)
                if j < 5:
                    act.wait_ge(g_wcen, j + 1)
                else:
                    act.wait_ge(loaded, n)
                if 6 <= j < 10:
                    act.wait_ge(d_wlo, j - 3)
                dst = wqh[:, j] if j < 6 else wohl[:, j - 6, 0] if j < 10 else wxh[:, j - 10]
                act.activation(dst, src, ACT.Copy, scale=SW).then_inc(a_whi, 1)

            def x_hi(b):
                wait(act, "pe_xT", b, 1)
                wait(act, "pe_qkv", b - 1, 6)
                act.activation(xh[:], A[1][:, 0:KT * S].rearrange("p (k s) -> p k s", k=KT), ACT.Copy)\
                   .then_inc(sig["a_xhi"], 1)

            def square(b, j):
                wait(act, "pe_qkv", b, j + 1)
                if j >= 2:
                    wait(act, "d_ssq", b, j - 1)
                else:
                    wait(act, "d_ssq", b - 1, 4 + j)
                act.activation(sq[:, j % 2], A[j % 2][0:S, :], ACT.Square).then_inc(sig["a_sq"], 1)

            def v_of(b):
                wait(act, "pe_qkv", b, 6)
                wait(act, "pe_av", b - 1, 4)
                act.activation(vv[:], A[1][0:S, :], ACT.Copy, scale=1.0 / (SX * SW)).then_inc(sig["a_v"], 1)

            def exps(b, g):
                wait(act, "d_negm", b, g + 1)
                if g == 0:
                    wait(act, "pe_pT", b - 1, 4)
                    wait(act, "d_rinv", b - 1, 4)
                for h in range(4):
                    n = 4 * g + h
                    act.activation(pr[:, n * S:(n + 1) * S], C[g][0:S, h * S:(h + 1) * S], ACT.Exp,
                                   bias=negm[:, n:n + 1], scale=float(D) ** -0.5,
                                   accum_out=rsum[:, n:n + 1]).then_inc(sig["a_exp"], 1)

            def p_back(b, g):
                wait(act, "pe_pT", b, g + 1)
                wait(act, "pe_av", b - 1, g + 1)
                act.activation(pT[:, g * 400:(g + 1) * 400], B[g % 2][0:S, 0:400], ACT.Copy)\
                   .then_inc(sig["a_pT"], 1)

            def a_hi(b, g):
                wait(act, "pe_av", b, g + 1)
                wait(act, "pe_o", b - 1, 1)
                act.activation(ah[:, 4 * g:4 * g + 4, :], C[g][:, 0:400].rearrange("p (h s) -> p h s", h=4),
                               ACT.Copy, scale=SA).then_inc(sig["a_ahi"], 1)

            def ctx_hi(b, lo=0, hi=KT):
                act.wait_ge(ld_ctx, (b + 1) * 16)
                wait(act, "pe_proj", b - 1, 7)
                ins = act.activation(ch[:, lo:hi], ctxs[:, lo:hi], ACT.Copy, scale=SX)
                if hi == KT:
                    ins.then_inc(sig["a_ctx"], 1)

            def x2_hi(b):
                wait(act, "pe_xT2", b, 1)
                wait(act, "pe_proj", b - 1, 1)
                act.activation(xh[:], A[0][:, 0:KT * S].rearrange("p (k s) -> p k s", k=KT), ACT.Copy)\
                   .then_inc(sig["a_x2"], 1)

            def keep_raw(b, n, par):
                wait(act, "pe_proj", b, n + 1)
                rows, slot = (S, 3) if n == 0 else (KC, n - 1)
                if n == 0:
                    wait(act, "g_kn", b - 2, 8)
                    wait(act, "g_qn", b - 2, 1)
                act.activation(raw[par][0:rows, slot], A[(n + 1) % 2][0:rows, :], ACT.Copy)
                if n >= 2:
                    wait(act, "d_ssq2", b, n - 1)
                else:
                    wait(act, "d_ssq2", b - 1, n + 3)
                act.activation(xsq[0:rows, n % 2], A[(n + 1) % 2][0:rows, :], ACT.Square).then_inc(sig["a_sq2"], 1)

            def v2_hi(b, c, par):
                wait(act, "pe_proj", b, 5 + c)
                if c == 0:
                    wait(act, "pe_pv", b - 2, 8)
                act.activation(vst[par][:, c].rearrange("p (h v) -> p h v", h=XH)[:, :, 0:XD],
                               A[(c + 1) % 2][0:KC, :].rearrange("p (h d) -> p h d", h=XH), ACT.Copy, scale=SV)\
                   .then_inc(sig["a_v2"], 1)

            def q_stack(b, par):
                wait(act, "g_qn", b, 1)
                wait(act, "pe_T", b - 2, 8)
                act.activation(qst[par].rearrange("p h (u w) d -> p h u w d", u=2)[:, :, :, 0, :],
                               qn.rearrange("p (h d) -> p h d", h=XH).unsqueeze(2).broadcast_to([S, XH, 2, XD]),
                               ACT.Copy).then_inc(sig["a_qst"], 1)

            def k_stack(b, m):
                wait(act, "g_kn", b, m + 1)
                bb, mm = later(b, m, -2)
                wait(act, "pe_T", bb, mm + 1)
                act.activation(kst[m % 2].rearrange("p c (h u d) -> p (c h) u d", h=GH, u=4)[:, :, 0:2, :],
                               kn[m % 2].unsqueeze(2).broadcast_to([KC, NC * GH, 2, XD]), ACT.Copy)\
                   .then_inc(sig["a_kst"], 1)

            def exp2(b, m):
                for c in range(NC):
                    wait(act, "pe_sc", b, m * NC + c + 1)
                    if c == 0:
                        bb, mm = later(b, m, -2)
                        wait(act, "g_el", bb, mm + 1)
                    act.activation(eb[m % 2][:, c], C[(m * NC + c) % 4][0:KC, 0:GH * S], ACT.Exp,
                                   scale=float(XD) ** -0.5 / SN ** 2).then_inc(sig["a_e"], 1)

            def keys_back(b, m):
                wait(act, "d_T", b, m + 1)
                bb, mm = later(b, m, -2)
                wait(act, "pe_sc", bb, mm * NC + NC)
                keys = B[0][:, :].bitcast(F16)[:, 0:2 * NC * KC].rearrange("p (n k) -> p n k", n=2 * NC)
                act.activation(kT[m % 2], keys, ACT.Copy).then_inc(sig["a_T"], 1)

            def magnitudes(b, w, par):
                if w == 0:
                    act.wait_ge(ld_f[par], (b - par) * 8 + 16)
                act.activation(stage[:, par, w], stage[:, par, w], ACT.Abs, accum_out=asum[:, w, b, :])\
                   .then_inc(sig["a_abs"], 1)

            def x3_hi(u, r, bank):
                wait(act, "pe_xT3", u, r + 1)
                wait(act, "pe_up", u - 1, 16)
                act.activation(fh[:, :, r * S:(r + 1) * S], bank[:, 0:KT * S].rearrange("p (k s) -> p k s", k=KT),
                               ACT.Copy).then_inc(sig["a_x3"], 1)

            def out_back(b, n):
                wait(act, "pe_pv", b, 2 * n + 2)
                if n == 0:
                    wait(act, "d_x2out", b - 1, 1)
                act.activation(ob[:, 8 * n:8 * n + 8, :], B[1][0:S, 0:8 * VW].rearrange("p (h v) -> p h v", h=8),
                               ACT.Copy).then_inc(sig["a_ob"], 1)

            x_hi(0)
            for j in range(3):
                w_hi(j)
            for j in range(5):
                square(0, j)
                w_hi(j + 3)
            v_of(0)
            x_hi(1)
            for j in range(8, 10):
                w_hi(j)

            def turn(b, last=False):
                for g in range(4):
                    exps(b, g)
                    square(b + 1, g)
                p_back(b, 0)
                square(b + 1, 4)
                for g in range(1, 4):
                    p_back(b, g)
                for g in range(4):
                    a_hi(b, g)
                v_of(b + 1)
                if not last:
                    x_hi(b + 2)

            with act.Fori(0, NB - 2) as b:
                turn(b)
            turn(NB - 2, last=True)
            b = NB - 1
            for j in range(10, 13):
                w_hi(j)
            exps(b, 0)
            act.wait_ge(g_zero, 1)
            ctx_hi(0)
            exps(b, 1)
            x2_hi(0)
            exps(b, 2)
            exps(b, 3)
            wait(act, "pe_zT", b, 5)
            keep_raw(0, 0, 0)
            p_back(b, 0)
            p_back(b, 1)
            keep_raw(0, 1, 0)
            p_back(b, 2)
            p_back(b, 3)
            keep_raw(0, 2, 0)
            for g in range(4):
                a_hi(b, g)
            keep_raw(0, 3, 0)
            for c in range(NC):
                v2_hi(0, c, 0)

            ctx_hi(1)
            q_stack(0, 0)
            k_stack(0, 0)
            k_stack(0, 1)
            keys_back(0, 0)
            k_stack(0, 2)
            keys_back(0, 1)
            x2_hi(1)
            wait(act, "pe_o", NB - 1, 1)
            exp2(0, 0)
            keep_raw(1, 0, 1)

            def turn(b, par, end):
                for m in range(NG):
                    if m in (2, 4, 6):
                        out_back(b, m // 2 - 1)
                    bb, mm = later(b, m, 1)
                    if mm > 0 or end < 2:
                        exp2(bb, mm)
                    bb, mm = later(b, m, 2)
                    if mm > 1 or end < 2:
                        keys_back(bb, mm)
                    bb, mm = later(b, m, 3)
                    if mm > 2 or end < 2:
                        k_stack(bb, mm)
                    if end < 2 and m < 3:
                        keep_raw(b + 1, m + 1, 1 - par)
                    elif end < 2 and m < 6:
                        v2_hi(b + 1, m - 3, 1 - par)
                    elif end < 1 and m == 6:
                        x2_hi(b + 2)
                        ctx_hi(b + 2, 0, 2)
                    elif end < 1 and m == 7:
                        ctx_hi(b + 2, 2)
                        keep_raw(b + 2, 0, par)
                    if m == 4 and end < 2:
                        q_stack(b + 1, 1 - par)
                    if end < 2 and 3 <= m < 6:
                        magnitudes(b, m - 3, par)
                    elif end == 1 and m == 6:
                        for w in range(3):
                            magnitudes(b + 1, w, 1 - par)
                    if end == 2 and m == 0:
                        wait(act, "g_kn", b - 1, 8)
                    if end == 2 and m < UB:
                        x3_hi(0, m, A[m % 2])
                out_back(b, 3)

            two_ways(act, turn)

            def silu(u, e):
                wait(act, "pe_up", u, e + 1)
                if e >= 2:
                    wait(act, "d_hd", u, e - 1)
                else:
                    wait(act, "d_hd", u - 1, 15 + e)
                act.activation(sg[e % 2], C[2 * (e % 2)][:, 0:UB * S], ACT.Silu, scale=fsc[:, 6:7])\
                   .then_inc(sig["a_sg"], 1)

            def hidden_hi(u, e):
                wait(act, "d_hd", u, e + 1)
                if e >= 2:
                    wait(act, "pe_dn", u, e - 1)
                else:
                    wait(act, "pe_dn", u - 1, 15 + e)
                act.activation(hh[e % 2], hd[e % 2], ACT.Copy).then_inc(sig["a_hh"], 1)

            def unit(u, last=False):
                silu(u, 0)
                for e in range(ET):
                    hidden_hi(u, e)
                    if e + 1 < ET:
                        silu(u, e + 1)
                    if e == ET - 2 and not last:
                        x3_hi(u + 1, 0, C[0])
                        x3_hi(u + 1, 1, C[1])
                if not last:
                    x3_hi(u + 1, 2, C[0])
                    x3_hi(u + 1, 3, C[1])
                wait(act, "pe_dn", u, 16)
                wait(act, "pe_yT", u - 1, 4)
                for k in range(2):
                    ins = act.activation(yT[:, k], A[k][:, 0:UB * S], ACT.Copy)
                ins.then_inc(sig["a_y"], 1)

            wait(act, "pe_pv", NB - 1, 8)
            unit(0)
            with act.Fori(0, NB // UB - 2) as i:
                unit(i + 1)
            unit(NB // UB - 1, last=True)

        @block.vector
        def _(dve):
            credit(dve, "d")
            st = Steps(dve, d_step)

            def rsqrt(y, v, n, p=S):
                a, c = nwt[0:p, 0, 0:n], nwt[0:p, 1, 0:n]
                st.chain(dve.tensor_scalar(y.bitcast(I32), v.bitcast(I32), 1, None, ALU.logical_shift_right))
                st.chain(dve.tensor_scalar(y.bitcast(I32), y.bitcast(I32), -1, 0x5f3759df, ALU.mult, ALU.add))
                for step in range(3):
                    st.chain(dve.scalar_tensor_tensor(a, y, -0.5, y, ALU.mult, ALU.mult))
                    st.chain(dve.tensor_tensor(c, a, v, ALU.mult))
                    ins = dve.scalar_tensor_tensor(y, c, 1.5, y, ALU.add, ALU.mult)
                    if step < 2:
                        st.chain(ins)
                return ins

            def row_stats(b, var):
                st.chain(dve.bn_stats(stats[:], xres[:, b, :]))
                st.did(dve.tensor_copy(statc[:], stats[:]))
                st.chain(dve.bn_aggr(mv[:], stats[:]))
                st.did(dve.tensor_scalar(var, mv[:, 1:2], EPS_LN, SX ** -2, ALU.add, ALU.mult))

            def normed(b, rs):
                wait(dve, "pe_xT", b - 1, 1)
                dve.tensor_scalar(xn[:], xres[:, b, :], mv[:, 0:1], rs, ALU.subtract, ALU.mult)\
                   .then_inc(sig["d_xn"], 1)

            def x_lo(b):
                wait(dve, "a_xhi", b, 1)
                wait(dve, "pe_qkv", b - 1, 6)
                dve.tensor_tensor(xl[:], A[1][:, 0:KT * S].rearrange("p (k s) -> p k s", k=KT), xh[:],
                                  ALU.subtract).then_inc(sig["d_xlo"], 1)

            def proj(b, j):
                wait(dve, "pe_qkv", b, j + 1)
                wait(dve, "a_sq", b, j + 1)
                if j >= 2:
                    wait(dve, "g_w", b, j - 1)
                else:
                    wait(dve, "g_w", b - 1, 4 + j)
                which = 0 if j == 0 else 1
                bank = A[j % 2][0:S, :].rearrange("p (h d) -> p h d", h=4)
                t = tb[:, j % 2].rearrange("p (h d) -> p h d", h=4)
                u = ub[:, j % 2].rearrange("p (h d) -> p h d", h=4)

                def table(tab, lo, hi):
                    return tab[:, which, lo:hi].unsqueeze(1).broadcast_to([S, 4, hi - lo])

                dve.tensor_tensor(t, bank, table(ropeA, 0, D), ALU.mult).then_inc(sig["d_t"], 1)
                st.did(dve.tensor_tensor(u[:, :, 0:HALF], bank[:, :, HALF:D], table(ropeB, 0, HALF), ALU.mult))
                dve.tensor_tensor(u[:, :, HALF:D], bank[:, :, 0:HALF], table(ropeB, HALF, D), ALU.mult)\
                   .then_inc(sig["d_u"], 1)
                if j == 0:
                    wait(dve, "d_rstd", b - 1, 1)
                dve.tensor_reduce(ssq[:, 4 * j:4 * j + 4], sq[:, j % 2].rearrange("p (h d) -> p h d", h=4),
                                  AX.X, ALU.add).then_inc(sig["d_ssq"], 1)

            def head_norm(b):
                wait(dve, "d_ssq", b, 5)
                st.chain(dve.tensor_scalar(ssq[:, 0:20], ssq[:, 0:20], 1.0 / D, EPS_LN * (SX * SW) ** 2,
                                           ALU.mult, ALU.add))
                wait(dve, "g_z", b - 1, 5)
                rsqrt(rstd[:], ssq[:], 21).then_inc(sig["d_rstd"], 1)
                wait(dve, "d_rstd", b, 1)

            def z_back(b, g):
                wait(dve, "pe_zT", b, g + 1)
                if g == 0:
                    wait(dve, "pe_s", b - 1, 4)
                c = ropeC[:, 0 if g == 0 else 1, :].unsqueeze(1).broadcast_to([128, 4, S])
                dve.tensor_tensor(qk[:, g], B[g % 2][:, 0:400].rearrange("p (h s) -> p h s", h=4), c,
                                  ALU.add).then_inc(sig["d_zT"], 1)

            def row_max(b, pair):
                bank = [c[0:S, 0:400].rearrange("p (h k) -> p h k", h=4) for c in C]
                for g in pair:
                    wait(dve, "pe_s", b, g + 1)
                    mask = cst[0:S, C_MASK:C_MASK + S].unsqueeze(1).broadcast_to([S, REP, S])
                    st.did(dve.tensor_tensor(bank[g], bank[g], mask, ALU.add))
                if pair[0] == 0:
                    wait(dve, "a_exp", b - 1, 16)
                for g in pair:
                    st.wait(back=1)
                    st.did(dve.tensor_reduce(smax[:, 4 * g:4 * g + 4], bank[g], AX.X, ALU.max))
                for g in pair:
                    st.wait(back=pair[1] - g)
                    dve.tensor_scalar(negm[:, 4 * g:4 * g + 4], smax[:, 4 * g:4 * g + 4], -float(D) ** -0.5, None,
                                      ALU.mult).then_inc(sig["d_negm"], 1)

            def sums(b, g):
                wait(dve, "a_exp", b, 4 * g + 4)
                if g == 0:
                    wait(dve, "g_p", b - 1, 4)
                dve.reciprocal(rinv[:, 4 * g:4 * g + 4], rsum[:, 4 * g:4 * g + 4]).then_inc(sig["d_rinv"], 1)

            def a_lo(b, g):
                wait(dve, "a_ahi", b, g + 1)
                dve.scalar_tensor_tensor(al[:, 4 * g:4 * g + 4, :],
                                         C[g][:, 0:400].rearrange("p (h s) -> p h s", h=4), SA,
                                         ah[:, 4 * g:4 * g + 4, :], ALU.mult, ALU.subtract)\
                   .then_inc(sig["d_alo"], 1)

            def add_attn(b):
                wait(dve, "pe_o", b, 1)
                dve.scalar_tensor_tensor(xres[:, b, :], A[0][0:S, :], 1.0 / (SA * SW), xres[:, b, :],
                                         ALU.mult, ALU.add).then_inc(sig["d_x1"], 1)

            def ctx_lo(b):
                wait(dve, "a_ctx", b, 1)
                wait(dve, "pe_proj", b - 1, 7)
                dve.scalar_tensor_tensor(cl.rearrange("p k n -> p (k n)"), ctxs.rearrange("p k n -> p (k n)"), SX,
                                         ch.rearrange("p k n -> p (k n)"), ALU.mult, ALU.subtract)\
                   .then_inc(sig["d_ctx"], 1)

            def row_stats2(b):
                st.chain(dve.bn_stats(stats[:], xres[:, b, :]))
                st.did(dve.tensor_copy(statc[:], stats[:]))
                st.chain(dve.bn_aggr(mv[:], stats[:]))
                st.did(dve.tensor_scalar(xssq[0:S, 128:129], mv[:, 1:2], EPS_LN, SX ** -2, ALU.add, ALU.mult))

            def normed2(b, rs):
                wait(dve, "pe_xT2", b - 1, 1)
                dve.tensor_scalar(xn[:], xres[:, b, :], mv[:, 0:1], rs, ALU.subtract, ALU.mult)\
                   .then_inc(sig["d_xn2"], 1)

            def x2_lo(b):
                wait(dve, "a_x2", b, 1)
                wait(dve, "pe_proj", b - 1, 1)
                dve.tensor_tensor(xl[:], A[0][:, 0:KT * S].rearrange("p (k s) -> p k s", k=KT), xh[:],
                                  ALU.subtract).then_inc(sig["d_x2"], 1)

            def square_sums(b, n):
                wait(dve, "a_sq2", b, n + 1)
                rows, slot = (S, 3) if n == 0 else (KC, n - 1)
                if n == 0:
                    wait(dve, "d_rstd2", b - 1, 1)
                dve.tensor_reduce(xssq[0:rows, slot * XH:(slot + 1) * XH],
                                  xsq[0:rows, n % 2].rearrange("p (h d) -> p h d", h=XH), AX.X, ALU.add)\
                   .then_inc(sig["d_ssq2"], 1)

            def rms_start(b, par):
                wait(dve, "d_ssq2", b, 4)
                wait(dve, "g_kn", b - 2, 8)
                wait(dve, "g_qn", b - 2, 1)
                wait(dve, "d_xn2", b, 1)
                st.chain(dve.tensor_scalar(xssq[:, 0:128], xssq[:, 0:128], SN ** -2 / XD,
                                           EPS_RMS * (SX * SW / SN) ** 2, ALU.mult, ALU.add))
                y = xrstd[par].bitcast(I32)
                st.chain(dve.tensor_scalar(y, xssq.bitcast(I32), 1, None, ALU.logical_shift_right))
                st.did(dve.tensor_scalar(y, y, -1, 0x5f3759df, ALU.mult, ALU.add))

            def rms_step(par, last=False):
                y = xrstd[par]
                a, c = xnw[:, 0, :], xnw[:, 1, :]
                st.wait()
                st.chain(dve.scalar_tensor_tensor(a, y, -0.5, y, ALU.mult, ALU.mult))
                st.chain(dve.tensor_tensor(c, a, xssq, ALU.mult))
                ins = dve.scalar_tensor_tensor(y, c, 1.5, y, ALU.add, ALU.mult)
                if last:
                    ins.then_inc(sig["d_rstd2"], 1)
                else:
                    st.did(ins)

            def v2_lo(b, c, par):
                wait(dve, "a_v2", b, c + 1)
                v = vst[par][:, c].rearrange("p (h v) -> p h v", h=XH)
                dve.scalar_tensor_tensor(v[:, :, XD:2 * XD], A[(c + 1) % 2][0:KC, :].rearrange("p (h d) -> p h d", h=XH), SV,
                                         v[:, :, 0:XD], ALU.mult, ALU.subtract).then_inc(sig["d_v2"], 1)

            def q_stack_lo(b, par):
                wait(dve, "a_qst", b, 1)
                q = qst[par].rearrange("p h (u w) d -> p h u w d", u=2)
                dve.tensor_tensor(q[:, :, :, 1, :],
                                  qn.rearrange("p (h d) -> p h d", h=XH).unsqueeze(2).broadcast_to([S, XH, 2, XD]),
                                  q[:, :, :, 0, :], ALU.subtract).then_inc(sig["d_qst"], 1)

            def k_stack_lo(b, m):
                wait(dve, "a_kst", b, m + 1)
                k = kst[m % 2].rearrange("p c (h u d) -> p (c h) u d", h=GH, u=4)
                dve.tensor_tensor(k[:, :, 2:4, :], kn[m % 2].unsqueeze(2).broadcast_to([KC, NC * GH, 2, XD]),
                                  k[:, :, 0:2, :], ALU.subtract).then_inc(sig["d_kst"], 1)

            def queries_back(b, m):
                wait(dve, "pe_T", b, m + 1)
                bb, mm = later(b, m, -2)
                wait(dve, "pe_sc", bb, mm * NC + NC)
                q = B[0][:, :].bitcast(F16)[:, 2 * NC * KC:2 * NC * KC + 2 * S].rearrange("p (n s) -> p n s", n=2)
                st.did(dve.tensor_copy(qbd[m % 2][0:64, :, 0:S], q[0:64]))
                dve.tensor_copy(qbd[m % 2][64:128, :, S:2 * S], q[64:128]).then_inc(sig["d_T"], 1)

            def e_high(b, m):
                wait(dve, "a_e", b, NC * (m + 1))
                bb, mm = later(b, m, -2)
                wait(dve, "pe_pv", bb, mm + 1)
                dve.tensor_copy(eh[m % 2], eb[m % 2]).then_inc(sig["d_eh"], 1)

            def scales3():
                dve.wait_ge(g_sum, 1)
                st.chain(dve.tensor_scalar(fsc[:, 3:6], fsc[:, 3:6], 1.0 / (FE * DM), 1e-8, ALU.mult, ALU.add))
                st.did(dve.tensor_scalar(fsc[:, 9:12], fsc[:, 3:6], 0.5, None, ALU.mult))
                st.did(dve.tensor_scalar(fsc[:, 12:15], fsc[:, 3:6], -0.5, None, ALU.mult))
                st.did(dve.tensor_scalar(fsc[:, 6:7], fsc[:, 3:4], -1.0 / SX, None, ALU.mult))
                st.chain(dve.reciprocal(fsc[:, 7:8], fsc[:, 3:4]))
                st.did(dve.tensor_scalar(fsc[:, 7:8], fsc[:, 7:8], 1.0 / (SX * SH), None, ALU.mult))
                st.chain(dve.tensor_tensor(fsc[:, 8:9], fsc[:, 3:4], fsc[:, 4:5], ALU.mult))
                st.chain(dve.scalar_tensor_tensor(fsc[:, 8:9], fsc[:, 8:9], SH, fsc[:, 5:6], ALU.mult, ALU.mult))

            def ternary(n):
                src, loaded, count = fstaged(n)
                dve.wait_ge(loaded, count)
                w = src.rearrange("p k n -> p (k n)")
                if n < 3:
                    if n > 0:
                        dve.wait_ge(d_tern, n)
                    st.chain(dve.tensor_scalar(wgt[0], w, fsc[:, 9 + n % 3:10 + n % 3], None, ALU.is_gt))
                else:
                    dve.wait_ge(g_gt, n - 2)
                dve.scalar_tensor_tensor(wf[:, n].rearrange("p k n -> p (k n)"), w, fsc[:, 12 + n % 3:13 + n % 3],
                                         wgt[0 if n < 3 else n % 2], ALU.is_lt, ALU.subtract).then_inc(d_tern, 1)

            def row_stats3(u, rows):
                for r in rows:
                    st.did(dve.bn_stats(stats3[:, r], xres[:, u * UB + r, :]))

            def row_scales3():
                st.wait()
                st.did(dve.tensor_copy(statc3[:], stats3[:]))
                for r in range(UB):
                    st.did(dve.bn_aggr(mv3[:, r], stats3[:, r]))
                st.wait()
                st.chain(dve.tensor_scalar(ms3[:], mv3[:, :, 1], EPS_LN, SX ** -2, ALU.add, ALU.mult))
                st.chain(rsqrt(rs3[:], ms3[:], UB))

            def normed3(u, r):
                wait(dve, "pe_xT3", u - 1, 4)
                dve.tensor_scalar(xn3[r], xres[:, u * UB + r, :], mv3[:, r, 0:1], rs3[:, r:r + 1],
                                  ALU.subtract, ALU.mult).then_inc(sig["d_xn3"], 1)

            def x3_lo(u, r, bank):
                wait(dve, "a_x3", u, r + 1)
                wait(dve, "pe_up", u - 1, 16)
                dve.tensor_tensor(fl[:, :, r * S:(r + 1) * S],
                                  bank[:, 0:KT * S].rearrange("p (k s) -> p k s", k=KT),
                                  fh[:, :, r * S:(r + 1) * S], ALU.subtract).then_inc(sig["d_x3"], 1)

            def add_cross(b):
                wait(dve, "a_ob", b, 4)
                st.did(dve.reciprocal(oinv, ob[:, :, 2 * XD]))
                st.chain(dve.tensor_tensor(osum.rearrange("p (h d) -> p h d", h=XH), ob[:, :, 0:XD],
                                           ob[:, :, XD:2 * XD], ALU.add))
                o = osum.rearrange("p (h d) -> p h d", h=XH)
                st.chain(dve.tensor_tensor(o, o, oinv.unsqueeze(2).broadcast_to([S, XH, XD]), ALU.mult))
                dve.scalar_tensor_tensor(xres[:, b, :], osum, 1.0 / (SX * SW * SV), xres[:, b, :],
                                         ALU.mult, ALU.add).then_inc(sig["d_x2out"], 1)

            dve.wait_ge(ld_x0, 16)
            row_stats(0, ms1[:])
            st.wait()
            st.chain(rsqrt(rs1[:], ms1[:], 1))
            normed(0, rs1[:, 0:1])
            dve.wait_ge(ld_c, 48)
            for w, g in ((0, 2), (1, 0)):
                dve.tensor_tensor(ropeA[:, w], gain[:, g * D:(g + 1) * D], cst[0:S, C_COS:C_COS + D],
                                  ALU.mult).then_inc(d_tab, 1)
                dve.tensor_tensor(ropeB[:, w], gain[:, (g + 1) * D:(g + 2) * D], cst[0:S, C_SIN:C_SIN + D],
                                  ALU.mult).then_inc(d_tab, 1)
                st.chain(dve.tensor_scalar(ropeC[:, w], cst[:, C_COST:C_COST + S], bcol[:, g:g + 1], None, ALU.mult))
                dve.scalar_tensor_tensor(ropeC[:, w], cst[:, C_SINT:C_SINT + S], bcol[:, g + 1:g + 2],
                                         ropeC[:, w], ALU.mult, ALU.add).then_inc(d_tab, 1)
            dve.wait_ge(d_tab, 6)

            def w_mean(j):
                src, loaded, n = staged(j)
                dve.wait_ge(loaded, n)
                st.chain(dve.tensor_reduce(wmean[:, j], src.rearrange("p k (h d) -> p (k h) d", h=4),
                                           AX.X, ALU.add))
                dve.tensor_scalar(wmean[:, j], wmean[:, j], 1.0 / D, None, ALU.mult).then_inc(d_wmean, 1)

            def w_lo(j):
                dve.wait_ge(a_whi, j + 1)
                dst, hi = (wql[:, j], wqh[:, j]) if j < 6 else (
                    wohl[:, j - 6, 1], wohl[:, j - 6, 0]) if j < 10 else (
                    wxl[:, j - 10], wxh[:, j - 10])
                dve.scalar_tensor_tensor(dst.rearrange("p k n -> p (k n)"),
                                         staged(j)[0].rearrange("p k n -> p (k n)"), SW,
                                         hi.rearrange("p k n -> p (k n)"), ALU.mult, ALU.subtract)\
                   .then_inc(d_wlo, 1)

            w_mean(0)
            x_lo(0)
            w_mean(1)
            for j in range(2, 5):
                w_mean(j)
                w_lo(j - 2)
            proj(0, 0)
            for j in range(3, 6):
                w_lo(j)
                proj(0, j - 2)
            proj(0, 4)
            dve.wait_ge(ld_x, 16)
            row_stats(1, ssq[:, 20:21])
            head_norm(0)
            normed(1, rstd[:, 20:21])
            w_lo(6)
            x_lo(1)
            w_lo(7)
            for g in range(5):
                z_back(0, g)

            def turn(b, first=False, last=False):
                row_max(b, (0, 1))
                row_max(b, (2, 3))
                if first:
                    w_lo(8)
                for g in range(4):
                    proj(b + 1, g)
                    sums(b, g)
                    if first and g == 1:
                        w_lo(9)
                if last:
                    wait(dve, "d_x1", 0, 1)
                row_stats(0 if last else b + 2, ssq[:, 20:21])
                proj(b + 1, 4)
                head_norm(b + 1)
                if last:
                    wait(dve, "pe_xT", b + 1, 1)
                    normed2(0, rstd[:, 20:21])
                else:
                    normed(b + 2, rstd[:, 20:21])
                for g in range(4):
                    a_lo(b, g)
                for g in range(4):
                    z_back(b + 1, g)
                    if g == 1 and not last:
                        x_lo(b + 2)
                add_attn(b)
                z_back(b + 1, 4)
                if last:
                    w_lo(10)

            turn(0, first=True)
            with dve.Fori(0, NB - 3) as i:
                st.begin(i, 28)
                turn(i + 1)
            st.end(NB - 3)
            turn(NB - 2, last=True)

            b = NB - 1
            row_max(b, (0, 1))
            w_lo(11)
            w_lo(12)
            x2_lo(0)
            row_max(b, (2, 3))
            ctx_lo(0)
            for g in range(4):
                sums(b, g)
            wait(dve, "pe_zT", b, 5)
            st.chain(dve.memset(xssq, 1.0))
            row_stats2(1)
            for n in range(3):
                square_sums(0, n)
            for g in range(4):
                a_lo(b, g)
            square_sums(0, 3)
            rms_start(0, 0)
            for n in range(3):
                rms_step(0, n == 2)
            wait(dve, "d_rstd2", 0, 1)
            normed2(1, xrstd[0][0:S, 128:129])
            for c in range(NC):
                v2_lo(0, c, 0)

            q_stack_lo(0, 0)
            k_stack_lo(0, 0)
            k_stack_lo(0, 1)
            add_attn(b)
            dve.wait_ge(g_zero, 3)
            queries_back(0, 0)
            k_stack_lo(0, 2)
            queries_back(0, 1)
            ctx_lo(1)
            x2_lo(1)
            e_high(0, 0)
            square_sums(1, 0)

            queries_back(0, 2)
            e_high(0, 1)

            def turn(b, par, end):
                for m in range(NG):
                    bb, mm = later(b, m, 3)
                    if mm > 2 or end < 2:
                        k_stack_lo(bb, mm)
                    if m == 3 and end < 2:
                        rms_step(1 - par)
                    if m == 5 and end < 2:
                        q_stack_lo(b + 1, 1 - par)
                    if end < 2 and m < 3:
                        square_sums(b + 1, m + 1)
                        if m == 2:
                            rms_start(b + 1, 1 - par)
                    elif end < 2 and m < 6:
                        v2_lo(b + 1, m - 3, 1 - par)
                        if m == 3:
                            rms_step(1 - par, last=True)
                    elif end < 1 and m == 6:
                        x2_lo(b + 2)
                    elif end < 1 and m == 7:
                        ctx_lo(b + 2)
                        square_sums(b + 2, 0)
                    if end == 1:
                        if m == 5:
                            wait(dve, "d_x2out", UB - 1, 1)
                            row_stats3(0, range(UB))
                        elif m == 6:
                            row_scales3()
                        elif m == 7:
                            for r in range(UB):
                                normed3(0, r)
                    if end == 2:
                        if m == 0:
                            wait(dve, "a_abs", NB - 1, 3)
                            dve.tensor_reduce(fsc[:, 0:3], asum[:, :, :, 0], AX.X, ALU.add).then_inc(d_fsc, 1)
                        elif m == 1:
                            scales3()
                            wait(dve, "pe_proj", b, 7)
                            wait(dve, "pe_pv", b - 1, 8)
                        elif m < 5:
                            ternary(m - 2)
                        if m < UB:
                            x3_lo(0, m, A[m % 2])
                    bb, mm = later(b, m, 3)
                    if mm > 2 or end < 2:
                        queries_back(bb, mm)
                    if m == 2 and end < 2:
                        rms_step(1 - par)
                    bb, mm = later(b, m, 2)
                    if mm > 1 or end < 2:
                        e_high(bb, mm)
                    if end < 1 and m == 0:
                        row_stats2(b + 2)
                    if m == 4 and end < 1:
                        wait(dve, "d_rstd2", b + 1, 1)
                        normed2(b + 2, xrstd[1 - par][0:S, 128:129])
                add_cross(b)

            two_ways(dve, turn, st, 52)

            def hidden(u, e):
                wait(dve, "a_sg", u, e + 1)
                if e >= 2:
                    wait(dve, "a_hh", u, e - 1)
                    wait(dve, "d_hl", u, e - 1)
                else:
                    wait(dve, "a_hh", u - 1, 15 + e)
                    wait(dve, "d_hl", u - 1, 15 + e)
                dve.scalar_tensor_tensor(hd[e % 2], C[2 * (e % 2) + 1][:, 0:UB * S], fsc[:, 7:8], sg[e % 2],
                                         ALU.mult, ALU.mult).then_inc(sig["d_hd"], 1)

            def hidden_lo(u, e):
                wait(dve, "a_hh", u, e + 1)
                if e >= 2:
                    wait(dve, "pe_dn", u, e - 1)
                else:
                    wait(dve, "pe_dn", u - 1, 15 + e)
                dve.tensor_tensor(hl[e % 2], hd[e % 2], hh[e % 2], ALU.subtract).then_inc(sig["d_hl"], 1)

            def add_ffn(u):
                for r in range(UB):
                    wait(dve, "pe_yT", u, r + 1)
                    dve.scalar_tensor_tensor(xres[:, u * UB + r, :], (A + B)[r][0:S, :], fsc[0:S, 8:9],
                                             xres[:, u * UB + r, :], ALU.mult, ALU.add).then_inc(sig["d_y"], 1)

            def unit(u, first=False, last=False):
                hidden(u, 0)
                if not first:
                    add_ffn(u - 1)
                for e in range(ET):
                    hidden_lo(u, e)
                    if e + 1 < ET:
                        hidden(u, e + 1)
                    if first and e in TERNARY_AT:
                        ternary(3 + TERNARY_AT.index(e))
                    if e in (3, 6) and not last:
                        row_stats3(u + 1, (0, 1) if e == 3 else (2, 3))
                    elif e == 10 and not last:
                        row_scales3()
                    elif e in (12, 13) and not last:
                        normed3(u + 1, 2 * (e - 12))
                        normed3(u + 1, 2 * (e - 12) + 1)
                    elif e == ET - 2 and not last:
                        x3_lo(u + 1, 0, C[0])
                        x3_lo(u + 1, 1, C[1])
                if not last:
                    x3_lo(u + 1, 2, C[0])
                    x3_lo(u + 1, 3, C[1])
                wait(dve, "pe_dn", u, 16)
                wait(dve, "pe_yT", u - 1, 4)
                for k in range(2, 4):
                    ins = dve.tensor_copy(yT[:, k], B[k - 2][:, 0:UB * S])
                ins.then_inc(sig["d_yc"], 1)

            wait(dve, "pe_pv", NB - 1, 8)
            wait(dve, "d_x2out", NB - 1, 1)
            unit(0, first=True)
            with dve.Fori(0, NB // UB - 2) as i:
                st.begin(i, 21)
                unit(i + 1)
            st.end(NB // UB - 2)
            unit(NB // UB - 1, last=True)
            add_ffn(NB // UB - 1)

        @block.tensor
        def _(pe):
            credit(pe, "p")
            ident = cst[0:128, C_ID:C_ID + 128]

            def x_turn(b):
                wait(pe, "d_xn", b, 1)
                wait(pe, "a_v", b - 1, 1)
                for k in range(KT):
                    ins = pe.transpose(A[1][:, k * S:(k + 1) * S], xn[:, k * 128:(k + 1) * 128], ident[0:S, 0:S])
                ins.then_inc(sig["pe_xT"], 1)

            def project(b, j):
                if j == 0:
                    wait(pe, "a_xhi", b, 1)
                    wait(pe, "d_xlo", b, 1)
                    wait(pe, "d_x1", b - 2, 1)
                elif j >= 2:
                    wait(pe, "a_sq", b, j - 1)
                    wait(pe, "d_t", b, j - 1)
                    wait(pe, "d_u", b, j - 1)
                n = 0
                for xp, wp in ((xh, wqh), (xh, wql), (xl, wqh)):
                    for k in range(KT):
                        ins = pe.matmul(A[j % 2][0:S, :], xp[:, k, :], wp[:, j, k, :], start=(n == 0), stop=(n == 11))
                        n += 1
                ins.then_inc(sig["pe_qkv"], 1)

            def z_turn(b, g):
                wait(pe, "g_z", b, g + 1)
                if g < 2:
                    wait(pe, "a_pT", b - 1, 3 + g)
                else:
                    wait(pe, "d_zT", b, g - 1)
                for h in range(4):
                    ins = pe.transpose(B[g % 2][:, h * S:(h + 1) * S], zb[:, g, h * D:(h + 1) * D], ident[0:S, 0:S])
                ins.then_inc(sig["pe_zT"], 1)

            def scores(b, g):
                wait(pe, "d_zT", b, g + 2)
                wait(pe, "d_alo", b - 1, g + 1)
                bank = C[g][0:S, 0:400]
                for h in range(4):
                    ins = pe.matmul(bank[:, h * S:(h + 1) * S], qk[:, g + 1, h, :], qk[:, 0, g, :],
                                    start=True, stop=True)
                ins.then_inc(sig["pe_s"], 1)

            def p_turn(b, g):
                wait(pe, "g_p", b, g + 1)
                if g == 0:
                    wait(pe, "d_zT", b, 5)
                elif g >= 2:
                    wait(pe, "a_pT", b, g - 1)
                for h in range(4):
                    n = 4 * g + h
                    ins = pe.transpose(B[g % 2][0:S, h * S:(h + 1) * S], pr[:, n * S:(n + 1) * S], ident[0:S, 0:S])
                ins.then_inc(sig["pe_pT"], 1)

            def attend(b, g):
                wait(pe, "a_pT", b, g + 1)
                if g == 0:
                    wait(pe, "a_v", b, 1)
                pe.matmul(C[g][:, 0:400], vv[:, g * D:(g + 1) * D], pT[:, g * 400:(g + 1) * 400],
                          start=True, stop=True).then_inc(sig["pe_av"], 1)

            def project_out(b, between=None):
                n = 0
                pe.wait_ge(a_whi, 10)
                pe.wait_ge(d_wlo, 10)
                for g in range(4):
                    if between and g > 0:
                        between(g - 1)
                    wait(pe, "a_ahi", b, g + 1)
                    wait(pe, "d_alo", b, g + 1)
                    for h in range(4 * g, 4 * g + 4):
                        for ap, part in ((ah, 0), (ah, 1), (al, 0)):
                            ins = pe.matmul(A[0][0:S, :], ap[:, h, :], wohl[:, g, part, h % 4, :], start=(n == 0), stop=(n == 47))
                            n += 1
                ins.then_inc(sig["pe_o"], 1)

            def x2_turn(b):
                wait(pe, "d_xn2", b, 1)
                wait(pe, "d_v2", b - 1, 2)
                for k in range(KT):
                    ins = pe.transpose(A[0][:, k * S:(k + 1) * S], xn[:, k * 128:(k + 1) * 128], ident[0:S, 0:S])
                ins.then_inc(sig["pe_xT2"], 1)

            def project2(b, n):
                if n == 0:
                    wait(pe, "a_x2", b, 1)
                    wait(pe, "d_x2", b, 1)
                    wait(pe, "d_v2", b - 1, 3)
                elif n == 1:
                    wait(pe, "a_ctx", b, 1)
                    wait(pe, "d_ctx", b, 1)
                elif n <= 5:
                    wait(pe, "a_sq2", b, n - 1)
                else:
                    wait(pe, "d_v2", b, 1)
                i = 0
                for hi, wp in ((1, wxh), (1, wxl), (0, wxh)):
                    for k in range(KT):
                        if n == 0:
                            rows, lhs = S, (xh if hi else xl)[:, k, :]
                        else:
                            c = (n - 1) % 3
                            rows, lhs = KC, (ch if hi else cl)[:, k, c * KC:(c + 1) * KC]
                        ins = pe.matmul(A[(n + 1) % 2][0:rows, :], lhs, wp[:, 0 if n == 0 else 1 if n < 4 else 2, k, :],
                                        start=(i == 0), stop=(i == 11))
                        i += 1
                ins.then_inc(sig["pe_proj"], 1)

            def turn_heads(b, m, par):
                wait(pe, "d_kst", b, m + 1)
                wait(pe, "a_kst", b, m + 1)
                wait(pe, "d_qst", b, 1)
                bb, mm = later(b, m, -1)
                wait(pe, "d_T", bb, mm + 1)
                wait(pe, "a_T", bb, mm + 1)
                bank = B[0][:, :].bitcast(F16)
                for j in range(2):
                    for c in range(NC):
                        n = j * NC + c
                        pe.transpose(bank[:, n * KC:(n + 1) * KC], kst[m % 2][:, c, j * 128:(j + 1) * 128],
                                     idh[0:KC, 0:KC])
                at = 2 * NC * KC
                for j in range(2):
                    h = m * GH + 2 * j
                    ins = pe.transpose(bank[:, at + j * S:at + (j + 1) * S],
                                       qst[par][:, h:h + 2].rearrange("p h u d -> p (h u d)"), idh[0:S, 0:S])
                ins.then_inc(sig["pe_T"], 1)

            def scores2(b, m):
                wait(pe, "d_T", b, m + 1)
                wait(pe, "a_T", b, m + 1)
                for c in range(NC):
                    n = m * NC + c
                    bb, mm = (b, n) if n >= 4 else (b - 1, n + 24)
                    wait(pe, "a_e", bb, mm - 3)
                    for j in range(2):
                        ins = pe.matmul(C[n % 4][0:KC, j * 2 * S:(j + 1) * 2 * S], kT[m % 2][:, j * NC + c, :],
                                        qbd[m % 2][:, j, :], start=True, stop=True)
                    ins.then_inc(sig["pe_sc"], 1)

            def attend2(b, m, par):
                wait(pe, "d_eh", b, m + 1)
                wait(pe, "g_el", b, m + 1)
                if m == 0:
                    wait(pe, "a_v2", b, 3)
                    wait(pe, "d_v2", b, 3)
                if m % 2 == 0:
                    bb, mm = (b, m // 2) if m else (b - 1, 4)
                    wait(pe, "a_ob", bb, mm)
                for h in range(GH):
                    n = 0
                    at = ((m % 2) * GH + h) * VW
                    for c in range(NC):
                        for e in (eh, el):
                            ins = pe.matmul(B[1][0:S, at:at + VW], e[m % 2][:, c, h * S:(h + 1) * S],
                                            vst[par][:, c, (m * GH + h) * VW:(m * GH + h + 1) * VW],
                                            start=(n == 0), stop=(n == 5))
                            n += 1
                ins.then_inc(sig["pe_pv"], 1)

            def x3_turn(u, r, bank):
                wait(pe, "d_xn3", u, r + 1)
                if r >= 2:
                    wait(pe, "d_x3", u, r - 1)
                for k in range(KT):
                    ins = pe.transpose(bank[:, k * S:(k + 1) * S], xn3[r][:, k * 128:(k + 1) * 128], ident[0:S, 0:S])
                ins.then_inc(sig["pe_xT3"], 1)

            pe.wait_ge(ld_c, 48)
            pe.wait_ge(g_setup, 1)
            x_turn(0)
            for j in range(6):
                pe.wait_ge(a_whi, j + 1)
                pe.wait_ge(d_wlo, j + 1)
                project(0, j)

            def turn(b, last=False):
                for g in range(4):
                    scores(b, g)
                for j in range(4):
                    project(b + 1, j)
                p_turn(b, 0)
                project(b + 1, 4)
                p_turn(b, 1)
                attend(b, 0)
                p_turn(b, 2)
                attend(b, 1)
                p_turn(b, 3)
                attend(b, 2)
                attend(b, 3)
                project(b + 1, 5)

                def between(g):
                    z_turn(b + 1, g)
                    if g == 1 and not last:
                        x_turn(b + 2)

                project_out(b, between)
                z_turn(b + 1, 3)
                z_turn(b + 1, 4)

            x_turn(1)
            for g in range(5):
                z_turn(0, g)
            with pe.Fori(0, NB - 2) as b:
                turn(b)
            turn(NB - 2, last=True)

            b = NB - 1
            scores(b, 0)
            scores(b, 1)
            wait(pe, "d_x1", b - 1, 1)
            wait(pe, "a_v", b, 1)
            x2_turn(0)
            scores(b, 2)
            scores(b, 3)
            pe.wait_ge(a_whi, 13)
            pe.wait_ge(d_wlo, 13)
            project2(0, 0)
            project2(0, 1)
            p_turn(b, 0)
            p_turn(b, 1)
            attend(b, 0)
            p_turn(b, 2)
            attend(b, 1)
            project2(0, 2)
            p_turn(b, 3)
            attend(b, 2)
            attend(b, 3)
            for n in range(3, 7):
                project2(0, n)
            wait(pe, "d_v2", 0, 2)
            project_out(b)

            wait(pe, "a_pT", b, 4)
            wait(pe, "d_alo", b, 4)
            turn_heads(0, 0, 0)
            turn_heads(0, 1, 0)
            wait(pe, "d_x1", b, 1)
            x2_turn(1)
            scores2(0, 0)
            project2(1, 0)
            pe.wait_ge(g_ones, 2)

            def turn(b, par, end):
                for m in range(NG):
                    bb, mm = later(b, m, 1)
                    if mm > 0 or end < 2:
                        scores2(bb, mm)
                    bb, mm = later(b, m, 2)
                    if mm > 1 or end < 2:
                        turn_heads(bb, mm, par if mm > 1 else 1 - par)
                    if end < 2 and m < 6:
                        project2(b + 1, m + 1)
                    elif end < 1 and m == 6:
                        x2_turn(b + 2)
                    elif end < 1 and m == 7:
                        project2(b + 2, 0)
                    elif end == 2 and m < UB:
                        if m == 0:
                            wait(pe, "d_v2", b, 3)
                        x3_turn(0, m, A[m % 2])
                    attend2(b, m, par)

            two_ways(pe, turn)

            def up_gate(u, e, first=False):
                if e == 0:
                    wait(pe, "d_x3", u, 4)
                if e >= 2:
                    wait(pe, "d_hd", u, e - 1)
                if first and e % 4 == 0:
                    pe.wait_ge(d_tern, 3 * (e // 4) + 2)
                for half in range(2):
                    n = 0
                    for part in (fh, fl):
                        for k in range(KT):
                            ins = pe.matmul(C[2 * (e % 2) + half][:, 0:UB * S],
                                            wf[:, 3 * (e // 4) + half, k, (e % 4) * 128:(e % 4 + 1) * 128],
                                            part[:, k, :], start=(n == 0), stop=(n == 7))
                            n += 1
                ins.then_inc(sig["pe_up"], 1)

            def down(u, e, first=False):
                wait(pe, "a_hh", u, e + 1)
                wait(pe, "d_hl", u, e + 1)
                if e == 0:
                    wait(pe, "d_y", u - 1, 4)
                if first and e % 4 == 0:
                    pe.wait_ge(d_tern, 3 * (e // 4) + 3)
                for k in range(KT):
                    for part in (hh, hl):
                        ins = pe.matmul((A + B)[k][:, 0:UB * S], wf[:, 3 * (e // 4) + 2, e % 4, k * 128:(k + 1) * 128], part[e % 2],
                                        start=(e == 0 and part is hh), stop=(e == ET - 1 and part is hl))
                ins.then_inc(sig["pe_dn"], 1)

            def y_turn(u):
                wait(pe, "a_y", u, 1)
                wait(pe, "d_yc", u, 1)
                for r in range(UB):
                    for k in range(KT):
                        ins = pe.transpose((A + B)[r][0:S, k * 128:(k + 1) * 128], yT[:, k, r * S:(r + 1) * S], ident)
                    ins.then_inc(sig["pe_yT"], 1)

            def unit(u, first=False, last=False):
                up_gate(u, 0, first)
                if not first:
                    y_turn(u - 1)
                for e in range(ET):
                    if e + 1 < ET:
                        up_gate(u, e + 1, first)
                    if not last and e == ET - 2:
                        wait(pe, "d_hd", u, ET - 1)
                        x3_turn(u + 1, 0, C[0])
                        x3_turn(u + 1, 1, C[1])
                    elif not last and e == ET - 1:
                        x3_turn(u + 1, 2, C[0])
                        x3_turn(u + 1, 3, C[1])
                    down(u, e, first)

            wait(pe, "a_e", NB - 1, 24)
            wait(pe, "a_ob", NB - 1, 4)
            unit(0, first=True)
            with pe.Fori(0, NB // UB - 2) as i:
                unit(i + 1)
            unit(NB // UB - 1, last=True)
            y_turn(NB // UB - 1)


def kernel(**inputs):
    import concourse.bacc as _bacc
    from concourse import mybir as _mybir
    from concourse.bass_utils import run_bass_kernel_spmd as _run

    f = {k: np.asarray(v) for k, v in inputs.items()}
    tiles = lambda w: w.T.reshape(w.shape[1] // 128, 128, w.shape[0]).transpose(1, 0, 2)
    wqkv = f["L0_attn_w_qkv"]
    q, k, v = wqkv[:H * D], wqkv[H * D:(H + HKV) * D], wqkv[(H + HKV) * D:]
    wqkv = tiles(np.concatenate([k, q, v]))
    wqkv = wqkv.reshape(128, KT, 6, 512).transpose(0, 2, 1, 3)
    wo = tiles(f["L0_attn_w_o"]).reshape(128, 4, 4, DM)
    wkv = np.concatenate([f["L0_xattn_Wk"], f["L0_xattn_Wv"]])
    wx = tiles(np.concatenate([f["L0_xattn_Wq"], wkv[0::2], wkv[1::2]]))
    wx = wx.reshape(128, KT, 3, 512).transpose(0, 2, 1, 3)
    ctxt = f["ctx_2048"].transpose(0, 2, 1).reshape(NB, KT, 128, CTX).transpose(0, 2, 1, 3)
    updown = [tiles(f["L0_ffn_" + n]).reshape(128, KT, 4, 512).transpose(0, 2, 1, 3) for n in ("W_up", "W_gate")]
    wffn = np.concatenate(updown + [tiles(f["L0_ffn_W_down"]).reshape(128, 4, 4, DM)], 1)
    swap = lambda a: np.concatenate([a[HALF:], a[:HALF]])
    gq, gk, bq, bk = (f["L0_attn_" + n] for n in ("qn_g", "kn_g", "qn_b", "kn_b"))
    gains = np.broadcast_to(np.concatenate([gq, swap(gq), gk, swap(gk)]), (S, 4 * D))
    bcols = np.stack([bq, swap(bq), bk, swap(bk)], 1)
    arrays = {
        "x": f["x"].reshape(NB * S, DM), "wqkv": wqkv, "wo": wo, "wx": wx, "ctxt": ctxt, "wffn": wffn, "gains": gains, "bcols": bcols,
        "consts": constants(),
    }
    arrays = {f"in_{n}": np.ascontiguousarray(a) for n, a in arrays.items()}
    nc = _bacc.Bacc("TRN2", target_bir_lowering=False, num_devices=1)
    args = [nc.dram_tensor(n, a.shape, _mybir.dt.from_np(a.dtype), kind="ExternalInput").ap() for n, a in arrays.items()]
    out = nc.dram_tensor("out_x", (NB * S, DM), F32, kind="ExternalOutput").ap()
    build(nc, *args, out)
    r = _run(nc, [arrays], core_ids=[0])
    return r.results[0]["out_x"].reshape(NB, S, DM)
```
